# Optimizing a Trainium2 kernel written in Bass

```python
import numpy as np
import jax
import jax.numpy as jnp

def _softmax(x, axis=-1):
    return jax.nn.softmax(x, axis=axis)

def _gelu(x):
    return jax.nn.gelu(x, approximate=True)

def _silu(x):
    return jax.nn.silu(x)

def _sigmoid(x):
    return jax.nn.sigmoid(x)

def _layernorm(x, axis=-1, eps=1e-05):
    m = jnp.mean(x, axis=axis, keepdims=True)
    v = jnp.var(x, axis=axis, keepdims=True)
    return (x - m) / jnp.sqrt(v + eps)

def _scatter_add(tgt, idx, src, axis=0):
    return tgt.at[idx].add(src)

def _segment_sum(src, seg, n):
    return jax.ops.segment_sum(src, seg, n)
kernel_name = 'mk_adj_ffn_d4_adj_r2_64be09'

def setup_inputs(seed: int=0):
    np.random.seed(seed)
    _w = jnp.asarray

    def _rec_inputs():
        import jax
        import jax.numpy as jnp
        _gk = jax.random.key(seed)
        x = -0.0002928 + 1 * jax.random.normal(jax.random.fold_in(_gk, 1), (128, 128, 128), jnp.float32)
        _a = jax.random.bernoulli(jax.random.fold_in(_gk, 2), 0.0625, (128, 128, 128))
        _a = jnp.logical_or(_a, jnp.swapaxes(_a, -1, -2))
        _a = jnp.logical_or(_a, jnp.eye(128, dtype=bool))
        _af = _a.astype(jnp.float32)
        _af = _af * jax.random.uniform(jax.random.fold_in(_gk, 3), (128, 128, 128), jnp.float32, 0.05, 1)
        adj = _af
        return (x, adj)
    x, adj = _rec_inputs()

    def _L0_gnn_setup():
        import jax, jax.numpy as jnp
        import numpy as np
        IN_FT = 128
        OUT_FT = 128
        key = jax.random.key(seed)
        k1, k2, k3 = jax.random.split(key, 3)
        B, N = (4, 2048)
        seq = jax.random.normal(k1, (B, N, IN_FT), dtype=jnp.float32)
        adj = jax.random.uniform(k2, (B, N, N), dtype=jnp.float32)
        limit = float(np.sqrt(6.0 / (IN_FT + OUT_FT)))
        W = jax.random.uniform(k3, (OUT_FT, IN_FT), minval=-limit, maxval=limit, dtype=jnp.float32)
        b = jnp.zeros((OUT_FT,), dtype=jnp.float32)
        alpha = jnp.array(0.25, dtype=jnp.float32)
        return {'seq': seq, 'adj': adj, 'W': W, 'b': b, 'alpha': alpha}
    _L0_gnn_all = _L0_gnn_setup()
    _L0_gnn_in = {k: v for k, v in _L0_gnn_all.items() if k in ('W', 'b', 'alpha')}
    del _L0_gnn_all

    def _L0_ffn_setup():
        import jax, jax.numpy as jnp
        import numpy as np
        D_MODEL = 128
        EXPERT_DIM = 256
        NUM_EXPERTS = 8
        TOP_K = 2
        SEQ_LEN = 1024
        BATCH = 2
        key = jax.random.key(seed)
        ks = jax.random.split(key, 8)
        s = 0.02
        x = jax.random.normal(ks[0], (SEQ_LEN, BATCH, D_MODEL), dtype=jnp.float32)
        Wg = jax.random.normal(ks[1], (D_MODEL, NUM_EXPERTS), dtype=jnp.float32) * s
        bg = jax.random.normal(ks[2], (NUM_EXPERTS,), dtype=jnp.float32) * s
        bias = jnp.zeros((NUM_EXPERTS,), dtype=jnp.float32)
        W1 = jax.random.normal(ks[3], (NUM_EXPERTS, D_MODEL, EXPERT_DIM), dtype=jnp.float32) * s
        b1 = jax.random.normal(ks[4], (NUM_EXPERTS, EXPERT_DIM), dtype=jnp.float32) * s
        W2 = jax.random.normal(ks[5], (NUM_EXPERTS, EXPERT_DIM, D_MODEL), dtype=jnp.float32) * s
        b2 = jax.random.normal(ks[6], (NUM_EXPERTS, D_MODEL), dtype=jnp.float32) * s
        return {'x': x, 'Wg': Wg, 'bg': bg, 'bias': bias, 'W1': W1, 'b1': b1, 'W2': W2, 'b2': b2}
    _L0_ffn_all = _L0_ffn_setup()
    _L0_ffn_in = {k: v for k, v in _L0_ffn_all.items() if k in ('Wg', 'bg', 'bias', 'W1', 'b1', 'W2', 'b2')}
    del _L0_ffn_all

    def _L1_gnn_setup():
        import jax, jax.numpy as jnp
        import numpy as np
        B, K, H = (32, 512, 128)
        LN_EPS = 1e-05

        def layer_norm(x, gamma, beta):
            mu = jnp.mean(x, axis=-1, keepdims=True)
            var = jnp.mean(jnp.square(x - mu), axis=-1, keepdims=True)
            return (x - mu) * jax.lax.rsqrt(var + LN_EPS) * gamma + beta
        key = jax.random.key(seed)
        k1, k2, k3, k4 = jax.random.split(key, 4)
        x = jax.random.normal(k1, (B, K, H), dtype=jnp.float32)
        adj = jax.random.uniform(k2, (B, K, K), dtype=jnp.float32)
        s = 1.0 / np.sqrt(H)
        W_rel = jax.random.normal(k3, (H, H), dtype=jnp.float32) * s
        b_rel = jnp.zeros((H,), dtype=jnp.float32)
        W_root = jax.random.normal(k4, (H, H), dtype=jnp.float32) * s
        ln_gamma = jnp.ones((H,), dtype=jnp.float32)
        ln_beta = jnp.zeros((H,), dtype=jnp.float32)
        return {'x': x, 'adj': adj, 'W_rel': W_rel, 'b_rel': b_rel, 'W_root': W_root, 'ln_gamma': ln_gamma, 'ln_beta': ln_beta}
    _L1_gnn_all = _L1_gnn_setup()
    _L1_gnn_in = {k: v for k, v in _L1_gnn_all.items() if k in ('W_rel', 'b_rel', 'W_root', 'ln_gamma', 'ln_beta')}
    del _L1_gnn_all

    def _L1_ffn_setup():
        import jax, jax.numpy as jnp
        import numpy as np
        C = 128
        HID = 512
        E = 8
        TEMP = 1.0
        key = jax.random.key(seed)
        ks = jax.random.split(key, 7)
        x = jax.random.normal(ks[0], (8, 8192, C), dtype=jnp.float32)
        W1 = jax.random.normal(ks[1], (C, HID), dtype=jnp.float32) * 0.02
        b1 = jnp.zeros((HID,), dtype=jnp.float32)
        Wg = jax.random.normal(ks[2], (HID, E), dtype=jnp.float32) * 0.02
        bg = jnp.zeros((E,), dtype=jnp.float32)
        Wd = jax.random.normal(ks[3], (E, HID, C), dtype=jnp.float32) * 0.02
        bd = jnp.zeros((E, C), dtype=jnp.float32)
        return {'x': x, 'W1': W1, 'b1': b1, 'Wg': Wg, 'bg': bg, 'Wd': Wd, 'bd': bd}
    _L1_ffn_all = _L1_ffn_setup()
    _L1_ffn_in = {k: v for k, v in _L1_ffn_all.items() if k in ('W1', 'b1', 'Wg', 'bg', 'Wd', 'bd')}
    del _L1_ffn_all

    def _L2_gnn_setup():
        import jax, jax.numpy as jnp
        import numpy as np
        LN_EPS = 1e-05
        key = jax.random.key(seed)
        k1, k2, k3, k4 = jax.random.split(key, 4)
        B, N, F, O = (8, 1024, 128, 128)
        x = jax.random.normal(k1, (B, N, F), dtype=jnp.float32)
        adj = jax.random.uniform(k2, (B, N, N), dtype=jnp.float32)
        gamma = jnp.ones((F,), jnp.float32)
        beta = jnp.zeros((F,), jnp.float32)
        W_self = jax.random.normal(k3, (F, O), dtype=jnp.float32) * (1.0 / np.sqrt(F))
        W_neigh = jax.random.normal(k4, (F, O), dtype=jnp.float32) * (1.0 / np.sqrt(F))
        return {'x': x, 'adj': adj, 'gamma': gamma, 'beta': beta, 'W_self': W_self, 'W_neigh': W_neigh}
    _L2_gnn_all = _L2_gnn_setup()
    _L2_gnn_in = {k: v for k, v in _L2_gnn_all.items() if k in ('gamma', 'beta', 'W_self', 'W_neigh')}
    del _L2_gnn_all

    def _L2_ffn_setup():
        import jax, jax.numpy as jnp
        import numpy as np
        B, S, D = (8, 2048, 128)
        H = 4 * D
        CAPACITY = 0.5
        key = jax.random.key(seed)
        ks = jax.random.split(key, 6)
        x = jax.random.normal(ks[0], (B, S, D), dtype=jnp.float32)
        attention_mask = jnp.zeros((B, 1, 1, S), dtype=jnp.float32)
        wr = jax.random.normal(ks[1], (D, 1), dtype=jnp.float32) * 0.02
        br = jnp.zeros((1,), dtype=jnp.float32)
        w1 = jax.random.normal(ks[2], (D, H), dtype=jnp.float32) * 0.02
        b1 = jnp.zeros((H,), dtype=jnp.float32)
        w2 = jax.random.normal(ks[3], (H, D), dtype=jnp.float32) * 0.02
        b2 = jnp.zeros((D,), dtype=jnp.float32)
        return {'x': x, 'attention_mask': attention_mask, 'wr': wr, 'br': br, 'w1': w1, 'b1': b1, 'w2': w2, 'b2': b2}
    _L2_ffn_all = _L2_ffn_setup()
    _L2_ffn_in = {k: v for k, v in _L2_ffn_all.items() if k in ('attention_mask', 'wr', 'br', 'w1', 'b1', 'w2', 'b2')}
    del _L2_ffn_all

    def _L3_gnn_setup():
        import jax, jax.numpy as jnp
        import numpy as np
        GROUPS = [list(range(25)), [0, 1, 2, 3, 4, 5, 6, 7, 8], [0, 9, 10, 11, 12, 13, 14], [6, 7, 8, 12, 13, 14], [3, 4, 5, 9, 10, 11]]
        B, N, D_IN, D_HID = (4096, 25, 128, 256)

        def _graph_conv(x, adj, W, b):
            n = adj.shape[-1]
            A = adj + jnp.eye(n, dtype=adj.dtype)
            deg = jnp.sum(A, axis=-1)
            deg_safe = jnp.where(deg == 0, 1.0, deg)
            dinv = jnp.where(deg == 0, 0.0, deg_safe ** (-0.5))
            norm_adj = dinv[:, :, None] * A * dinv[:, None, :]
            support = jnp.einsum('bnd,de->bne', x, W)
            out = jnp.einsum('bnm,bme->bne', norm_adj, support) + b
            return jax.nn.relu(out)
        key = jax.random.key(seed)
        ks = jax.random.split(key, 7)
        s1 = float(np.sqrt(6.0 / (D_IN + D_HID)))
        s2 = float(np.sqrt(6.0 / (D_HID + D_IN)))
        return {'x': jax.random.normal(ks[0], (B, N, D_IN), dtype=jnp.float32), 'adj': jax.random.uniform(ks[1], (B, N, N), dtype=jnp.float32), 'W1': jax.random.uniform(ks[2], (5, D_IN, D_HID), jnp.float32, -s1, s1), 'b1': jnp.zeros((5, D_HID), dtype=jnp.float32), 'W2': jax.random.uniform(ks[3], (5, D_HID, D_IN), jnp.float32, -s2, s2), 'b2': jnp.zeros((5, D_IN), dtype=jnp.float32), 'fusion_w': jnp.ones((5,), dtype=jnp.float32)}
    _L3_gnn_all = _L3_gnn_setup()
    _L3_gnn_in = {k: v for k, v in _L3_gnn_all.items() if k in ('W1', 'b1', 'W2', 'b2', 'fusion_w')}
    del _L3_gnn_all

    def _L3_ffn_setup():
        import jax, jax.numpy as jnp
        import numpy as np
        B, N, D = (16, 2048, 128)
        NUM_EXPERTS, TOP_K, HEADS = (4, 2, 4)
        N_EDGES = 524288
        LN_EPS = 1e-05

        def _layernorm(x, g, b):
            mu = x.mean(-1, keepdims=True)
            var = ((x - mu) ** 2).mean(-1, keepdims=True)
            return (x - mu) * jax.lax.rsqrt(var + LN_EPS) * g + b

        def _forward(x, edge_index, W_gat, att_src, att_dst, b_gat, ln_gamma, ln_beta, W1, b1, W2, b2):
            Bc, Nc, Dc = x.shape
            M = Bc * Nc
            x_flat = x.reshape(M, Dc)
            h = (x_flat @ W_gat).reshape(M, HEADS, NUM_EXPERTS)
            loops = jnp.arange(M, dtype=edge_index.dtype)
            src = jnp.concatenate([edge_index[0], loops])
            dst = jnp.concatenate([edge_index[1], loops])
            a_src = (h * att_src).sum(-1)
            a_dst = (h * att_dst).sum(-1)
            e = jax.nn.leaky_relu(a_src[src] + a_dst[dst], negative_slope=0.2)
            e_max = jax.ops.segment_max(e, dst, num_segments=M)
            ee = jnp.exp(e - e_max[dst])
            denom = jax.ops.segment_sum(ee, dst, num_segments=M)
            alpha = ee / (denom[dst] + 1e-16)
            msg = h[src] * alpha[:, :, None]
            agg = jax.ops.segment_sum(msg, dst, num_segments=M).reshape(M, HEADS * NUM_EXPERTS) + b_gat
            scores = _layernorm(agg, ln_gamma, ln_beta).reshape(M, HEADS, NUM_EXPERTS).mean(1)
            scores = scores.reshape(Bc, Nc, NUM_EXPERTS)
            topk_s, topk_i = jax.lax.top_k(scores, TOP_K)
            w = jax.nn.softmax(topk_s, axis=-1)
            out = jnp.zeros_like(x)
            for ei in range(NUM_EXPERTS):
                g = jnp.where(topk_i == ei, w, 0.0).sum(-1)
                hh = jax.nn.gelu(x @ W1[ei] + b1[ei], approximate=False)
                out = out + g[..., None] * (hh @ W2[ei] + b2[ei])
            return out
        key = jax.random.key(seed)
        ks = jax.random.split(key, 8)
        s = 0.05
        return {'x': jax.random.normal(ks[0], (B, N, D), jnp.float32), 'W_gat': jax.random.normal(ks[1], (D, HEADS * NUM_EXPERTS), jnp.float32) * s, 'att_src': jax.random.normal(ks[2], (HEADS, NUM_EXPERTS), jnp.float32) * s, 'att_dst': jax.random.normal(ks[3], (HEADS, NUM_EXPERTS), jnp.float32) * s, 'b_gat': jnp.zeros((HEADS * NUM_EXPERTS,), jnp.float32), 'ln_gamma': jnp.ones((HEADS * NUM_EXPERTS,), jnp.float32), 'ln_beta': jnp.zeros((HEADS * NUM_EXPERTS,), jnp.float32), 'W1': jax.random.normal(ks[4], (NUM_EXPERTS, D, 2 * D), jnp.float32) * s, 'b1': jnp.zeros((NUM_EXPERTS, 2 * D), jnp.float32), 'W2': jax.random.normal(ks[5], (NUM_EXPERTS, 2 * D, D), jnp.float32) * s, 'b2': jnp.zeros((NUM_EXPERTS, D), jnp.float32), 'edge_index': jax.random.randint(ks[6], (2, N_EDGES), 0, B * N, jnp.int32)}
    _L3_ffn_all = _L3_ffn_setup()
    _L3_ffn_in = {k: v for k, v in _L3_ffn_all.items() if k in ('W_gat', 'att_src', 'att_dst', 'b_gat', 'ln_gamma', 'ln_beta', 'W1', 'b1', 'W2', 'b2', 'edge_index')}
    del _L3_ffn_all
    return {'x': x, 'adj': adj, 'L0_gnn_W': _L0_gnn_in['W'], 'L0_gnn_b': _L0_gnn_in['b'], 'L0_gnn_alpha': _L0_gnn_in['alpha'], 'L0_ffn_Wg': _L0_ffn_in['Wg'], 'L0_ffn_bg': _L0_ffn_in['bg'], 'L0_ffn_bias': _L0_ffn_in['bias'], 'L0_ffn_W1': _L0_ffn_in['W1'], 'L0_ffn_b1': _L0_ffn_in['b1'], 'L0_ffn_W2': _L0_ffn_in['W2'], 'L0_ffn_b2': _L0_ffn_in['b2'], 'L1_gnn_W_rel': _L1_gnn_in['W_rel'], 'L1_gnn_b_rel': _L1_gnn_in['b_rel'], 'L1_gnn_W_root': _L1_gnn_in['W_root'], 'L1_gnn_ln_gamma': _L1_gnn_in['ln_gamma'], 'L1_gnn_ln_beta': _L1_gnn_in['ln_beta'], 'L1_ffn_W1': _L1_ffn_in['W1'], 'L1_ffn_b1': _L1_ffn_in['b1'], 'L1_ffn_Wg': _L1_ffn_in['Wg'], 'L1_ffn_bg': _L1_ffn_in['bg'], 'L1_ffn_Wd': _L1_ffn_in['Wd'], 'L1_ffn_bd': _L1_ffn_in['bd'], 'L2_gnn_gamma': _L2_gnn_in['gamma'], 'L2_gnn_beta': _L2_gnn_in['beta'], 'L2_gnn_W_self': _L2_gnn_in['W_self'], 'L2_gnn_W_neigh': _L2_gnn_in['W_neigh'], 'L2_ffn_attention_mask': _L2_ffn_in['attention_mask'], 'L2_ffn_wr': _L2_ffn_in['wr'], 'L2_ffn_br': _L2_ffn_in['br'], 'L2_ffn_w1': _L2_ffn_in['w1'], 'L2_ffn_b1': _L2_ffn_in['b1'], 'L2_ffn_w2': _L2_ffn_in['w2'], 'L2_ffn_b2': _L2_ffn_in['b2'], 'L3_gnn_W1': _L3_gnn_in['W1'], 'L3_gnn_b1': _L3_gnn_in['b1'], 'L3_gnn_W2': _L3_gnn_in['W2'], 'L3_gnn_b2': _L3_gnn_in['b2'], 'L3_gnn_fusion_w': _L3_gnn_in['fusion_w'], 'L3_ffn_W_gat': _L3_ffn_in['W_gat'], 'L3_ffn_att_src': _L3_ffn_in['att_src'], 'L3_ffn_att_dst': _L3_ffn_in['att_dst'], 'L3_ffn_b_gat': _L3_ffn_in['b_gat'], 'L3_ffn_ln_gamma': _L3_ffn_in['ln_gamma'], 'L3_ffn_ln_beta': _L3_ffn_in['ln_beta'], 'L3_ffn_W1': _L3_ffn_in['W1'], 'L3_ffn_b1': _L3_ffn_in['b1'], 'L3_ffn_W2': _L3_ffn_in['W2'], 'L3_ffn_b2': _L3_ffn_in['b2'], 'L3_ffn_edge_index': _L3_ffn_in['edge_index']}

def reference(x, adj, L0_gnn_W, L0_gnn_b, L0_gnn_alpha, L0_ffn_Wg, L0_ffn_bg, L0_ffn_bias, L0_ffn_W1, L0_ffn_b1, L0_ffn_W2, L0_ffn_b2, L1_gnn_W_rel, L1_gnn_b_rel, L1_gnn_W_root, L1_gnn_ln_gamma, L1_gnn_ln_beta, L1_ffn_W1, L1_ffn_b1, L1_ffn_Wg, L1_ffn_bg, L1_ffn_Wd, L1_ffn_bd, L2_gnn_gamma, L2_gnn_beta, L2_gnn_W_self, L2_gnn_W_neigh, L2_ffn_attention_mask, L2_ffn_wr, L2_ffn_br, L2_ffn_w1, L2_ffn_b1, L2_ffn_w2, L2_ffn_b2, L3_gnn_W1, L3_gnn_b1, L3_gnn_W2, L3_gnn_b2, L3_gnn_fusion_w, L3_ffn_W_gat, L3_ffn_att_src, L3_ffn_att_dst, L3_ffn_b_gat, L3_ffn_ln_gamma, L3_ffn_ln_beta, L3_ffn_W1, L3_ffn_b1, L3_ffn_W2, L3_ffn_b2, L3_ffn_edge_index):
    import jax
    import jax.numpy as jnp

    def _L0_gnn_ref(seq, adj, W, b, alpha):
        import jax, jax.numpy as jnp
        import numpy as np
        IN_FT = 128
        OUT_FT = 128
        h = jnp.einsum('bni,oi->bno', seq, W) + b
        h = jnp.einsum('bnm,bmo->bno', adj, h)
        return jnp.where(h > 0, h, alpha * h)

    def _L0_ffn_ref(x, Wg, bg, bias, W1, b1, W2, b2):
        import jax, jax.numpy as jnp
        import numpy as np
        D_MODEL = 128
        EXPERT_DIM = 256
        NUM_EXPERTS = 8
        TOP_K = 2
        SEQ_LEN = 1024
        BATCH = 2
        x_flat = x.reshape(-1, D_MODEL)
        gate_logits = x_flat @ Wg + bg + bias
        topk_vals, topk_idx = jax.lax.top_k(gate_logits, TOP_K)
        topk_w = jax.nn.softmax(topk_vals, axis=-1)
        combine = (jax.nn.one_hot(topk_idx, NUM_EXPERTS, dtype=x.dtype) * topk_w[..., None]).sum(axis=1)
        h = jax.nn.relu(jnp.einsum('td,edh->teh', x_flat, W1) + b1)
        y = jnp.einsum('teh,ehd->ted', h, W2) + b2
        out = jnp.einsum('ted,te->td', y, combine)
        return out.reshape(x.shape)

    def _L1_gnn_ref(x, adj, W_rel, b_rel, W_root, ln_gamma, ln_beta):
        import jax, jax.numpy as jnp
        import numpy as np
        B, K, H = (32, 512, 128)
        LN_EPS = 1e-05

        def layer_norm(x, gamma, beta):
            mu = jnp.mean(x, axis=-1, keepdims=True)
            var = jnp.mean(jnp.square(x - mu), axis=-1, keepdims=True)
            return (x - mu) * jax.lax.rsqrt(var + LN_EPS) * gamma + beta
        h = layer_norm(x, ln_gamma, ln_beta)
        agg = jnp.einsum('bij,bjh->bih', adj, h)
        conv = jnp.einsum('bkh,ho->bko', agg, W_rel) + b_rel + jnp.einsum('bkh,ho->bko', h, W_root)
        return x + jax.nn.relu(conv)

    def _L1_ffn_ref(x, W1, b1, Wg, bg, Wd, bd):
        import jax, jax.numpy as jnp
        import numpy as np
        C = 128
        HID = 512
        E = 8
        TEMP = 1.0
        orig_shape = x.shape
        xf = x.reshape(-1, orig_shape[-1])
        H = jax.nn.gelu(xf @ W1 + b1, approximate=False)
        probs = jax.nn.softmax((H @ Wg + bg) / TEMP, axis=-1)
        assign = jnp.argmax(probs, axis=-1)
        out = jnp.zeros_like(xf)
        for e in range(Wd.shape[0]):
            y = H @ Wd[e] + bd[e]
            sel = (assign == e)[:, None]
            out = out + jnp.where(sel, probs[:, e:e + 1] * y, 0.0)
        return out.reshape(orig_shape)

    def _L2_gnn_ref(x, adj, gamma, beta, W_self, W_neigh):
        import jax, jax.numpy as jnp
        import numpy as np
        LN_EPS = 1e-05
        mu = jnp.mean(x, axis=-1, keepdims=True)
        var = jnp.mean(jnp.square(x - mu), axis=-1, keepdims=True)
        xn = (x - mu) * jax.lax.rsqrt(var + LN_EPS) * gamma + beta
        d_out = jnp.sum(adj, axis=1)
        d_in = jnp.sum(adj, axis=2)
        s_out = jnp.where(d_out != 0, jax.lax.rsqrt(d_out), 0.0)
        s_in = jnp.where(d_in != 0, jax.lax.rsqrt(d_in), 0.0)
        A_norm = s_out[:, :, None] * adj * s_in[:, None, :]
        eye = jnp.eye(adj.shape[1], dtype=adj.dtype)
        L = eye[None, :, :] - A_norm
        neighbor = jnp.einsum('bij,bjf->bif', L, xn)
        pre = xn @ W_self + neighbor @ W_neigh
        return jax.nn.softplus(pre)

    def _L2_ffn_ref(x, attention_mask, wr, br, w1, b1, w2, b2):
        import jax, jax.numpy as jnp
        import numpy as np
        B, S, D = (8, 2048, 128)
        H = 4 * D
        CAPACITY = 0.5
        b, s, d = x.shape
        weights = (jnp.einsum('bsd,do->bso', x, wr) + br)[..., 0]
        k = max(1, int(CAPACITY * s))
        kk = k - 1 if k > 1 else 1
        _, idx = jax.lax.top_k(weights, k)
        sel_idx = idx[:, :kk]
        sel = jnp.take_along_axis(x, sel_idx[:, :, None], axis=1)
        h = jax.nn.gelu(jnp.einsum('bkd,dh->bkh', sel, w1) + b1)
        y = jnp.einsum('bkh,hd->bkd', h, w2) + b2
        w_sel = jnp.take_along_axis(weights, sel_idx, axis=1)
        y = y * w_sel[..., None]
        batch_idx = jnp.arange(b)[:, None]
        processed = jnp.zeros_like(x).at[batch_idx, sel_idx].set(y)
        return processed + x

    def _L3_gnn_ref(x, adj, W1, b1, W2, b2, fusion_w):
        import jax, jax.numpy as jnp
        import numpy as np
        GROUPS = [list(range(25)), [0, 1, 2, 3, 4, 5, 6, 7, 8], [0, 9, 10, 11, 12, 13, 14], [6, 7, 8, 12, 13, 14], [3, 4, 5, 9, 10, 11]]
        B, N, D_IN, D_HID = (4096, 25, 128, 256)

        def _graph_conv(x, adj, W, b):
            n = adj.shape[-1]
            A = adj + jnp.eye(n, dtype=adj.dtype)
            deg = jnp.sum(A, axis=-1)
            deg_safe = jnp.where(deg == 0, 1.0, deg)
            dinv = jnp.where(deg == 0, 0.0, deg_safe ** (-0.5))
            norm_adj = dinv[:, :, None] * A * dinv[:, None, :]
            support = jnp.einsum('bnd,de->bne', x, W)
            out = jnp.einsum('bnm,bme->bne', norm_adj, support) + b
            return jax.nn.relu(out)
        norm_w = jax.nn.softmax(fusion_w)
        fused = jnp.zeros_like(x)
        for g, idx_list in enumerate(GROUPS):
            idx = jnp.asarray(idx_list)
            x_g = x[:, idx, :]
            adj_g = adj[:, idx][:, :, idx]
            h = _graph_conv(x_g, adj_g, W1[g], b1[g])
            out_g = _graph_conv(h, adj_g, W2[g], b2[g])
            fused = fused.at[:, idx, :].add(norm_w[g] * out_g)
        return fused

    def _L3_ffn_ref(x, W_gat, att_src, att_dst, b_gat, ln_gamma, ln_beta, W1, b1, W2, b2, edge_index):
        import jax, jax.numpy as jnp
        import numpy as np
        B, N, D = (16, 2048, 128)
        NUM_EXPERTS, TOP_K, HEADS = (4, 2, 4)
        N_EDGES = 524288
        LN_EPS = 1e-05

        def _layernorm(x, g, b):
            mu = x.mean(-1, keepdims=True)
            var = ((x - mu) ** 2).mean(-1, keepdims=True)
            return (x - mu) * jax.lax.rsqrt(var + LN_EPS) * g + b

        def _forward(x, edge_index, W_gat, att_src, att_dst, b_gat, ln_gamma, ln_beta, W1, b1, W2, b2):
            Bc, Nc, Dc = x.shape
            M = Bc * Nc
            x_flat = x.reshape(M, Dc)
            h = (x_flat @ W_gat).reshape(M, HEADS, NUM_EXPERTS)
            loops = jnp.arange(M, dtype=edge_index.dtype)
            src = jnp.concatenate([edge_index[0], loops])
            dst = jnp.concatenate([edge_index[1], loops])
            a_src = (h * att_src).sum(-1)
            a_dst = (h * att_dst).sum(-1)
            e = jax.nn.leaky_relu(a_src[src] + a_dst[dst], negative_slope=0.2)
            e_max = jax.ops.segment_max(e, dst, num_segments=M)
            ee = jnp.exp(e - e_max[dst])
            denom = jax.ops.segment_sum(ee, dst, num_segments=M)
            alpha = ee / (denom[dst] + 1e-16)
            msg = h[src] * alpha[:, :, None]
            agg = jax.ops.segment_sum(msg, dst, num_segments=M).reshape(M, HEADS * NUM_EXPERTS) + b_gat
            scores = _layernorm(agg, ln_gamma, ln_beta).reshape(M, HEADS, NUM_EXPERTS).mean(1)
            scores = scores.reshape(Bc, Nc, NUM_EXPERTS)
            topk_s, topk_i = jax.lax.top_k(scores, TOP_K)
            w = jax.nn.softmax(topk_s, axis=-1)
            out = jnp.zeros_like(x)
            for ei in range(NUM_EXPERTS):
                g = jnp.where(topk_i == ei, w, 0.0).sum(-1)
                hh = jax.nn.gelu(x @ W1[ei] + b1[ei], approximate=False)
                out = out + g[..., None] * (hh @ W2[ei] + b2[ei])
            return out
        return _forward(x, edge_index, W_gat, att_src, att_dst, b_gat, ln_gamma, ln_beta, W1, b1, W2, b2)
    x = x + _L0_gnn_ref(_layernorm(x, axis=-1), adj, L0_gnn_W, L0_gnn_b, L0_gnn_alpha)
    x = x + _L0_ffn_ref(_layernorm(x, axis=-1), L0_ffn_Wg, L0_ffn_bg, L0_ffn_bias, L0_ffn_W1, L0_ffn_b1, L0_ffn_W2, L0_ffn_b2)
    x = x + _L1_gnn_ref(_layernorm(x, axis=-1), adj, L1_gnn_W_rel, L1_gnn_b_rel, L1_gnn_W_root, L1_gnn_ln_gamma, L1_gnn_ln_beta)
    x = x + _L1_ffn_ref(_layernorm(x, axis=-1), L1_ffn_W1, L1_ffn_b1, L1_ffn_Wg, L1_ffn_bg, L1_ffn_Wd, L1_ffn_bd)
    x = x + _L2_gnn_ref(_layernorm(x, axis=-1), adj, L2_gnn_gamma, L2_gnn_beta, L2_gnn_W_self, L2_gnn_W_neigh)
    x = x + _L2_ffn_ref(_layernorm(x, axis=-1), L2_ffn_attention_mask, L2_ffn_wr, L2_ffn_br, L2_ffn_w1, L2_ffn_b1, L2_ffn_w2, L2_ffn_b2)
    x = x + _L3_gnn_ref(_layernorm(x, axis=-1), adj, L3_gnn_W1, L3_gnn_b1, L3_gnn_W2, L3_gnn_b2, L3_gnn_fusion_w)
    x = x + _L3_ffn_ref(_layernorm(x, axis=-1), L3_ffn_W_gat, L3_ffn_att_src, L3_ffn_att_dst, L3_ffn_b_gat, L3_ffn_ln_gamma, L3_ffn_ln_beta, L3_ffn_W1, L3_ffn_b1, L3_ffn_W2, L3_ffn_b2, L3_ffn_edge_index)
    return x

_drawn_inputs = setup_inputs


def setup_inputs(seed=0):
    import zlib

    import numpy as np

    out = dict(_drawn_inputs(seed))
    spreads = {'L0_gnn_b': (0.0, 0.1),
     'L0_ffn_bias': (0.0, 0.8),
     'L1_gnn_b_rel': (0.0, 0.558),
     'L1_gnn_ln_gamma': (1.0, 0.2),
     'L1_gnn_ln_beta': (0.0, 0.1),
     'L1_ffn_b1': (0.0, 0.8),
     'L1_ffn_bg': (0.0, 0.8),
     'L1_ffn_bd': (0.0, 0.8),
     'L2_gnn_gamma': (1.0, 0.6),
     'L2_gnn_beta': (0.0, 0.655),
     'L2_ffn_b1': (0.0, 0.8),
     'L2_ffn_b2': (0.0, 0.8),
     'L3_gnn_b1': (0.0, 0.8),
     'L3_gnn_b2': (0.0, 2.0),
     'L3_gnn_fusion_w': (1.0, 0.6),
     'L3_ffn_b_gat': (0.0, 0.513),
     'L3_ffn_ln_gamma': (1.0, 0.6),
     'L3_ffn_ln_beta': (0.0, 0.71),
     'L3_ffn_b1': (0.0, 2.0),
     'L3_ffn_b2': (0.0, 0.785)}
    factors = {'L0_ffn_Wg': 4.586,
     'L0_ffn_bg': 8.0,
     'L0_ffn_W1': 5.036,
     'L0_ffn_b1': 8.0,
     'L0_ffn_W2': 3.596,
     'L0_ffn_b2': 7.239,
     'L1_ffn_W1': 8.0,
     'L1_ffn_Wg': 8.0,
     'L1_ffn_Wd': 8.0,
     'L2_ffn_wr': 8.0,
     'L2_ffn_w1': 8.0,
     'L2_ffn_w2': 8.0,
     'L3_gnn_W1': 8.0,
     'L3_gnn_W2': 8.0,
     'L3_ffn_att_src': 30.941,
     'L3_ffn_att_dst': 52.952,
     'L3_ffn_W_gat': 3.251,
     'L3_ffn_W1': 2.951}
    for name, (base, spread) in spreads.items():
        noise = np.random.default_rng([zlib.crc32(name.encode()), seed]).standard_normal(out[name].shape)
        drawn = base * np.exp(spread * noise) if base else spread * noise
        out[name] = jnp.asarray(drawn.astype(out[name].dtype))
    for name, factor in factors.items():
        out[name] = (out[name] * factor).astype(out[name].dtype)
    return out
```

```python
from contextlib import ExitStack

import concourse.bass as bass
import numpy as np
from concourse import mybir

F32, BF16 = mybir.dt.float32, mybir.dt.bfloat16
I32, U32 = mybir.dt.int32, mybir.dt.uint32
ALU, ACT, AX = mybir.AluOpType, mybir.ActivationFunctionType, mybir.AxisListType

P = 128
B, N, D = 128, 128, 128
NODES = B * N
EDGES = 524288
G = 4
NET_TURNS = B // G
NORMS = 10
HIDS, YS = 24, 16
JOINTS, GJ = 25, G * 25
JOINT_GROUPS = [list(range(25)), [0, 1, 2, 3, 4, 5, 6, 7, 8], [0, 9, 10, 11, 12, 13, 14], [6, 7, 8, 12, 13, 14],
                [3, 4, 5, 9, 10, 11]]
GROUPS = len(JOINT_GROUPS)
KEPT = max(1, N // 2) - 1
HEADS, EXPERTS = 4, 4
HE = HEADS * EXPERTS
ROW = HE + 2 * HEADS
CARRY = HEADS + HE
EPS = 1e-5
BIG, HUGE = 1e30, 3e38

LOOPS = NODES // P
TILES = LOOPS + EDGES // P
PLACES = TILES * P
BLOCKS = TILES // P
WIDTH = PLACES // P
CHUNK = TILES // 4
UNROLL = 4
TURNS = TILES // (4 * UNROLL)
SCATTERS = TILES // 32
LOOP_BIT = 1 << 21
EMPTY = 1 << 22
FAR = 1 << 20
SPAN = 64
SCAN_TURNS = WIDTH // (2 * SPAN)
OWN = 32

NET_STEPS, RANK_STEPS, SCAN_STEPS, TAIL_STEPS = 95, 9, 30, 39

ROWS = [("L0_gnn_b", D), ("L0_gnn_alpha", 1), ("L0_ffn_bg", 8), ("L0_ffn_bias", 8), ("L1_gnn_ln_gamma", D),
        ("L1_gnn_ln_beta", D), ("L1_gnn_b_rel", D), ("L1_ffn_bg", 8), ("L2_gnn_gamma", D), ("L2_gnn_beta", D),
        ("L2_ffn_br", 1), ("L2_ffn_b2", D), ("L3_gnn_b2", GROUPS * D), ("L3_gnn_fusion_w", GROUPS),
        ("L3_ffn_att_src", HE), ("L3_ffn_att_dst", HE), ("L3_ffn_b_gat", HE), ("L3_ffn_ln_gamma", HE),
        ("L3_ffn_ln_beta", HE)]
ROW_AT = {}
for _name, _n in ROWS:
    ROW_AT[_name] = (sum(n for _, n in ROWS[:len(ROW_AT)]), _n)
ROW_TOTAL = sum(n for _, n in ROWS)

MATS = [("wt0", D), ("wg0", 8), ("w1_0", 8 * 256), ("w2_0", 8 * 256), ("w_rel", D), ("w_root", D), ("w1_1", 512),
        ("wg1", 4 * 8), ("wd_1", 8 * 512), ("w_self", D), ("w_neigh", D), ("wr", 1), ("w1_2", 512), ("w2_2", 512),
        ("w1_3", GROUPS * 256), ("w2_3", GROUPS * 256), ("w_gat", HE), ("w1_4", EXPERTS * 256),
        ("w2_4", EXPERTS * 256), ("b1_0", 16), ("b1_1", 4), ("b1_2", 4), ("b1_3", 2 * GROUPS), ("b1_4", 8)]
CONSTS = [("ident", P), ("iota", P), ("before", P), ("earlier", P), ("falling", 8), ("cut_row", P),
          ("member", GROUPS * GJ), ("joint_share", GROUPS)]
CONST_TOTAL = sum(n for _, n in CONSTS)

def build(nc, x_in, adj_in, adjT_in, edges, rows_in_dram, consts_in, expert_biases, mats, out):
    table = nc.dram_tensor("table", (NODES, ROW), F32).ap()
    x_mid = nc.dram_tensor("x_mid", (NET_TURNS, P, G * D), F32).ap()
    zT_mid = nc.dram_tensor("zT_mid", (NET_TURNS, P, G * D), F32).ap()
    by_low = nc.dram_tensor("by_low", (PLACES, 1), F32).ap()
    order = nc.dram_tensor("order", (PLACES, 1), I32).ap()
    order_rows = order.rearrange("(p c) o -> p (c o)", p=P)
    state_rows = nc.dram_tensor("state_rows", (P, WIDTH * ROW), F32).ap()
    carry_rows = nc.dram_tensor("carry_rows", (P, 2 * CARRY), F32).ap()

    with ExitStack() as ctx:
        def sb(name, shape, dt=F32, stack=ctx):
            return stack.enter_context(nc.sbuf_tensor(name, shape, dt))

        def bank(name, shape=(P, 512)):
            return ctx.enter_context(nc.psum_tensor(name, list(shape), F32))

        def sem(name):
            return ctx.enter_context(nc.semaphore(name))

        T = bank("T")
        HP = [bank(f"HP{i}") for i in range(2)]
        Y = [bank(f"Y{i}", (P, 4, D)) for i in range(2)]
        M = bank("M")
        BS = bank("BS", (P, 4, D))

        consts = sb("consts", [P, CONST_TOTAL])
        at = 0
        const = {}
        for name, n in CONSTS:
            const[name] = consts[:, at:at + n]
            at += n
        ident, iota, before, earlier, falling, cut_row = (
            const[n] for n in ("ident", "iota", "before", "earlier", "falling", "cut_row"))
        member = const["member"][0:GJ, :].rearrange("p (k n) -> p k n", k=GROUPS)
        row_tile = sb("row_tile", [P, ROW_TOTAL])

        def row(name):
            a, n = ROW_AT[name]
            return row_tile[:, a:a + n]

        mat = {name: sb(name, [P, n]) for name, n in MATS}
        (wt0, wg0, w1_0, w2_0, w_rel, w_root, w1_1, wg1, wd_1, w_self, w_neigh, wr, w1_2, w2_2, w1_3, w2_3, w_gat,
         w1_4, w2_4, b1_0, b1_1, b1_2, b1_3, b1_4) = (mat[name] for name, _ in MATS)
        b2_0 = sb("b2_0", [G * 8, G * D])
        b2_1 = sb("b2_1", [G * 8, G * D])
        b2_4 = sb("b2_4", [G * EXPERTS, G * D])
        wr_wide = sb("wr_wide", [P, P])
        before_b = sb("before_b", [P, P], BF16)
        ones_b = sb("ones_b", [P, P], BF16)
        zeros_b = sb("zeros_b", [P, P], BF16)
        ones = sb("ones", [P, P])
        zeros = sb("zeros", [P, P])
        eps = sb("eps", [P, 1])
        one = sb("one", [P, 1])
        gate_bias0 = sb("gate_bias0", [P, 8])
        share = sb("share", [P, GROUPS])
        share_sum = sb("share_sum", [P, 1])

        count, countT = sb("count", [P, P]), sb("countT", [P, P])
        totals = sb("totals", [P, P])
        base_low, base_high = sb("base_low", [P, P]), sb("base_high", [P, P])
        first_place, last_place = sb("first_place", [P, P]), sb("last_place", [P, P])

        XIN, A, AT, X, Z, H, XS, NB, R, W, SP = (
            sb(n, [P, G, D]) for n in ("XIN", "A", "AT", "X", "Z", "H", "XS", "NB", "R", "W", "SP"))
        ZT, NBT, AGT = (sb(n, [P, G * N]) for n in ("ZT", "NBT", "AGT"))
        HT = sb("HT", [P, 4, G * N])
        stats, moments = sb("stats", [P, G, 6]), sb("moments", [P, G, 2])
        deviation, rstd, peak, first, gap_exp, weight = (
            sb(n, [P, G]) for n in ("deviation", "rstd", "peak", "first", "gap_exp", "weight"))
        top = sb("top", [P, 2, G])
        degree, no_edge, degree_root, scale_io = (
            sb(n, [P, 2 * G]) for n in ("degree", "no_edge", "degree_root", "scale_io"))
        logits, probs, chosen, second, gate = (
            sb(n, [P, G, 8]) for n in ("logits", "probs", "chosen", "second", "gate"))
        CT = sb("CT", [G * 8, P])
        ABIN, AB = sb("ABIN", [GJ, GJ]), sb("AB", [GJ, GJ])
        A5, NT5 = sb("A5", [GJ, GROUPS, GJ]), sb("NT5", [GJ, GROUPS, GJ])
        deg5, no5, root5, inv5 = (sb(n, [GJ, GROUPS]) for n in ("deg5", "no5", "root5", "inv5"))
        ZS, F = sb("ZS", [GJ, D]), sb("F", [GJ, D])
        UT = sb("UT", [P, GROUPS * GJ])
        H3 = sb("H3", [P, 2, GROUPS, GJ])
        V5, F5 = sb("V5", [GJ, GROUPS * D]), sb("F5", [GJ, GROUPS, D])
        FB = sb("FB", [JOINTS, G, D])
        TAB = sb("TAB", [P, G, ROW])
        gat_part = sb("gat_part", [P, G, HE])
        bits = sb("bits", [P, CHUNK], I32)
        bitsf = bits[:, :].bitcast(F32)

        with ExitStack() as sorting:
            POS_t = sb("POS", [P, TILES], F32, sorting)
            VAL_t = sb("VAL", [P, TILES], F32, sorting)
            POS, VAL = POS_t[:, :], VAL_t[:, :]
            digit = sb("digit", [P, TILES], BF16, sorting)
            high = sb("high", [P, TILES], BF16, sorting)
            bits2 = sb("bits2", [P, CHUNK], I32, sorting)
            loop_ids = sb("loop_ids", [P, LOOPS], I32, sorting)
            OH = sb("OH", [P, 2, 4, P], BF16, sorting)
            OH2 = sb("OH2", [P, 2, 4, P], BF16, sorting)
            places = sb("places", [P, 4, P], F32, sorting)
            run = sb("run", [P, 2, P], F32, sorting)
            place16 = sb("place16", [P, 16], F32, sorting)
            skip16 = sb("skip16", [P, 16], F32, sorting)
            stage_place = sb("stage_place", [P, 2, 16], I32, sorting)
            stage_value = sb("stage_value", [P, 2, 16], F32, sorting)
        begun = sb("begun", [P, OWN, P], BF16)
        begun_sum = sb("begun_sum", [P, P])
        owner = sb("owner", [P, 1], I32)
        owner_row = sb("owner_row", [P, ROW])
        end_place, end_part = sb("end_place", [P, P], I32), sb("end_part", [P, P], I32)
        node_a, node_b, node_c, uncut = (sb(n, [P, P]) for n in ("node_a", "node_b", "node_c", "uncut"))
        indices, source = sb("indices", [P, 2, SPAN], I32), sb("source", [P, 2, SPAN], I32)
        loop_here = sb("loop_here", [P, 2, SPAN])
        going, restart = sb("going", [P, SPAN]), sb("restart", [P, SPAN])
        loop_any, loops_seen = sb("loop_any", [P, 1]), sb("loops_seen", [P, 1])
        rows_in = sb("rows_in", [P, 2, SPAN * ROW])
        states = sb("states", [P, 2, SPAN, ROW])
        adst_run = sb("adst_run", [P, 2, HEADS, SPAN])
        high_run = sb("high_run", [P, 2, HEADS, SPAN + 1])
        adst, score, decay, mass = (sb(n, [P, HEADS, SPAN]) for n in ("adst", "score", "decay", "mass"))
        weighed = sb("weighed", [P, HE, SPAN])
        chain_in, chain = sb("chain_in", [P, 3, CARRY]), sb("chain", [CARRY, 3, P])
        chain_high, chain_sum = sb("chain_high", [CARRY, P + 1]), sb("chain_sum", [CARRY, P + 1])
        carry_out = sb("carry_out", [P, 2 * CARRY])
        tail_index = sb("tail_index", [P, 2, G], I32)
        node_states, node_carry = sb("node_states", [P, G * ROW]), sb("node_carry", [P, G * 2 * CARRY])
        own_high, taken_high, both_high = (sb(n, [P, G, CARRY]) for n in ("own_high", "taken_high", "both_high"))
        denominator = sb("denominator", [P, G, HEADS])
        agg = sb("agg", [P, G, HE])
        tail_gate = sb("tail_gate", [P, G, EXPERTS])

        scattered = [sem(f"scattered{i}") for i in range(4)]
        indices_loaded = [sem(f"indices_loaded{i}") for i in range(2)]
        gathered = [sem(f"gathered{i}") for i in range(2)]
        states_stored = [sem(f"states_stored{i}") for i in range(2)]
        vector_ticks, variance_ready, deviation_ready, vector_steps = (
            sem(n) for n in ("vector_ticks", "variance_ready", "deviation_ready", "vector_steps"))
        outputs_ready, outputs_used, adj_loaded, adj_rows_used = (
            sem(n) for n in ("outputs_ready", "outputs_used", "adj_loaded", "adj_rows_used"))
        degrees_ready, degree_roots_ready, x_loaded, results_stored = (
            sem(n) for n in ("degrees_ready", "degree_roots_ready", "x_loaded", "results_stored"))
        h0_ready, h_ready, mixed0_ready, x_used = (
            sem(n) for n in ("h0_ready", "h_ready", "mixed0_ready", "x_used"))
        gates_ready, gate_gap_ready, gate_exp_ready, gate_ready = (
            sem(n) for n in ("gates_ready", "gate_gap_ready", "gate_exp_ready", "gate_ready"))
        bias_sum_ready, z_ready, conv1_ready, shifted_ready = (
            sem(n) for n in ("bias_sum_ready", "z_ready", "conv1_ready", "shifted_ready"))
        probs_ready, mixed2_ready, softplus_ready, weights_ready = (
            sem(n) for n in ("probs_ready", "mixed2_ready", "softplus_ready", "weights_ready"))
        deep_ready, blocks_loaded, joint_degrees_ready, joint_roots_ready = (
            sem(n) for n in ("deep_ready", "blocks_loaded", "joint_degrees_ready", "joint_roots_ready"))
        joint_adj_ready, joint_turned, joint_norm_ready, joint_out_ready = (
            sem(n) for n in ("joint_adj_ready", "joint_turned", "joint_norm_ready", "joint_out_ready"))
        fused_ready, fused_back, gat_ready, table_ready = (
            sem(n) for n in ("fused_ready", "fused_back", "gat_ready", "table_ready"))
        turned, turned_copied, hidden_ready, hidden_done = (
            sem(n) for n in ("turned", "turned_copied", "hidden_ready", "hidden_done"))
        gates_turned, gate_columns_ready, mixed1_ready, mixed1_copied = (
            sem(n) for n in ("gates_turned", "gate_columns_ready", "mixed1_ready", "mixed1_copied"))
        pre_ready, softplus_steps, joint_mixed_ready, joint_mixed_copied = (
            sem(n) for n in ("pre_ready", "softplus_steps", "joint_mixed_ready", "joint_mixed_copied"))
        joint_hidden_ready, joint_hidden_done, joint_values_ready, joint_values_copied = (
            sem(n) for n in ("joint_hidden_ready", "joint_hidden_done", "joint_values_ready", "joint_values_copied"))
        joints_stacked, joints_ready, edges_loaded, loops_made = (
            sem(n) for n in ("joints_stacked", "joints_ready", "edges_loaded", "loops_made"))
        pairs_counted, pairs_ready, counts_ready, count_copied = (
            sem(n) for n in ("pairs_counted", "pairs_ready", "counts_ready", "count_copied"))
        sums_ready, count_turned, count_turn_copied, onehots_ready = (
            sem(n) for n in ("sums_ready", "count_turned", "count_turn_copied", "onehots_ready"))
        prefixes_ready, ranks_taken, places_ready, staged = (
            sem(n) for n in ("prefixes_ready", "ranks_taken", "places_ready", "staged"))
        blocks_turned_copied, sorted_loaded, blocks_turned, begun_ready = (
            sem(n) for n in ("blocks_turned_copied", "sorted_loaded", "blocks_turned", "begun_ready"))
        owner_ready, owner_written, ends_ready, owner_row_loaded = (
            sem(n) for n in ("owner_ready", "owner_written", "ends_ready", "owner_row_loaded"))
        states_ready, sources_ready, exponents_ready, exps_ready = (
            sem(n) for n in ("states_ready", "sources_ready", "exponents_ready", "exps_ready"))
        scan_steps, chain_in_ready, chain_turned, chain_exponents_ready = (
            sem(n) for n in ("scan_steps", "chain_in_ready", "chain_turned", "chain_exponents_ready"))
        chain_exps_ready, chain_ready, chain_back, carry_ready = (
            sem(n) for n in ("chain_exps_ready", "chain_ready", "chain_back", "carry_ready"))
        node_rows_used, tail_staged, node_rows_loaded, tail_steps = (
            sem(n) for n in ("node_rows_used", "tail_staged", "node_rows_loaded", "tail_steps"))
        node_exponents_ready, node_exps_ready, agg_variance_ready, agg_deviation_ready = (
            sem(n) for n in ("node_exponents_ready", "node_exps_ready", "agg_variance_ready", "agg_deviation_ready"))
        tail_gap_ready, tail_gap_exp_ready, tail_gate_ready, tail_x_loaded = (
            sem(n) for n in ("tail_gap_ready", "tail_gap_exp_ready", "tail_gate_ready", "tail_x_loaded"))
        tail_outputs_ready, tail_outputs_used, tail_bias_ready, out_stored = (
            sem(n) for n in ("tail_outputs_ready", "tail_outputs_used", "tail_bias_ready", "out_stored"))
        out_ready, tail_hidden_ready, tail_hidden_done, tail_gates_turned = (
            sem(n) for n in ("out_ready", "tail_hidden_ready", "tail_hidden_done", "tail_gates_turned"))
        tail_gate_columns_ready, tail_z_loaded, consts_loaded, weights_loaded = (
            sem(n) for n in ("tail_gate_columns_ready", "tail_z_loaded", "consts_loaded", "weights_loaded"))
        cleared, places_blanked, bf_consts_ready, fusion_shifted = (
            sem(n) for n in ("cleared", "places_blanked", "bf_consts_ready", "fusion_shifted"))
        fusion_exp_ready, weights_ready0, carry_stored, vector_links = (
            sem(n) for n in ("fusion_exp_ready", "weights_ready0", "carry_stored", "vector_links"))
        rank_steps, sync_ticks, pool_ticks = (
            sem(n) for n in ("rank_steps", "sync_ticks", "pool_ticks"))

        def vector_norms(eng, t, src, dst, k, link, last_signal=None):
            for g in range(G):
                ins = eng.bn_stats(stats[:, g, :], src[:, g, :])
            link(ins)
            eng.sem_inc(vector_ticks, 1)
            for g in range(G):
                ins = eng.bn_aggr(moments[:, g, :], stats[:, g, :])
            ins.then_inc(variance_ready, 1)
            eng.wait_ge(deviation_ready, t * NORMS + k)
            link(eng.reciprocal(rstd[:, :], deviation[:, :]))
            for g in range(G):
                ins = eng.tensor_scalar(dst[:, g, :], src[:, g, :], moments[:, g, 0:1], rstd[:, g:g + 1],
                                        ALU.subtract, ALU.mult)
            if last_signal is None:
                link(ins)
            else:
                ins.then_inc(last_signal, 1)

        def first_largest(eng, link, onehot, values, n):
            link(eng.tensor_reduce(peak[:, :], values, AX.X, ALU.max))
            link(eng.tensor_tensor(onehot, values, peak[:, :].unsqueeze(2).broadcast_to([P, G, n]), ALU.is_equal))
            link(eng.tensor_tensor(onehot, onehot, falling[:, 0:n].unsqueeze(1).broadcast_to([P, G, n]), ALU.mult))
            link(eng.tensor_reduce(first[:, :], onehot, AX.X, ALU.max))
            link(eng.tensor_tensor(onehot, onehot, first[:, :].unsqueeze(2).broadcast_to([P, G, n]), ALU.is_equal))

        def vector_network(eng, t):
            count = [0]

            def link(ins):
                ins.then_inc(vector_steps, 1)
                count[0] += 1
                eng.wait_ge(vector_steps, t * NET_STEPS + count[0])

            def wide(row, n=D):
                return row.unsqueeze(1).broadcast_to([P, G, n])

            def per_token(cols, n=D):
                return cols.unsqueeze(2).broadcast_to([P, G, n])

            def expert_sum(first_y, experts):
                for e in range(experts):
                    eng.wait_ge(outputs_ready, t * YS + first_y + e + 1)
                    for g in range(G):
                        ins = eng.scalar_tensor_tensor(X[:, g, :], Y[(first_y + e) % 2][:, g, :], gate[:, g, e:e + 1],
                                                       X[:, g, :], ALU.mult, ALU.add)
                    ins.then_inc(outputs_used, 1)
                    eng.wait_ge(outputs_used, t * YS + first_y + e + 1)

            eng.wait_ge(adj_loaded, t * 32 + 32)
            link(eng.tensor_reduce(degree[:, 0:G], AT[:, :, :], AX.X, ALU.add))
            eng.tensor_reduce(degree[:, G:2 * G], A[:, :, :], AX.X, ALU.add).then_inc(adj_rows_used, 1)
            eng.wait_ge(adj_rows_used, t + 1)
            link(eng.tensor_scalar(no_edge[:, :], degree[:, :], 0.0, None, ALU.is_equal))
            eng.tensor_tensor(degree[:, :], degree[:, :], no_edge[:, :], ALU.add).then_inc(degrees_ready, 1)
            eng.wait_ge(degree_roots_ready, t + 1)
            link(eng.tensor_scalar(no_edge[:, :], no_edge[:, :], -1.0, 1.0, ALU.mult, ALU.add))
            link(eng.reciprocal(scale_io[:, :], degree_root[:, :]))
            link(eng.tensor_tensor(scale_io[:, :], scale_io[:, :], no_edge[:, :], ALU.mult))

            eng.wait_ge(x_loaded, t * 16 + 16)
            eng.wait_ge(results_stored, t * 48)
            vector_norms(eng, t, XIN, Z, 1, link, z_ready)
            eng.wait_ge(h0_ready, t + 1)
            eng.tensor_tensor(H[:, :, :], Y[0][:, :, :], wide(row("L0_gnn_b")), ALU.add).then_inc(h_ready, 1)
            eng.wait_ge(mixed0_ready, t + 1)
            link(eng.tensor_scalar(R[:, :, :], Y[1][:, :, :], 0.0, row("L0_gnn_alpha"), ALU.min, ALU.mult))
            link(eng.scalar_tensor_tensor(R[:, :, :], Y[1][:, :, :], 0.0, R[:, :, :], ALU.max, ALU.add))
            eng.tensor_tensor(X[:, :, :], XIN[:, :, :], R[:, :, :], ALU.add).then_inc(x_used, 1)
            eng.wait_ge(x_used, t + 1)

            vector_norms(eng, t, X, Z, 2, link, z_ready)
            eng.wait_ge(gates_ready, t * 2 + 1)
            link(eng.tensor_tensor(logits[:, :, :], M[:, 0:G * 8].rearrange("p (g e) -> p g e", g=G),
                                   wide(gate_bias0[:, :], 8), ALU.add))
            first_largest(eng, link, chosen[:, :, :], logits[:, :, :], 8)
            link(eng.tensor_copy(top[:, 0, :], peak[:, :]))
            link(eng.scalar_tensor_tensor(logits[:, :, :], chosen[:, :, :], -BIG, logits[:, :, :], ALU.mult, ALU.add))
            first_largest(eng, link, second[:, :, :], logits[:, :, :], 8)
            eng.tensor_tensor(top[:, 1, :], peak[:, :], top[:, 0, :], ALU.subtract).then_inc(gate_gap_ready, 1)
            eng.wait_ge(gate_exp_ready, t + 1)
            link(eng.tensor_scalar(top[:, 0, :], gap_exp[:, :], 1.0, None, ALU.add))
            link(eng.reciprocal(top[:, 1, :], top[:, 0, :]))
            link(eng.tensor_tensor(top[:, 0, :], gap_exp[:, :], top[:, 1, :], ALU.mult))
            link(eng.tensor_tensor(chosen[:, :, :], chosen[:, :, :], per_token(top[:, 1, :], 8), ALU.mult))
            link(eng.tensor_tensor(second[:, :, :], second[:, :, :], per_token(top[:, 0, :], 8), ALU.mult))
            eng.tensor_tensor(gate[:, :, :], chosen[:, :, :], second[:, :, :], ALU.add).then_inc(gate_ready, 1)
            eng.wait_ge(gate_ready, t * 2 + 1)
            expert_sum(0, 8)
            eng.wait_ge(bias_sum_ready, t * 2 + 1)
            link(eng.tensor_tensor(X[:, :, :], X[:, :, :], BS[:, :, :], ALU.add))

            vector_norms(eng, t, X, Z, 3, link)
            vector_norms(eng, t, Z, H, 4, link)
            link(eng.tensor_tensor(H[:, :, :], H[:, :, :], wide(row("L1_gnn_ln_gamma")), ALU.mult))
            eng.tensor_tensor(H[:, :, :], H[:, :, :], wide(row("L1_gnn_ln_beta")), ALU.add).then_inc(z_ready, 1)
            eng.wait_ge(conv1_ready, t + 1)
            link(eng.tensor_tensor(R[:, :, :], Y[1][:, :, :], wide(row("L1_gnn_b_rel")), ALU.add))
            link(eng.scalar_tensor_tensor(R[:, :, :], R[:, :, :], 0.0, Z[:, :, :], ALU.max, ALU.add))
            link(eng.tensor_tensor(X[:, :, :], X[:, :, :], R[:, :, :], ALU.add))

            vector_norms(eng, t, X, Z, 5, link, z_ready)
            eng.wait_ge(gates_ready, t * 2 + 2)
            link(eng.tensor_tensor(logits[:, :, :], M[:, 0:G * 8].rearrange("p (g e) -> p g e", g=G),
                                   wide(row("L1_ffn_bg"), 8), ALU.add))
            link(eng.tensor_reduce(peak[:, :], logits[:, :, :], AX.X, ALU.max))
            eng.tensor_tensor(logits[:, :, :], logits[:, :, :], per_token(peak[:, :], 8),
                              ALU.subtract).then_inc(shifted_ready, 1)
            eng.wait_ge(probs_ready, t + 1)
            link(eng.tensor_reduce(top[:, 0, :], probs[:, :, :], AX.X, ALU.add))
            link(eng.reciprocal(top[:, 1, :], top[:, 0, :]))
            first_largest(eng, link, chosen[:, :, :], probs[:, :, :], 8)
            link(eng.tensor_tensor(chosen[:, :, :], chosen[:, :, :], probs[:, :, :], ALU.mult))
            eng.tensor_tensor(gate[:, :, :], chosen[:, :, :], per_token(top[:, 1, :], 8), ALU.mult).then_inc(gate_ready, 1)
            eng.wait_ge(gate_ready, t * 2 + 2)
            expert_sum(8, 8)
            eng.wait_ge(bias_sum_ready, t * 2 + 2)
            link(eng.tensor_tensor(X[:, :, :], X[:, :, :], BS[:, :, :], ALU.add))

            vector_norms(eng, t, X, Z, 6, link)
            vector_norms(eng, t, Z, H, 7, link)
            link(eng.tensor_tensor(H[:, :, :], H[:, :, :], wide(row("L2_gnn_gamma")), ALU.mult))
            eng.tensor_tensor(H[:, :, :], H[:, :, :], wide(row("L2_gnn_beta")), ALU.add).then_inc(z_ready, 1)
            eng.wait_ge(z_ready, t * 8 + 5)
            eng.tensor_tensor(XS[:, :, :], H[:, :, :], per_token(scale_io[:, G:2 * G]), ALU.mult).then_inc(h_ready, 1)
            eng.wait_ge(mixed2_ready, t + 1)
            link(eng.tensor_tensor(R[:, :, :], Y[0][:, :, :], per_token(scale_io[:, 0:G]), ALU.mult))
            eng.tensor_tensor(NB[:, :, :], H[:, :, :], R[:, :, :], ALU.subtract).then_inc(z_ready, 1)
            eng.wait_ge(softplus_ready, t + 1)
            link(eng.scalar_tensor_tensor(R[:, :, :], Y[1][:, :, :], 0.0, SP[:, :, :], ALU.max, ALU.add))
            link(eng.tensor_tensor(X[:, :, :], X[:, :, :], R[:, :, :], ALU.add))

            vector_norms(eng, t, X, Z, 8, link, z_ready)
            eng.wait_ge(weights_ready, t + 1)
            link(eng.tensor_scalar(W[:, :, :], M[:, 0:G * N].rearrange("p (g n) -> p g n", g=G),
                                   row("L2_ffn_br"), None, ALU.add))
            link(eng.tensor_tensor(R[:, :, :], W[:, :, :], wide(ident[:, :], N), ALU.mult))
            link(eng.tensor_reduce(weight[:, :], R[:, :, :], AX.X, ALU.add))
            link(eng.tensor_tensor(R[:, :, :], W[:, :, :], per_token(weight[:, :], N), ALU.is_equal))
            link(eng.tensor_tensor(R[:, :, :], R[:, :, :], wide(earlier[:, :], N), ALU.mult))
            link(eng.tensor_tensor(W[:, :, :], W[:, :, :], per_token(weight[:, :], N), ALU.is_gt))
            link(eng.tensor_tensor(W[:, :, :], W[:, :, :], R[:, :, :], ALU.add))
            link(eng.tensor_reduce(peak[:, :], W[:, :, :], AX.X, ALU.add))
            link(eng.scalar_tensor_tensor(weight[:, :], peak[:, :], float(KEPT), weight[:, :], ALU.is_lt, ALU.mult))
            link(eng.tensor_tensor(X[:, :, :], X[:, :, :], Z[:, :, :], ALU.add))
            eng.wait_ge(deep_ready, t + 1)
            link(eng.tensor_tensor(R[:, :, :], Y[0][:, :, :], wide(row("L2_ffn_b2")), ALU.add))
            for g in range(G):
                ins = eng.scalar_tensor_tensor(X[:, g, :], R[:, g, :], weight[:, g:g + 1], X[:, g, :], ALU.mult, ALU.add)
            link(ins)

            vector_norms(eng, t, X, Z, 9, link, joints_ready)
            eng.wait_ge(blocks_loaded, t * 16 * G + 16 * G)
            link(eng.tensor_tensor(AB[:, :], ABIN[:, :], ident[0:GJ, 0:GJ], ALU.add))
            link(eng.tensor_tensor(A5[:, :, :], AB[:, :].unsqueeze(1).broadcast_to([GJ, GROUPS, GJ]), member[:, :, :],
                                   ALU.mult))
            link(eng.tensor_reduce(deg5[:, :], A5[:, :, :], AX.X, ALU.add))
            link(eng.tensor_scalar(no5[:, :], deg5[:, :], 0.0, None, ALU.is_equal))
            eng.tensor_tensor(deg5[:, :], deg5[:, :], no5[:, :], ALU.add).then_inc(joint_degrees_ready, 1)
            eng.wait_ge(joint_roots_ready, t + 1)
            link(eng.tensor_scalar(no5[:, :], no5[:, :], -1.0, 1.0, ALU.mult, ALU.add))
            link(eng.reciprocal(inv5[:, :], root5[:, :]))
            link(eng.tensor_tensor(inv5[:, :], inv5[:, :], no5[:, :], ALU.mult))
            inv_wide = inv5[:, :].unsqueeze(2).broadcast_to([GJ, GROUPS, GJ])
            eng.tensor_tensor(A5[:, :, :], A5[:, :, :], inv_wide, ALU.mult).then_inc(joint_adj_ready, 1)
            eng.wait_ge(joint_turned, t + 1)
            eng.tensor_tensor(NT5[:, :, :], T[0:GJ, 0:GROUPS * GJ].rearrange("p (k n) -> p k n", k=GROUPS), inv_wide,
                              ALU.mult).then_inc(joint_norm_ready, 1)
            eng.wait_ge(joint_out_ready, t + 1)
            bias5 = row("L3_gnn_b2")[0:GJ, :].rearrange("p (k d) -> p k d", k=GROUPS)
            eng.tensor_tensor(F5[:, 0:4, :], Y[0][0:GJ, :, :], bias5[:, 0:4, :], ALU.add)
            link(eng.tensor_tensor(F5[:, 4, :], Y[1][0:GJ, 0, :], bias5[:, 4, :], ALU.add))
            for k in range(GROUPS):
                ins = eng.tensor_scalar(F5[:, k, :], F5[:, k, :], 0.0, share[0:GJ, k:k + 1], ALU.max, ALU.mult)
            link(ins)
            eng.tensor_reduce(F[:, :], F5[:, :, :].rearrange("p k d -> p d k"), AX.X, ALU.add).then_inc(fused_ready, 1)
            eng.wait_ge(fused_back, t * 16 * G + 16 * G)
            link(eng.tensor_tensor(X[0:JOINTS, :, :], X[0:JOINTS, :, :], FB[:, :, :], ALU.add))

            vector_norms(eng, t, X, Z, 10, link, z_ready)
            eng.wait_ge(gat_ready, t + 1)
            gat = M[:, 0:G * HE].rearrange("p (g c) -> p g c", g=G)
            link(eng.tensor_copy(TAB[:, :, 0:HE], gat))
            for k, name in enumerate(("L3_ffn_att_src", "L3_ffn_att_dst")):
                link(eng.tensor_tensor(gat_part[:, :, :], TAB[:, :, 0:HE], wide(row(name), HE), ALU.mult))
                ins = eng.tensor_reduce(TAB[:, :, HE + HEADS * k:HE + HEADS * (k + 1)],
                                        gat_part[:, :, :].rearrange("p g (h e) -> p g h e", h=HEADS), AX.X, ALU.add)
                if k == 0:
                    link(ins)
                else:
                    ins.then_inc(table_ready, 1)
            assert count[0] == NET_STEPS, count[0]

        def scalar_network(eng, t):
            def root(k):
                eng.wait_ge(variance_ready, t * NORMS + k)
                eng.activation(deviation[:, :], moments[:, :, 1], ACT.Sqrt, bias=eps[:, 0:1]).then_inc(deviation_ready, 1)

            def evacuate(k, dst):
                eng.wait_ge(turned, t * 8 + k)
                eng.activation(dst[:, :], T[:, :], ACT.Copy).then_inc(turned_copied, 1)

            def hidden(n, func, bias):
                eng.wait_ge(hidden_ready, t * HIDS + n + 1)
                eng.activation(HT[:, n % 4, :], HP[n % 2][:, :], func, bias=bias).then_inc(hidden_done, 1)

            def gate_columns(k):
                eng.wait_ge(gates_turned, t * 2 + k)
                eng.activation(CT[:, :], M[0:G * 8, 0:P], ACT.Copy).then_inc(gate_columns_ready, 1)

            eng.wait_ge(degrees_ready, t + 1)
            eng.activation(degree_root[:, :], degree[:, :], ACT.Sqrt).then_inc(degree_roots_ready, 1)
            root(1)
            evacuate(1, ZT)
            root(2)
            evacuate(2, ZT)
            for n in range(4):
                hidden(n, ACT.Relu, b1_0[:, n:n + 1])
            eng.wait_ge(gate_gap_ready, t + 1)
            eng.activation(gap_exp[:, :], top[:, 1, :], ACT.Exp).then_inc(gate_exp_ready, 1)
            for n in range(4, 16):
                eng.wait_ge(outputs_ready, t * YS + n // 2 - 1)
                hidden(n, ACT.Relu, b1_0[:, n:n + 1])
            gate_columns(1)
            root(3)
            root(4)
            evacuate(3, ZT)
            eng.wait_ge(mixed1_ready, t + 1)
            eng.activation(AGT[:, :], Y[0][:, :, :].rearrange("p g n -> p (g n)"), ACT.Copy).then_inc(mixed1_copied, 1)
            root(5)
            evacuate(4, ZT)
            for n in range(4):
                hidden(16 + n, ACT.Gelu, b1_1[:, n:n + 1])
            eng.wait_ge(shifted_ready, t + 1)
            eng.activation(probs[:, :, :], logits[:, :, :], ACT.Exp).then_inc(probs_ready, 1)
            gate_columns(2)
            root(6)
            root(7)
            evacuate(5, ZT)
            evacuate(6, NBT)
            eng.wait_ge(pre_ready, t + 1)
            pre = Y[1][:, :, :].rearrange("p g n -> p (g n)")
            soft = SP[:, :, :].rearrange("p g n -> p (g n)")
            eng.activation(soft, pre, ACT.Abs).then_inc(softplus_steps, 1)
            eng.wait_ge(softplus_steps, t * 2 + 1)
            eng.activation(soft, soft, ACT.Exp, scale=-1.0).then_inc(softplus_steps, 1)
            eng.wait_ge(softplus_steps, t * 2 + 2)
            eng.activation(soft, soft, ACT.Ln, bias=one[:, 0:1]).then_inc(softplus_ready, 1)
            root(8)
            evacuate(7, ZT)
            for n in range(4):
                hidden(20 + n, ACT.Gelu_apprx_tanh, b1_2[:, n:n + 1])
            root(9)
            eng.wait_ge(joint_degrees_ready, t + 1)
            eng.activation(root5[:, :], deg5[:, :], ACT.Sqrt).then_inc(joint_roots_ready, 1)
            eng.wait_ge(joint_mixed_ready, t + 1)
            eng.activation(UT[:, :], T[:, 0:GROUPS * GJ], ACT.Copy).then_inc(joint_mixed_copied, 1)
            eng.wait_ge(joint_hidden_ready, t + 1)
            for c in range(2):
                for k in range(GROUPS):
                    ins = eng.activation(H3[:, c, k, :], HP[c][:, k * GJ:(k + 1) * GJ], ACT.Relu,
                                         bias=b1_3[:, 2 * k + c:2 * k + c + 1])
            ins.then_inc(joint_hidden_done, 1)
            eng.wait_ge(joint_values_ready, t + 1)
            eng.activation(V5[:, 0:4 * D], Y[0][0:GJ, :, :].rearrange("p g n -> p (g n)"), ACT.Copy)
            eng.activation(V5[:, 4 * D:5 * D], Y[1][0:GJ, 0, :], ACT.Copy).then_inc(joint_values_copied, 1)
            root(10)
            evacuate(8, ZT)

        def tensor_network(eng, t):
            def turn(k, src):
                eng.wait_ge(z_ready, t * 8 + k)
                for g in range(G):
                    ins = eng.transpose(T[:, g * N:(g + 1) * N], src[:, g, :], ident[:, :])
                ins.then_inc(turned, 1)

            def cols(buf, g):
                return buf[:, g * N:(g + 1) * N]

            def hidden(n, w, src):
                if n >= 2:
                    eng.wait_ge(hidden_done, t * HIDS + n - 1)
                eng.matmul(HP[n % 2][:, :], w, src[:, :], start=True, stop=True).then_inc(hidden_ready, 1)

            def second(y, slots, ws):
                for g in range(G):
                    for i, (s, w) in enumerate(zip(slots, ws)):
                        ins = eng.matmul(Y[y % 2][:, g, :], HT[:, s, g * N:(g + 1) * N], w,
                                         start=(i == 0), stop=(i == len(slots) - 1))
                return ins

            def bias_sum(k, b2):
                eng.wait_ge(gate_ready, t * 2 + k)
                eng.transpose(M[0:G * 8, 0:P], gate[:, :, :].rearrange("p g e -> p (g e)"),
                              ident[:, :]).then_inc(gates_turned, 1)
                eng.wait_ge(gate_columns_ready, t * 2 + k)
                eng.matmul(BS[:, :, :].rearrange("p g n -> p (g n)"), CT[:, :], b2[:, :], start=True,
                           stop=True).then_inc(bias_sum_ready, 1)

            turn(1, Z)
            eng.wait_ge(turned_copied, t * 8 + 1)
            for g in range(G):
                ins = eng.matmul(Y[0][:, g, :], cols(ZT, g), wt0[:, :], start=True, stop=True)
            ins.then_inc(h0_ready, 1)
            eng.wait_ge(h_ready, t * 2 + 1)
            for g in range(G):
                ins = eng.matmul(Y[1][:, g, :], AT[:, g, :], H[:, g, :], start=True, stop=True)
            ins.then_inc(mixed0_ready, 1)
            turn(2, Z)
            eng.wait_ge(turned_copied, t * 8 + 2)
            for g in range(G):
                ins = eng.matmul(M[:, g * 8:(g + 1) * 8], cols(ZT, g), wg0[:, :], start=True, stop=True)
            ins.then_inc(gates_ready, 1)
            for n in range(2):
                hidden(n, w1_0[:, n * D:(n + 1) * D], ZT)
            for e in range(8):
                if e + 1 < 8:
                    for n in (2 * e + 2, 2 * e + 3):
                        hidden(n, w1_0[:, n * D:(n + 1) * D], ZT)
                eng.wait_ge(hidden_done, t * HIDS + 2 * e + 2)
                if e >= 2:
                    eng.wait_ge(outputs_used, t * YS + e - 1)
                slots = [(2 * e) % 4, (2 * e + 1) % 4]
                second(e, slots, [w2_0[:, (2 * e + c) * D:(2 * e + c + 1) * D] for c in range(2)]).then_inc(outputs_ready, 1)
            bias_sum(1, b2_0)
            turn(3, H)
            for g in range(G):
                ins = eng.matmul(Y[0][:, g, :], H[:, g, :], AT[:, g, :], start=True, stop=True)
            ins.then_inc(mixed1_ready, 1)
            eng.wait_ge(turned_copied, t * 8 + 3)
            eng.wait_ge(mixed1_copied, t + 1)
            for g in range(G):
                eng.matmul(Y[1][:, g, :], cols(AGT, g), w_rel[:, :], start=True, stop=False)
                ins = eng.matmul(Y[1][:, g, :], cols(ZT, g), w_root[:, :], start=False, stop=True)
            ins.then_inc(conv1_ready, 1)
            turn(4, Z)
            eng.wait_ge(turned_copied, t * 8 + 4)
            for n in range(4):
                hidden(16 + n, w1_1[:, n * D:(n + 1) * D], ZT)
            eng.wait_ge(hidden_done, t * HIDS + 20)
            for g in range(G):
                for c in range(4):
                    ins = eng.matmul(M[:, g * 8:(g + 1) * 8], HT[:, c, g * N:(g + 1) * N], wg1[:, c * 8:(c + 1) * 8],
                                     start=(c == 0), stop=(c == 3))
            ins.then_inc(gates_ready, 1)
            for e in range(8):
                if e >= 2:
                    eng.wait_ge(outputs_used, t * YS + 8 + e - 1)
                if e == 2:
                    bias_sum(2, b2_1)
                second(8 + e, range(4), [wd_1[:, (4 * e + c) * D:(4 * e + c + 1) * D] for c in range(4)])\
                    .then_inc(outputs_ready, 1)
            turn(5, H)
            eng.wait_ge(h_ready, t * 2 + 2)
            for g in range(G):
                ins = eng.matmul(Y[0][:, g, :], AT[:, g, :], XS[:, g, :], start=True, stop=True)
            ins.then_inc(mixed2_ready, 1)
            eng.wait_ge(turned_copied, t * 8 + 5)
            turn(6, NB)
            eng.wait_ge(turned_copied, t * 8 + 6)
            for g in range(G):
                eng.matmul(Y[1][:, g, :], cols(ZT, g), w_self[:, :], start=True, stop=False)
                ins = eng.matmul(Y[1][:, g, :], cols(NBT, g), w_neigh[:, :], start=False, stop=True)
            ins.then_inc(pre_ready, 1)
            turn(7, Z)
            eng.wait_ge(turned_copied, t * 8 + 7)
            eng.matmul(M[:, :], wr_wide[:, :], ZT[:, :], start=True, stop=True).then_inc(weights_ready, 1)
            for n in range(4):
                hidden(20 + n, w1_2[:, n * D:(n + 1) * D], ZT)
            eng.wait_ge(hidden_done, t * HIDS + 24)
            second(0, range(4), [w2_2[:, c * D:(c + 1) * D] for c in range(4)]).then_inc(deep_ready, 1)
            eng.wait_ge(joint_adj_ready, t + 1)
            for k in range(GROUPS):
                ins = eng.transpose(T[0:GJ, k * GJ:(k + 1) * GJ], A5[:, k, :], ident[0:GJ, 0:GJ])
            ins.then_inc(joint_turned, 1)
            eng.wait_ge(joint_norm_ready, t + 1)
            eng.wait_ge(joints_stacked, t * 16 * G + 16 * G)
            eng.matmul(T[:, 0:GROUPS * GJ], ZS[:, :], NT5[:, :, :].rearrange("p k n -> p (k n)"), start=True,
                       stop=True).then_inc(joint_mixed_ready, 1)
            eng.wait_ge(joint_mixed_copied, t + 1)
            for c in range(2):
                for k in range(GROUPS):
                    ins = eng.matmul(HP[c][:, k * GJ:(k + 1) * GJ], w1_3[:, (2 * k + c) * D:(2 * k + c + 1) * D],
                                     UT[:, k * GJ:(k + 1) * GJ], start=True, stop=True)
            ins.then_inc(joint_hidden_ready, 1)
            eng.wait_ge(joint_hidden_done, t + 1)

            def joint_bank(k):
                return Y[0][0:GJ, k, :] if k < 4 else Y[1][0:GJ, 0, :]

            for k in range(GROUPS):
                for c in range(2):
                    ins = eng.matmul(joint_bank(k), H3[:, c, k, :], w2_3[:, (2 * k + c) * D:(2 * k + c + 1) * D],
                                     start=(c == 0), stop=(c == 1))
            ins.then_inc(joint_values_ready, 1)
            eng.wait_ge(joint_values_copied, t + 1)
            for k in range(GROUPS):
                ins = eng.matmul(joint_bank(k), NT5[:, k, :], V5[:, k * D:(k + 1) * D], start=True, stop=True)
            ins.then_inc(joint_out_ready, 1)
            turn(8, Z)
            eng.wait_ge(turned_copied, t * 8 + 8)
            for g in range(G):
                ins = eng.matmul(M[:, g * HE:(g + 1) * HE], cols(ZT, g), w_gat[:, :], start=True, stop=True)
            ins.then_inc(gat_ready, 1)

        def hold(eng, sem, value, ticks):
            eng.wait_ge(sem, value)
            eng.sem_inc(ticks, 1)

        def load_x(eng, t):
            eng.dma_start(XIN[:, :, :], x_in[bass.ds(t * G, G)].rearrange("g n d -> n g d")).then_inc(x_loaded, 16)

        def load_adj(eng, t):
            eng.dma_start(A[:, :, :], adj_in[bass.ds(t * G, G)].rearrange("g n m -> n g m")).then_inc(adj_loaded, 16)

        def load_adjT(eng, t):
            eng.dma_start(AT[:, :, :], adjT_in[bass.ds(t * G, G)].rearrange("g n m -> n g m")).then_inc(adj_loaded, 16)

        def load_blocks(eng, t):
            for g in range(G):
                eng.dma_start(ABIN[g * JOINTS:(g + 1) * JOINTS, g * JOINTS:(g + 1) * JOINTS],
                              adj_in[bass.ds(t * G + g, 1), 0:JOINTS, 0:JOINTS].rearrange("g n m -> n (g m)"))\
                    .then_inc(blocks_loaded, 16)

        def sync_network(eng, t, more=True):
            if more:
                hold(eng, adj_rows_used, t + 1, sync_ticks)
                load_adj(eng, t + 1)
                hold(eng, x_used, t + 1, sync_ticks)
                load_x(eng, t + 1)
                hold(eng, mixed2_ready, t + 1, sync_ticks)
                load_adjT(eng, t + 1)
            hold(eng, joints_ready, t + 1, sync_ticks)
            for g in range(G):
                eng.dma_start(ZS[g * JOINTS:(g + 1) * JOINTS, :], Z[0:JOINTS, g, :]).then_inc(joints_stacked, 16)
            if more:
                hold(eng, joint_degrees_ready, t + 1, sync_ticks)
                load_blocks(eng, t + 1)
            hold(eng, fused_ready, t + 1, sync_ticks)
            for g in range(G):
                eng.dma_start(FB[:, g, :], F[g * JOINTS:(g + 1) * JOINTS, :]).then_inc(fused_back, 16)
            hold(eng, table_ready, t + 1, sync_ticks)
            eng.dma_start(table[bass.ds(t * G * N, G * N), :].rearrange("(g n) c -> n g c", g=G),
                          TAB[:, :, :]).then_inc(results_stored, 16)
            eng.dma_start(x_mid[bass.ds(t, 1)].rearrange("t p c -> p (t c)"),
                          X[:, :, :].rearrange("p g d -> p (g d)")).then_inc(results_stored, 16)
            eng.dma_start(zT_mid[bass.ds(t, 1)].rearrange("t p c -> p (t c)"), ZT[:, :]).then_inc(results_stored, 16)

        def vector_prepare_low(eng, link):
            eng.wait_ge(edges_loaded, 32)
            eng.wait_ge(loops_made, 1)
            link(eng.tensor_copy(POS.bitcast(I32)[:, 0:LOOPS], loop_ids[:, :]))
            link(eng.tensor_copy(VAL.bitcast(I32)[:, 0:LOOPS], loop_ids[:, :]))
            for c in range(0, TILES, CHUNK):
                cs = slice(c, c + CHUNK)
                link(eng.tensor_scalar(bits[:, :], POS.bitcast(I32)[:, cs], 7, None, ALU.logical_shift_right))
                link(eng.tensor_copy(high[:, cs], bits[:, :]))
                link(eng.tensor_scalar(bits[:, :], POS.bitcast(I32)[:, cs], 127, None, ALU.bitwise_and))
                link(eng.tensor_copy(digit[:, cs], bits[:, :]))
                link(eng.tensor_scalar(bitsf, high[:, cs], 127.5, 128.0, ALU.is_gt, ALU.mult))
                link(eng.tensor_tensor(digit[:, cs], digit[:, cs], bitsf, ALU.add))
                link(eng.tensor_scalar(bitsf, VAL.bitcast(I32)[:, cs], float(NODES - 1), None, ALU.min))
                link(eng.scalar_tensor_tensor(VAL[:, cs], high[:, cs], float(NODES), bitsf, ALU.mult, ALU.add))
            link(eng.tensor_scalar(VAL[:, 0:LOOPS], VAL[:, 0:LOOPS], float(LOOP_BIT), None, ALU.add))

        def onehot_of(eng, out, digits, column):
            return eng.tensor_tensor(out, iota[:, :].unsqueeze(1).broadcast_to([P, 4, P]),
                                     digits[:, bass.ds(column, 4)].unsqueeze(2).broadcast_to([P, 4, P]), ALU.is_equal)

        def vector_count(eng, t):
            for u in range(UNROLL):
                b = u % 2
                eng.wait_ge(pairs_counted, t * UNROLL + max(u - 1, 0))
                onehot_of(eng, OH[:, b, :, :], digit, t * 4 * UNROLL + 4 * u)
                onehot_of(eng, OH2[:, b, :, :], high, t * 4 * UNROLL + 4 * u).then_inc(pairs_ready, 1)

        def tensor_count(eng, t):
            for u in range(UNROLL):
                b = u % 2
                eng.wait_ge(pairs_ready, t * UNROLL + u + 1)
                for k in range(4):
                    ins = eng.matmul(M[:, 0:P], OH[:, b, k, :], OH2[:, b, k, :], start=False, stop=False,
                                     skip_group_check=True)
                ins.then_inc(pairs_counted, 1)

        def vector_bases(eng, link):
            eng.wait_ge(counts_ready, 1)
            eng.tensor_copy(count[:, :], M[:, 0:P]).then_inc(count_copied, 1)
            eng.wait_ge(sums_ready, 1)
            for bank, base in ((Y[0], base_low), (Y[1], base_high)):
                total = bank[:, 0, :]
                link(eng.tensor_copy(totals[:, :], total))
                link(eng.tensor_tensor_scan(base[:, :], totals[:, :], zeros[:, :], 0.0, ALU.add, ALU.add))
                link(eng.tensor_tensor(base[:, :], base[:, :], totals[:, :], ALU.subtract))
            link(eng.tensor_tensor(first_place[:, :], Y[0][:, 1, :], base_high[:, :], ALU.add))
            link(eng.tensor_tensor(last_place[:, :], first_place[:, :], count[:, :], ALU.add))
            link(eng.tensor_scalar(last_place[:, :], last_place[:, :], -1.0, None, ALU.add))

        def tensor_bases(eng):
            eng.wait_ge(count_copied, 1)
            eng.transpose(T[:, 0:P], count[:, :], ident[:, :]).then_inc(count_turned, 1)
            eng.wait_ge(count_turn_copied, 1)
            eng.matmul(Y[0][:, 0, :], ones[:, :], countT[:, :], start=True, stop=True)
            eng.matmul(Y[1][:, 0, :], ones[:, :], count[:, :], start=True, stop=True)
            eng.matmul(Y[0][:, 1, :], before[:, :], count[:, :], start=True, stop=True).then_inc(sums_ready, 1)

        def vector_rank(eng, t, s, link):
            q = t * UNROLL

            def build(u):
                onehot_of(eng, OH[:, u % 2, :, :], digit, (t - s * TURNS) * 4 * UNROLL + 4 * u).then_inc(onehots_ready, 1)

            build(0)
            for u in range(UNROLL):
                if u + 1 < UNROLL:
                    build(u + 1)
                eng.wait_ge(prefixes_ready, q + u + 1)
                link(eng.tensor_tensor(places[:, :, :], HP[u % 2][:, :].rearrange("p (k d) -> p k d", k=4),
                                       run[:, u % 2, :].unsqueeze(1).broadcast_to([P, 4, P]), ALU.add))
                link(eng.tensor_tensor(places[:, :, :], places[:, :, :], OH[:, u % 2, :, :], ALU.mult))
                eng.tensor_reduce(place16[:, 4 * u:4 * u + 4], places[:, :, :], AX.X, ALU.add)
                eng.tensor_tensor(run[:, (u + 1) % 2, :], run[:, u % 2, :], Y[u % 2][:, 0, :], ALU.add)\
                    .then_inc(ranks_taken, 1)
                eng.wait_ge(ranks_taken, q + u + 1)
            here = bass.ds((t - s * TURNS) * 4 * UNROLL, 4 * UNROLL)
            link(eng.tensor_scalar(skip16[:, :], digit[:, here], 127.5, float(FAR), ALU.is_gt, ALU.mult))
            eng.tensor_tensor(POS.bitcast(I32)[:, here], place16[:, :], skip16[:, :], ALU.add).then_inc(places_ready, 1)

        def tensor_rank(eng, t):
            q = t * UNROLL
            for u in range(UNROLL):
                b = u % 2
                prefix, total = HP[b], Y[b][:, 0, :]
                eng.wait_ge(onehots_ready, q + u + 1)
                if u >= 2:
                    eng.wait_ge(ranks_taken, q + u - 1)
                flat = OH[:, b, :, :].rearrange("p k d -> p (k d)")
                eng.matmul(prefix[:, :], before_b[:, :], flat, start=True, stop=False)
                for k in range(3):
                    later = OH[:, b, k, :].unsqueeze(1).broadcast_to([P, 3 - k, P])
                    eng.matmul(prefix[:, (k + 1) * P:].rearrange("p (k d) -> p k d", d=P), ones_b[:, :], later,
                               start=False, stop=(k == 2))
                for k in range(4):
                    ins = eng.matmul(total, ones_b[:, :], OH[:, b, k, :], start=(k == 0), stop=(k == 3))
                ins.then_inc(prefixes_ready, 1)

        def pool_scatter(eng, t, s, target, dt):
            for half in range(2):
                here = bass.ds((t - s * SCATTERS) * 32 + 16 * half, 16)
                hold(eng, places_ready, t * 2 + half + 1, pool_ticks)
                hold(eng, scattered[2 * s + half], (t - s * SCATTERS) * 256, pool_ticks)
                eng.tensor_copy(stage_place[:, half, :], POS.bitcast(I32)[:, here])
                eng.tensor_copy(stage_value[:, half, :].bitcast(I32), VAL.bitcast(I32)[:, here]).then_inc(staged, 1)
                hold(eng, staged, t * 2 + half + 1, pool_ticks)
                for j in range(16):
                    eng.indirect_dma_start(target, bass.IndirectOffsetOnAxis(stage_place[:, half, j:j + 1].bitcast(U32), 0),
                                           stage_value[:, half, j:j + 1].bitcast(dt), None,
                                           bounds_check=PLACES - 1, oob_is_err=False).then_inc(scattered[2 * s + half], 16)

        def vector_prepare_high(eng, link):
            eng.wait_ge(blocks_turned_copied, BLOCKS)
            for c in range(0, TILES, CHUNK):
                cs = slice(c, c + CHUNK)
                link(eng.tensor_copy(bits[:, :], VAL[:, cs]))
                link(eng.tensor_scalar(bits2[:, :], bits[:, :], 14, 127, ALU.logical_shift_right, ALU.bitwise_and))
                link(eng.tensor_copy(digit[:, cs], bits2[:, :]))
                link(eng.tensor_scalar(high[:, cs], VAL[:, cs], EMPTY - 0.5, 128.0, ALU.is_gt, ALU.mult))
                link(eng.tensor_tensor(digit[:, cs], digit[:, cs], high[:, cs], ALU.add))
                link(eng.tensor_scalar(bits[:, :], bits[:, :], NODES - 1, None, ALU.bitwise_and))
                link(eng.tensor_scalar(VAL[:, cs], VAL[:, cs], LOOP_BIT - 0.5, float(NODES), ALU.is_gt, ALU.mult))
                link(eng.tensor_tensor(VAL.bitcast(I32)[:, cs], VAL[:, cs], bits[:, :], ALU.add))

        def tensor_turn_blocks(eng):
            eng.wait_ge(sorted_loaded, 16)
            for c in range(BLOCKS):
                if c >= 2:
                    eng.wait_ge(blocks_turned_copied, c - 1)
                eng.transpose(HP[c % 2][:, 0:P], POS[:, c * P:(c + 1) * P], ident[:, :]).then_inc(blocks_turned, 1)

        def scalar_turn_blocks(eng):
            for c in range(BLOCKS):
                eng.wait_ge(blocks_turned, c + 1)
                eng.activation(VAL[:, c * P:(c + 1) * P], HP[c % 2][:, 0:P], ACT.Copy).then_inc(blocks_turned_copied, 1)

        def vector_owner(eng, link):
            for c in range(0, P, OWN):
                cuts = cut_row[:, c:c + OWN].unsqueeze(2).broadcast_to([P, OWN, P])
                link(eng.tensor_tensor(begun[:, :, :], first_place[:, :].unsqueeze(1).broadcast_to([P, OWN, P]), cuts,
                                       ALU.is_le))
                ins = eng.tensor_reduce(begun_sum[:, c:c + OWN], begun[:, :, :], AX.X, ALU.add)
                if c + OWN < P:
                    link(ins)
            ins.then_inc(begun_ready, 1)
            eng.wait_ge(owner_ready, 1)
            eng.tensor_scalar(owner[:, :], M[:, 0:1], -1.0, None, ALU.add).then_inc(owner_written, 1)
            link(eng.tensor_copy(end_place[:, :], last_place[:, :]))
            link(eng.tensor_scalar(node_a[:, :], last_place[:, :], 1.0 / WIDTH, None, ALU.mult))
            link(eng.tensor_copy(end_part[:, :], node_a[:, :]))
            link(eng.tensor_copy(node_a[:, :], end_part[:, :]))
            link(eng.scalar_tensor_tensor(node_b[:, :], node_a[:, :], -float(WIDTH), last_place[:, :], ALU.mult, ALU.add))
            link(eng.tensor_scalar(node_c[:, :], node_b[:, :], 0.0, None, ALU.is_lt))
            link(eng.tensor_tensor(node_a[:, :], node_a[:, :], node_c[:, :], ALU.subtract))
            link(eng.tensor_scalar(node_c[:, :], node_b[:, :], float(WIDTH), None, ALU.is_ge))
            link(eng.tensor_tensor(node_a[:, :], node_a[:, :], node_c[:, :], ALU.add))
            link(eng.tensor_copy(end_part[:, :], node_a[:, :]))
            link(eng.scalar_tensor_tensor(node_b[:, :], node_a[:, :], float(WIDTH), first_place[:, :], ALU.mult,
                                          ALU.is_le))
            eng.tensor_scalar(uncut[:, :], node_b[:, :], -HUGE, None, ALU.mult).then_inc(ends_ready, 1)

        def vector_scan_start(eng, link):
            eng.memset(adst_run[:, 1, :, :], 0.0)
            eng.memset(high_run[:, 1, :, :], -BIG)
            eng.memset(loops_seen[:, :], 0.0)
            link(eng.memset(states[:, 1, :, :], 0.0))
            eng.wait_ge(owner_row_loaded, 16)
            eng.tensor_copy(adst_run[:, 1, :, SPAN - 1], owner_row[:, HE + HEADS:ROW]).then_inc(states_ready, 1)
            eng.wait_ge(states_ready, 1)

        def vector_sources(eng, t, h, link):
            eng.wait_ge(indices_loaded[h], t * 16 + 16)
            link(eng.tensor_scalar(bits[:, 0:SPAN], indices[:, h, :], 14, None, ALU.logical_shift_right))
            link(eng.tensor_copy(loop_here[:, h, :], bits[:, 0:SPAN]))
            eng.tensor_scalar(source[:, h, :], indices[:, h, :], NODES - 1, None, ALU.bitwise_and)\
                .then_inc(sources_ready, 1)

        def vector_scan(eng, t, h, link):
            o = 1 - h
            n = t * 2 + h
            loops = loop_here[:, h, :]
            link(eng.tensor_scalar(going[:, :], loops, -1.0, 1.0, ALU.mult, ALU.add))
            link(eng.tensor_scalar(restart[:, :], loops, -HUGE, None, ALU.mult))
            link(eng.tensor_reduce(loop_any[:, :], loops, AX.X, ALU.max))
            link(eng.tensor_tensor(loops_seen[:, :], loops_seen[:, :], loop_any[:, :], ALU.max))
            eng.wait_ge(gathered[h], (t + 1) * (SPAN * 16))
            rows = rows_in[:, h, :].rearrange("p (c f) -> p c f", f=ROW)

            def each_head(x):
                return x.unsqueeze(1).broadcast_to([P, HEADS, SPAN])

            link(eng.tensor_tensor(adst[:, :, :], rows[:, :, HE + HEADS:ROW].rearrange("p c h -> p h c"),
                                   each_head(loops), ALU.mult))
            for k in range(HEADS):
                ins = eng.tensor_tensor_scan(adst_run[:, h, k, :], going[:, :], adst[:, k, :],
                                             adst_run[:, o, k, SPAN - 1:SPAN], ALU.mult, ALU.add)
            link(ins)
            link(eng.tensor_tensor(score[:, :, :], rows[:, :, HE:HE + HEADS].rearrange("p c h -> p h c"),
                                   adst_run[:, h, :, :], ALU.add))
            link(eng.scalar_tensor_tensor(score[:, :, :], score[:, :, :], 0.2, score[:, :, :], ALU.mult, ALU.max))
            link(eng.tensor_copy(high_run[:, h, :, 0], high_run[:, o, :, SPAN]))
            for k in range(HEADS):
                ins = eng.tensor_tensor_scan(high_run[:, h, k, 1:SPAN + 1], restart[:, :], score[:, k, :],
                                             high_run[:, h, k, 0:1], ALU.add, ALU.max)
            link(ins)
            link(eng.tensor_tensor(decay[:, :, :], high_run[:, h, :, 0:SPAN], each_head(restart[:, :]), ALU.add))
            link(eng.tensor_tensor(decay[:, :, :], decay[:, :, :], high_run[:, h, :, 1:SPAN + 1], ALU.subtract))
            eng.tensor_tensor(mass[:, :, :], score[:, :, :], high_run[:, h, :, 1:SPAN + 1],
                              ALU.subtract).then_inc(exponents_ready, 1)
            eng.wait_ge(exps_ready, n + 1)
            for k in range(HEADS):
                ins = eng.tensor_tensor(weighed[:, EXPERTS * k:EXPERTS * (k + 1), :],
                                        rows[:, :, EXPERTS * k:EXPERTS * (k + 1)].rearrange("p c e -> p e c"),
                                        mass[:, k, :].unsqueeze(1).broadcast_to([P, EXPERTS, SPAN]), ALU.mult)
            link(ins)
            eng.wait_ge(states_stored[h], t * 16)
            for k in range(HEADS):
                eng.tensor_tensor_scan(states[:, h, :, HEADS + k], decay[:, k, :], mass[:, k, :],
                                       states[:, o, SPAN - 1:SPAN, HEADS + k], ALU.mult, ALU.add)
            for k in range(HE):
                eng.tensor_tensor_scan(states[:, h, :, 2 * HEADS + k], decay[:, k // EXPERTS, :], weighed[:, k, :],
                                       states[:, o, SPAN - 1:SPAN, 2 * HEADS + k], ALU.mult, ALU.add)
            eng.tensor_copy(states[:, h, :, 0:HEADS], high_run[:, h, :, 1:SPAN + 1].rearrange("p h c -> p c h"))\
                .then_inc(states_ready, 1)
            eng.wait_ge(states_ready, n + 2)

        def vector_scan_turn(eng, t, more=True):
            count = [0]

            def link(ins):
                ins.then_inc(scan_steps, 1)
                count[0] += 1
                eng.wait_ge(scan_steps, t * SCAN_STEPS + count[0] + 2)

            vector_sources(eng, t, 1, link)
            vector_scan(eng, t, 0, link)
            if more:
                vector_sources(eng, t + 1, 0, link)
            vector_scan(eng, t, 1, link)
            assert count[0] == SCAN_STEPS - (0 if more else 2), count[0]

        def scalar_scan(eng, t):
            for h in range(2):
                eng.wait_ge(exponents_ready, t * 2 + h + 1)
                eng.activation(decay[:, :, :], decay[:, :, :], ACT.Exp)
                eng.activation(mass[:, :, :], mass[:, :, :], ACT.Exp).then_inc(exps_ready, 1)

        def pool_gather(eng, t):
            for h in range(2):
                hold(eng, sources_ready, t * 2 + h + 1, pool_ticks)
                hold(eng, states_ready, t * 2 + h, pool_ticks)
                for j in range(SPAN):
                    eng.indirect_dma_start(rows_in[:, h, j * ROW:(j + 1) * ROW], None, table,
                                           bass.IndirectOffsetOnAxis(source[:, h, j:j + 1].bitcast(U32), 0),
                                           bounds_check=NODES - 1, oob_is_err=False).then_inc(gathered[h], 16)

        def load_indices(eng, t, h):
            eng.dma_start(indices[:, h, :], order_rows[:, bass.ds((t * 2 + h) * SPAN, SPAN)]).then_inc(indices_loaded[h], 16)

        def sync_scan(eng, t, more=True):
            for h in range(2):
                if more:
                    hold(eng, sources_ready, t * 2 + h + 1, sync_ticks)
                    load_indices(eng, t + 1, h)
                hold(eng, states_ready, t * 2 + h + 2, sync_ticks)
                eng.dma_start(state_rows[:, bass.ds((t * 2 + h) * (SPAN * ROW), SPAN * ROW)],
                              states[:, h, :, :].rearrange("p c f -> p (c f)")).then_inc(states_stored[h], 16)

        def vector_chain(eng, link):
            link(eng.tensor_copy(chain_in[:, 0, 0:HEADS], states[:, 1, SPAN - 1, 0:HEADS]))
            link(eng.tensor_copy(chain_in[:, 0, HEADS:CARRY].rearrange("p (h e) -> p h e", h=HEADS),
                                 states[:, 1, SPAN - 1, 0:HEADS].unsqueeze(2).broadcast_to([P, HEADS, EXPERTS])))
            link(eng.tensor_copy(chain_in[:, 1, :], states[:, 1, SPAN - 1, HEADS:ROW]))
            eng.tensor_copy(chain_in[:, 2, :], loops_seen[:, 0:1].broadcast_to([P, CARRY])).then_inc(chain_in_ready, 1)
            eng.wait_ge(chain_turned, 1)
            for k in range(3):
                ins = eng.tensor_copy(chain[:, k, :], T[0:CARRY, k * P:(k + 1) * P])
            link(ins)
            maximum, sums, loop = chain[:, 0, :], chain[:, 1, :], chain[:, 2, :]
            link(eng.tensor_scalar(loop, loop, -HUGE, None, ALU.mult))
            link(eng.memset(chain_high[:, 0:1], -BIG))
            link(eng.tensor_tensor_scan(chain_high[:, 1:P + 1], loop, maximum, chain_high[:, 0:1], ALU.add, ALU.max))
            link(eng.tensor_tensor(loop, loop, chain_high[:, 0:P], ALU.add))
            link(eng.tensor_tensor(loop, loop, chain_high[:, 1:P + 1], ALU.subtract))
            eng.tensor_tensor(maximum, maximum, chain_high[:, 1:P + 1], ALU.subtract).then_inc(chain_exponents_ready, 1)
            eng.wait_ge(chain_exps_ready, 1)
            link(eng.tensor_tensor(sums, sums, maximum, ALU.mult))
            link(eng.memset(chain_sum[:, 0:1], 0.0))
            eng.tensor_tensor_scan(chain_sum[:, 1:P + 1], loop, sums, chain_sum[:, 0:1], ALU.mult, ALU.add)\
                .then_inc(chain_ready, 1)
            eng.wait_ge(chain_back, 1)
            eng.tensor_copy(carry_out[:, 0:CARRY], T[:, 0:CARRY])
            eng.tensor_copy(carry_out[:, CARRY:2 * CARRY], T[:, CARRY:2 * CARRY]).then_inc(carry_ready, 1)

        def tensor_chain(eng):
            eng.wait_ge(chain_in_ready, 1)
            for k in range(3):
                ins = eng.transpose(T[0:CARRY, k * P:(k + 1) * P], chain_in[:, k, :], ident[:, :])
            ins.then_inc(chain_turned, 1)
            eng.wait_ge(chain_ready, 1)
            eng.transpose(T[:, 0:CARRY], chain_high[:, 0:P], ident[0:CARRY, 0:CARRY])
            eng.transpose(T[:, CARRY:2 * CARRY], chain_sum[:, 0:P], ident[0:CARRY, 0:CARRY]).then_inc(chain_back, 1)

        def pool_tail(eng, t):
            hold(eng, node_rows_used, t, pool_ticks)
            eng.tensor_copy(tail_index[:, 0, :], end_place.bitcast(I32)[:, bass.ds(t * G, G)])
            eng.tensor_copy(tail_index[:, 1, :], end_part.bitcast(I32)[:, bass.ds(t * G, G)]).then_inc(tail_staged, 1)
            hold(eng, tail_staged, t + 1, pool_ticks)
            for g in range(G):
                eng.indirect_dma_start(node_states[:, g * ROW:(g + 1) * ROW], None,
                                       state_rows.rearrange("p (c f) -> (p c) f", f=ROW),
                                       bass.IndirectOffsetOnAxis(tail_index[:, 0, g:g + 1].bitcast(U32), 0),
                                       bounds_check=PLACES - 1, oob_is_err=False).then_inc(node_rows_loaded, 16)
                eng.indirect_dma_start(node_carry[:, g * 2 * CARRY:(g + 1) * 2 * CARRY], None, carry_rows,
                                       bass.IndirectOffsetOnAxis(tail_index[:, 1, g:g + 1].bitcast(U32), 0),
                                       bounds_check=P - 1, oob_is_err=False).then_inc(node_rows_loaded, 16)

        def vector_tail(eng, t):
            count = [0]

            def link(ins):
                ins.then_inc(tail_steps, 1)
                count[0] += 1
                eng.wait_ge(tail_steps, t * TAIL_STEPS + count[0])

            eng.wait_ge(node_rows_loaded, t * 32 * G + 32 * G)
            own = node_states[:, :].rearrange("p (g f) -> p g f", g=G)
            taken = node_carry[:, :].rearrange("p (g f) -> p g f", g=G)
            link(eng.tensor_copy(own_high[:, :, 0:HEADS], own[:, :, 0:HEADS]))
            for g in range(G):
                ins = eng.tensor_copy(own_high[:, g, HEADS:CARRY].rearrange("p (h e) -> p h e", h=HEADS),
                                      own[:, g, 0:HEADS].unsqueeze(2).broadcast_to([P, HEADS, EXPERTS]))
            link(ins)
            link(eng.tensor_tensor(taken_high[:, :, :], taken[:, :, 0:CARRY],
                                   uncut[:, bass.ds(t * G, G)].unsqueeze(2).broadcast_to([P, G, CARRY]), ALU.add))
            link(eng.tensor_tensor(both_high[:, :, :], own_high[:, :, :], taken_high[:, :, :], ALU.max))
            link(eng.tensor_tensor(own_high[:, :, :], own_high[:, :, :], both_high[:, :, :], ALU.subtract))
            eng.tensor_tensor(taken_high[:, :, :], taken_high[:, :, :], both_high[:, :, :],
                              ALU.subtract).then_inc(node_exponents_ready, 1)
            eng.wait_ge(node_exps_ready, t + 1)
            link(eng.tensor_tensor(own_high[:, :, :], own_high[:, :, :], own[:, :, HEADS:ROW], ALU.mult))
            link(eng.tensor_tensor(taken_high[:, :, :], taken_high[:, :, :], taken[:, :, CARRY:2 * CARRY], ALU.mult))
            eng.tensor_tensor(own_high[:, :, :], own_high[:, :, :], taken_high[:, :, :], ALU.add)\
                .then_inc(node_rows_used, 1)
            eng.wait_ge(node_rows_used, t + 1)
            link(eng.tensor_scalar(denominator[:, :, :], own_high[:, :, 0:HEADS], 1e-16, None, ALU.add))
            link(eng.reciprocal(denominator[:, :, :], denominator[:, :, :]))
            for g in range(G):
                ins = eng.tensor_tensor(agg[:, g, :].rearrange("p (h e) -> p h e", h=HEADS),
                                        own_high[:, g, HEADS:CARRY].rearrange("p (h e) -> p h e", h=HEADS),
                                        denominator[:, g, :].unsqueeze(2).broadcast_to([P, HEADS, EXPERTS]), ALU.mult)
            link(ins)

            def wide(x):
                return x.unsqueeze(1).broadcast_to([P, G, HE])

            def over(x, n=HE):
                return x.unsqueeze(2).broadcast_to([P, G, n])

            link(eng.tensor_tensor(agg[:, :, :], agg[:, :, :], wide(row("L3_ffn_b_gat")), ALU.add))
            link(eng.tensor_reduce(peak[:, :], agg[:, :, :], AX.X, ALU.add))
            link(eng.tensor_scalar(peak[:, :], peak[:, :], 1.0 / HE, None, ALU.mult))
            link(eng.tensor_tensor(agg[:, :, :], agg[:, :, :], over(peak[:, :]), ALU.subtract))
            link(eng.tensor_tensor(gat_part[:, :, :], agg[:, :, :], agg[:, :, :], ALU.mult))
            link(eng.tensor_reduce(peak[:, :], gat_part[:, :, :], AX.X, ALU.add))
            eng.tensor_scalar(peak[:, :], peak[:, :], 1.0 / HE, None, ALU.mult).then_inc(agg_variance_ready, 1)
            eng.wait_ge(agg_deviation_ready, t + 1)
            link(eng.reciprocal(rstd[:, :], deviation[:, :]))
            link(eng.tensor_tensor(agg[:, :, :], agg[:, :, :], over(rstd[:, :]), ALU.mult))
            link(eng.tensor_tensor(agg[:, :, :], agg[:, :, :], wide(row("L3_ffn_ln_gamma")), ALU.mult))
            link(eng.tensor_tensor(agg[:, :, :], agg[:, :, :], wide(row("L3_ffn_ln_beta")), ALU.add))
            link(eng.tensor_reduce(logits[:, :, 0:EXPERTS], agg[:, :, :].rearrange("p g (h e) -> p g e h", h=HEADS),
                                   AX.X, ALU.add))
            link(eng.tensor_scalar(logits[:, :, 0:EXPERTS], logits[:, :, 0:EXPERTS], 1.0 / HEADS, None, ALU.mult))
            small = logits[:, :, 0:EXPERTS]
            ch, se = chosen[:, :, 0:EXPERTS], second[:, :, 0:EXPERTS]
            first_largest(eng, link, ch, small, EXPERTS)
            link(eng.tensor_copy(top[:, 0, :], peak[:, :]))
            link(eng.scalar_tensor_tensor(small, ch, -BIG, small, ALU.mult, ALU.add))
            first_largest(eng, link, se, small, EXPERTS)
            eng.tensor_tensor(top[:, 1, :], peak[:, :], top[:, 0, :], ALU.subtract).then_inc(tail_gap_ready, 1)
            eng.wait_ge(tail_gap_exp_ready, t + 1)
            link(eng.tensor_scalar(top[:, 0, :], gap_exp[:, :], 1.0, None, ALU.add))
            link(eng.reciprocal(top[:, 1, :], top[:, 0, :]))
            link(eng.tensor_tensor(top[:, 0, :], gap_exp[:, :], top[:, 1, :], ALU.mult))
            link(eng.tensor_tensor(ch, ch, over(top[:, 1, :], EXPERTS), ALU.mult))
            link(eng.tensor_tensor(se, se, over(top[:, 0, :], EXPERTS), ALU.mult))
            eng.tensor_tensor(tail_gate[:, :, :], ch, se, ALU.add).then_inc(tail_gate_ready, 1)
            eng.wait_ge(tail_gate_ready, t + 1)
            eng.wait_ge(tail_x_loaded, t * 16 + 16)
            for e in range(EXPERTS):
                eng.wait_ge(tail_outputs_ready, t * EXPERTS + e + 1)
                for g in range(G):
                    ins = eng.scalar_tensor_tensor(X[:, g, :], Y[e % 2][:, g, :], tail_gate[:, g, e:e + 1], X[:, g, :],
                                                   ALU.mult, ALU.add)
                ins.then_inc(tail_outputs_used, 1)
                eng.wait_ge(tail_outputs_used, t * EXPERTS + e + 1)
            eng.wait_ge(tail_bias_ready, t + 1)
            eng.wait_ge(out_stored, t * 16)
            eng.tensor_tensor(XIN[:, :, :], X[:, :, :], BS[:, :, :], ALU.add).then_inc(out_ready, 1)
            assert count[0] == TAIL_STEPS, count[0]

        def scalar_tail(eng, t):
            for n in range(8):
                eng.wait_ge(tail_hidden_ready, t * 8 + n + 1)
                if n >= 4:
                    eng.wait_ge(tail_outputs_ready, t * EXPERTS + n // 2 - 1)
                eng.activation(HT[:, n % 4, :], HP[n % 2][:, :], ACT.Gelu, bias=b1_4[:, n:n + 1])\
                    .then_inc(tail_hidden_done, 1)
                if n == 3:
                    eng.wait_ge(node_exponents_ready, t + 1)
                    eng.activation(own_high[:, :, :], own_high[:, :, :], ACT.Exp)
                    eng.activation(taken_high[:, :, :], taken_high[:, :, :], ACT.Exp).then_inc(node_exps_ready, 1)
                    eng.wait_ge(agg_variance_ready, t + 1)
                    eng.activation(deviation[:, :], peak[:, :], ACT.Sqrt, bias=eps[:, 0:1])\
                        .then_inc(agg_deviation_ready, 1)
                    eng.wait_ge(tail_gap_ready, t + 1)
                    eng.activation(gap_exp[:, :], top[:, 1, :], ACT.Exp).then_inc(tail_gap_exp_ready, 1)
            eng.wait_ge(tail_gates_turned, t + 1)
            eng.activation(CT[0:G * EXPERTS, :], M[0:G * EXPERTS, 0:P], ACT.Copy).then_inc(tail_gate_columns_ready, 1)

        def tensor_tail(eng, t):
            def hidden(n):
                if n >= 2:
                    eng.wait_ge(tail_hidden_done, t * 8 + n - 1)
                eng.matmul(HP[n % 2][:, :], w1_4[:, n * D:(n + 1) * D], ZT[:, :], start=True, stop=True)\
                    .then_inc(tail_hidden_ready, 1)

            eng.wait_ge(tail_z_loaded, t * 16 + 16)
            eng.wait_ge(tail_hidden_done, t * 8)
            hidden(0)
            hidden(1)
            for e in range(EXPERTS):
                if e + 1 < EXPERTS:
                    hidden(2 * e + 2)
                    hidden(2 * e + 3)
                eng.wait_ge(tail_hidden_done, t * 8 + 2 * e + 2)
                eng.wait_ge(tail_outputs_used, t * EXPERTS + max(e - 1, 0))
                for g in range(G):
                    for c in range(2):
                        n = 2 * e + c
                        ins = eng.matmul(Y[e % 2][:, g, :], HT[:, n % 4, g * N:(g + 1) * N], w2_4[:, n * D:(n + 1) * D],
                                         start=(c == 0), stop=(c == 1))
                ins.then_inc(tail_outputs_ready, 1)
            eng.wait_ge(tail_gate_ready, t + 1)
            eng.transpose(M[0:G * EXPERTS, 0:P], tail_gate[:, :, :].rearrange("p g e -> p (g e)"),
                          ident[:, :]).then_inc(tail_gates_turned, 1)
            eng.wait_ge(tail_gate_columns_ready, t + 1)
            eng.wait_ge(out_ready, t)
            eng.matmul(BS[:, :, :].rearrange("p g n -> p (g n)"), CT[0:G * EXPERTS, :], b2_4[:, :], start=True,
                       stop=True).then_inc(tail_bias_ready, 1)

        def load_tail_z(eng, t):
            eng.dma_start(ZT[:, :], zT_mid[bass.ds(t, 1)].rearrange("t p c -> p (t c)")).then_inc(tail_z_loaded, 16)

        def load_tail_x(eng, t):
            eng.dma_start(X[:, :, :].rearrange("p g d -> p (g d)"),
                          x_mid[bass.ds(t, 1)].rearrange("t p c -> p (t c)")).then_inc(tail_x_loaded, 16)

        def sync_tail(eng, t, more=True):
            if more:
                hold(eng, tail_outputs_ready, (t + 1) * EXPERTS, sync_ticks)
                load_tail_z(eng, t + 1)
            hold(eng, out_ready, t + 1, sync_ticks)
            if more:
                load_tail_x(eng, t + 1)
            eng.dma_start(out[bass.ds(t * G, G)].rearrange("g n d -> n g d"), XIN[:, :, :]).then_inc(out_stored, 16)

        def pool_setup(eng):
            eng.iota(loop_ids[:, :], [[P, LOOPS]], base=0, channel_multiplier=1).then_inc(loops_made, 1)

        def sync_setup(eng):
            eng.dma_start(consts[:, :], consts_in).then_inc(consts_loaded, 16)
            eng.dma_start(row_tile[:, :], rows_in_dram.partition_broadcast(P)).then_inc(consts_loaded, 16)
            eng.dma_start(POS.bitcast(I32)[:, LOOPS:TILES], edges[1].rearrange("(p c) -> p c", p=P))\
                .then_inc(edges_loaded, 16)
            eng.dma_start(VAL.bitcast(I32)[:, LOOPS:TILES], edges[0].rearrange("(p c) -> p c", p=P))\
                .then_inc(edges_loaded, 16)
            load_x(eng, 0)
            load_adj(eng, 0)
            load_adjT(eng, 0)
            for name, _ in MATS:
                eng.dma_start(mat[name][:, :], mats[name]).then_inc(weights_loaded, 16)
            eng.wait_ge(cleared, 1)
            for tile, bias, n in ((b2_0, 0, 8), (b2_1, 1, 8), (b2_4, 2, EXPERTS)):
                for g in range(G):
                    eng.dma_start(tile[g * n:(g + 1) * n, g * D:(g + 1) * D], expert_biases[bias])\
                        .then_inc(weights_loaded, 16)
            load_blocks(eng, 0)
            for c in range(4):
                eng.dma_start(by_low.rearrange("(p c) o -> p (c o)", p=P)[:, c * CHUNK:(c + 1) * CHUNK],
                              bits2[:, :].bitcast(F32)).then_inc(places_blanked, 16)
                eng.dma_start(order_rows[:, c * CHUNK:(c + 1) * CHUNK], high[:, 0:2 * CHUNK].bitcast(I32))\
                    .then_inc(places_blanked, 16)

        def vector_setup(eng, link):
            eng.memset(b2_0[:, :], 0.0)
            eng.memset(b2_1[:, :], 0.0)
            eng.memset(b2_4[:, :], 0.0)
            eng.memset(ABIN[:, :], 0.0)
            eng.memset(high[:, :], 0.0)
            eng.memset(bits2[:, :].bitcast(F32), float(EMPTY)).then_inc(cleared, 1)
            eng.memset(ones_b[:, :], 1.0)
            eng.memset(zeros_b[:, :], 0.0)
            eng.memset(ones[:, :], 1.0)
            eng.memset(zeros[:, :], 0.0)
            eng.memset(eps[:, :], EPS)
            link(eng.memset(one[:, :], 1.0))
            eng.wait_ge(consts_loaded, 32)
            eng.tensor_copy(before_b[:, :], before).then_inc(bf_consts_ready, 1)
            link(eng.tensor_tensor(gate_bias0[:, :], row("L0_ffn_bg"), row("L0_ffn_bias"), ALU.add))
            fusion = row("L3_gnn_fusion_w")
            link(eng.tensor_reduce(share_sum[:, :], fusion, AX.X, ALU.max))
            eng.tensor_scalar(share[:, :], fusion, share_sum[:, 0:1], None, ALU.subtract).then_inc(fusion_shifted, 1)
            eng.wait_ge(fusion_exp_ready, 1)
            link(eng.tensor_reduce(share_sum[:, :], share[:, :], AX.X, ALU.add))
            link(eng.reciprocal(share_sum[:, :], share_sum[:, :]))
            link(eng.tensor_scalar(share[:, :], share[:, :], share_sum[:, 0:1], None, ALU.mult))
            link(eng.tensor_tensor(share[:, :], share[:, :], const["joint_share"], ALU.mult))
            eng.wait_ge(weights_loaded, 16 * (len(MATS) + 3 * G))
            eng.tensor_copy(wr_wide[:, :], wr[:, 0:1].broadcast_to([P, P])).then_inc(weights_ready0, 1)

        block = ctx.enter_context(nc.Block())
        HALF = NET_TURNS // 2

        @block.sync
        def _(sp):
            sync_setup(sp)
            with sp.Fori(0, HALF) as t:
                sync_network(sp, t)
            for half in range(2):
                sp.wait_ge(scattered[half], SCATTERS * 256)
            sp.dma_start(POS.rearrange("p (c j) -> p c j", j=P),
                         by_low.rearrange("(c p j) o -> p c (j o)", p=P, j=P)).then_inc(sorted_loaded, 16)
            with sp.Fori(HALF, NET_TURNS - 1) as t:
                sync_network(sp, t)
            sync_network(sp, NET_TURNS - 1, more=False)
            for half in range(2):
                sp.wait_ge(scattered[2 + half], SCATTERS * 256)
            load_indices(sp, 0, 0)
            load_indices(sp, 0, 1)
            with sp.Fori(0, SCAN_TURNS - 1) as t:
                sync_scan(sp, t)
            sync_scan(sp, SCAN_TURNS - 1, more=False)
            load_tail_z(sp, 0)
            load_tail_x(sp, 0)
            sp.wait_ge(carry_ready, 1)
            sp.dma_start(carry_rows, carry_out[:, :]).then_inc(carry_stored, 16)
            with sp.Fori(0, NET_TURNS - 1) as t:
                sync_tail(sp, t)
            sync_tail(sp, NET_TURNS - 1, more=False)
            sp.wait_ge(out_stored, NET_TURNS * 16)
            sp.wait_ge(results_stored, NET_TURNS * 48)
            sp.wait_ge(places_blanked, 128)
            for h in range(2):
                sp.wait_ge(states_stored[h], SCAN_TURNS * 16)

        @block.gpsimd
        def _(pool):
            pool_setup(pool)
            pool.wait_ge(places_blanked, 128)
            with pool.Fori(0, SCATTERS) as t:
                pool_scatter(pool, t, 0, by_low, F32)
            with pool.Fori(SCATTERS, 2 * SCATTERS) as t:
                pool_scatter(pool, t, 1, order, I32)
            pool.wait_ge(owner_written, 1)
            pool.wait_ge(results_stored, NET_TURNS * 48)
            pool.indirect_dma_start(owner_row[:, :], None, table, bass.IndirectOffsetOnAxis(owner[:, :].bitcast(U32), 0),
                                    bounds_check=NODES - 1, oob_is_err=False).then_inc(owner_row_loaded, 16)
            with pool.Fori(0, SCAN_TURNS) as t:
                pool_gather(pool, t)
            for h in range(2):
                pool.wait_ge(states_stored[h], SCAN_TURNS * 16)
            pool.wait_ge(carry_stored, 16)
            with pool.Fori(0, NET_TURNS) as t:
                pool_tail(pool, t)

        @block.scalar
        def _(act):
            act.wait_ge(fusion_shifted, 1)
            act.activation(share[:, :], share[:, :], ACT.Exp).then_inc(fusion_exp_ready, 1)
            act.wait_ge(count_turned, 1)
            act.activation(countT[:, :], T[:, 0:P], ACT.Copy).then_inc(count_turn_copied, 1)
            with act.Fori(0, HALF) as t:
                scalar_network(act, t)
            scalar_turn_blocks(act)
            with act.Fori(HALF, NET_TURNS) as t:
                scalar_network(act, t)
            with act.Fori(0, SCAN_TURNS) as t:
                scalar_scan(act, t)
            act.wait_ge(chain_exponents_ready, 1)
            act.activation(chain[:, 0, :], chain[:, 0, :], ACT.Exp)
            act.activation(chain[:, 2, :], chain[:, 2, :], ACT.Exp).then_inc(chain_exps_ready, 1)
            with act.Fori(0, NET_TURNS) as t:
                scalar_tail(act, t)

        @block.vector
        def _(dve):
            chain_count = [0]

            def link(ins):
                ins.then_inc(vector_links, 1)
                chain_count[0] += 1
                dve.wait_ge(vector_links, chain_count[0])

            def rank_link(s):
                def make(t):
                    n = [0]

                    def linked(ins):
                        ins.then_inc(rank_steps, 1)
                        n[0] += 1
                        dve.wait_ge(rank_steps, t * RANK_STEPS + n[0])
                    return linked
                return make

            vector_setup(dve, link)
            dve.wait_ge(places_blanked, 128)
            vector_prepare_low(dve, link)
            with dve.Fori(0, TURNS) as t:
                vector_count(dve, t)
            vector_bases(dve, link)
            link(dve.tensor_copy(run[:, 0, :], base_low[:, :]))
            with dve.Fori(0, TURNS) as t:
                vector_rank(dve, t, 0, rank_link(0)(t))
            with dve.Fori(0, HALF) as t:
                vector_network(dve, t)
            vector_prepare_high(dve, link)
            link(dve.tensor_copy(run[:, 0, :], base_high[:, :]))
            with dve.Fori(TURNS, 2 * TURNS) as t:
                vector_rank(dve, t, 1, rank_link(1)(t))
            with dve.Fori(HALF, NET_TURNS) as t:
                vector_network(dve, t)
            for half in range(2):
                dve.wait_ge(scattered[2 + half], SCATTERS * 256)
            vector_owner(dve, link)
            vector_scan_start(dve, link)

            def first_link(ins, n=[0]):
                ins.then_inc(scan_steps, 1)
                n[0] += 1
                dve.wait_ge(scan_steps, n[0])

            vector_sources(dve, 0, 0, first_link)
            with dve.Fori(0, SCAN_TURNS - 1) as t:
                vector_scan_turn(dve, t)
            vector_scan_turn(dve, SCAN_TURNS - 1, more=False)
            vector_chain(dve, link)
            with dve.Fori(0, NET_TURNS) as t:
                vector_tail(dve, t)

        @block.tensor
        def _(pe):
            pe.wait_ge(bf_consts_ready, 1)
            pe.matmul(M[:, 0:P], zeros_b[:, :], zeros_b[:, :], start=True, stop=False, skip_group_check=True)
            with pe.Fori(0, TURNS) as t:
                tensor_count(pe, t)
            pe.matmul(M[:, 0:P], zeros_b[:, :], zeros_b[:, :], start=False, stop=True,
                      skip_group_check=True).then_inc(counts_ready, 1)
            tensor_bases(pe)
            with pe.Fori(0, TURNS) as t:
                tensor_rank(pe, t)
            pe.wait_ge(weights_ready0, 1)
            with pe.Fori(0, HALF) as t:
                tensor_network(pe, t)
            tensor_turn_blocks(pe)
            with pe.Fori(TURNS, 2 * TURNS) as t:
                tensor_rank(pe, t)
            with pe.Fori(HALF, NET_TURNS) as t:
                tensor_network(pe, t)
            pe.wait_ge(begun_ready, 1)
            pe.matmul(M[:, 0:1], begun_sum[:, :], ones[:, 0:1], start=True, stop=True).then_inc(owner_ready, 1)
            tensor_chain(pe)
            with pe.Fori(0, NET_TURNS) as t:
                tensor_tail(pe, t)

def kernel(**inputs):
    import concourse.bacc as bacc
    from concourse.bass_utils import run_bass_kernel_spmd

    a = {k: np.asarray(v) for k, v in inputs.items()}

    def hidden_major(w):
        e, h, d = w.shape
        return w.reshape(e, h // P, P, d).transpose(2, 0, 1, 3).reshape(P, -1)

    def feature_major(w):
        return w.transpose(1, 0, 2).reshape(P, -1)

    def bias_columns(b):
        return b.reshape(-1, P).transpose(1, 0)

    mats = {
        "wt0": a["L0_gnn_W"].T, "wg0": a["L0_ffn_Wg"], "w1_0": feature_major(a["L0_ffn_W1"]),
        "w2_0": hidden_major(a["L0_ffn_W2"]), "w_rel": a["L1_gnn_W_rel"], "w_root": a["L1_gnn_W_root"],
        "w1_1": a["L1_ffn_W1"], "wg1": hidden_major(a["L1_ffn_Wg"][None]), "wd_1": hidden_major(a["L1_ffn_Wd"]),
        "w_self": a["L2_gnn_W_self"], "w_neigh": a["L2_gnn_W_neigh"], "wr": a["L2_ffn_wr"], "w1_2": a["L2_ffn_w1"],
        "w2_2": hidden_major(a["L2_ffn_w2"][None]), "w1_3": feature_major(a["L3_gnn_W1"]),
        "w2_3": hidden_major(a["L3_gnn_W2"]), "w_gat": a["L3_ffn_W_gat"], "w1_4": feature_major(a["L3_ffn_W1"]),
        "w2_4": hidden_major(a["L3_ffn_W2"]), "b1_0": bias_columns(a["L0_ffn_b1"]),
        "b1_1": bias_columns(a["L1_ffn_b1"]), "b1_2": bias_columns(a["L2_ffn_b1"]),
        "b1_3": bias_columns(a["L3_gnn_b1"]), "b1_4": bias_columns(a["L3_ffn_b1"]),
    }
    lower = np.tril(np.ones((P, P), np.float32), -1)
    groups_of = np.zeros((GROUPS, JOINTS), np.float32)
    for k, nodes in enumerate(JOINT_GROUPS):
        groups_of[k, nodes] = 1.0
    one_of = np.tile(groups_of, (1, G))
    member = np.zeros((P, GROUPS, GJ), np.float32)
    member[:GJ] = one_of.T[:, :, None] * one_of[None]
    joint_share = np.zeros((P, GROUPS), np.float32)
    joint_share[:GJ] = one_of.T
    tables = {
        "ident": np.eye(P, dtype=np.float32), "iota": np.tile(np.arange(P, dtype=np.float32), (P, 1)),
        "before": lower.T, "earlier": lower, "falling": np.tile(np.arange(8, 0, -1, dtype=np.float32), (P, 1)),
        "cut_row": np.tile(np.arange(P, dtype=np.float32) * WIDTH, (P, 1)), "member": member.reshape(P, -1),
        "joint_share": joint_share,
    }
    data = {
        "x_in": a["x"], "adj_in": a["adj"], "adjT_in": a["adj"].transpose(0, 2, 1), "edges": a["L3_ffn_edge_index"],
        "rows_in_dram": np.concatenate([a[name].reshape(-1) for name, _ in ROWS]),
        "consts_in": np.concatenate([tables[name] for name, _ in CONSTS], axis=1),
        "bias0": a["L0_ffn_b2"], "bias1": a["L1_ffn_bd"], "bias2": a["L3_ffn_b2"],
    }
    data.update({f"m_{name}": w for name, w in mats.items()})
    data = {name: np.ascontiguousarray(v) for name, v in data.items()}

    nc = bacc.Bacc("TRN2", target_bir_lowering=False, num_devices=1)
    t = {name: nc.dram_tensor(name, v.shape, mybir.dt.from_np(v.dtype), kind="ExternalInput").ap()
         for name, v in data.items()}
    out = nc.dram_tensor("out", (B, N, D), F32, kind="ExternalOutput").ap()
    build(nc, t["x_in"], t["adj_in"], t["adjT_in"], t["edges"], t["rows_in_dram"], t["consts_in"],
          [t["bias0"], t["bias1"], t["bias2"]], {name: t[f"m_{name}"] for name, _ in MATS}, out)
    return run_bass_kernel_spmd(nc, [data], core_ids=[0]).results[0]["out"]
```

```python
from contextlib import ExitStack
from itertools import zip_longest

import concourse.bass as bass
import numpy as np
from concourse import mybir

F32, BF16 = mybir.dt.float32, mybir.dt.bfloat16
I32, U32 = mybir.dt.int32, mybir.dt.uint32
ALU, ACT, AX = mybir.AluOpType, mybir.ActivationFunctionType, mybir.AxisListType

P = 128
B, N, D = 128, 128, 128
NODES = B * N
EDGES = 524288
G = 4
NET_TURNS = B // G
NORMS = 10
HIDS, YS = 24, 16
JOINTS, GJ = 25, G * 25
JOINT_GROUPS = [list(range(25)), [0, 1, 2, 3, 4, 5, 6, 7, 8], [0, 9, 10, 11, 12, 13, 14], [6, 7, 8, 12, 13, 14],
                [3, 4, 5, 9, 10, 11]]
GROUPS = len(JOINT_GROUPS)
KEPT = max(1, N // 2) - 1
HEADS, EXPERTS = 4, 4
HE = HEADS * EXPERTS
ROW = HE + 2 * HEADS
CARRY = HEADS + HE
EPS = 1e-5
BIG, HUGE = 1e30, 3e38

LOOPS = NODES // P
TILES = LOOPS + EDGES // P
PLACES = TILES * P
WIDTH = PLACES // P
CHUNK = TILES // 4
UNROLL = 4
TURNS = TILES // (4 * UNROLL)
SCATTERS = TILES // 32
FAR = 1 << 20
SPAN = 64
SCAN_TURNS = WIDTH // (2 * SPAN)
OWN = 32
FREE = 1

NET_STEPS, RANK_STEPS, SCAN_STEPS, TAIL_STEPS = 95, 2, 30, 39

ROWS = [("L0_gnn_b", D), ("L0_gnn_alpha", 1), ("L0_ffn_bg", 8), ("L0_ffn_bias", 8), ("L1_gnn_ln_gamma", D),
        ("L1_gnn_ln_beta", D), ("L1_gnn_b_rel", D), ("L1_ffn_bg", 8), ("L2_gnn_gamma", D), ("L2_gnn_beta", D),
        ("L2_ffn_br", 1), ("L2_ffn_b2", D), ("L3_gnn_b2", GROUPS * D), ("L3_gnn_fusion_w", GROUPS),
        ("L3_ffn_att_src", HE), ("L3_ffn_att_dst", HE), ("L3_ffn_b_gat", HE), ("L3_ffn_ln_gamma", HE),
        ("L3_ffn_ln_beta", HE)]
ROW_AT = {}
for _name, _n in ROWS:
    ROW_AT[_name] = (sum(n for _, n in ROWS[:len(ROW_AT)]), _n)
ROW_TOTAL = sum(n for _, n in ROWS)

MATS = [("wt0", D), ("wg0", 8), ("w1_0", 8 * 256), ("w2_0", 8 * 256), ("w_rel", D), ("w_root", D), ("w1_1", 512),
        ("wg1", 4 * 8), ("wd_1", 8 * 512), ("w_self", D), ("w_neigh", D), ("wr", 1), ("w1_2", 512), ("w2_2", 512),
        ("w1_3", GROUPS * 256), ("w2_3", GROUPS * 256), ("w_gat", HE), ("w1_4", EXPERTS * 256),
        ("w2_4", EXPERTS * 256), ("b1_0", 16), ("b1_1", 4), ("b1_2", 4), ("b1_3", 2 * GROUPS), ("b1_4", 8)]
CONSTS = [("ident", P), ("iota", P), ("before", P), ("earlier", P), ("falling", 8), ("cut_row", P),
          ("member", GROUPS * GJ), ("joint_share", GROUPS)]
CONST_TOTAL = sum(n for _, n in CONSTS)

def build(nc, x_in, adj_in, adjT_in, edges, rows_in_dram, consts_in, expert_biases, mats, out):
    table = nc.dram_tensor("table", (NODES, ROW), F32).ap()
    x_mid = nc.dram_tensor("x_mid", (NET_TURNS, P, G * D), F32).ap()
    zT_mid = nc.dram_tensor("zT_mid", (NET_TURNS, P, G * D), F32).ap()
    order = nc.dram_tensor("order", (PLACES, 1), I32).ap()
    order_rows = order.rearrange("(p c) o -> p (c o)", p=P)
    state_rows = nc.dram_tensor("state_rows", (P, WIDTH * ROW), F32).ap()
    carry_rows = nc.dram_tensor("carry_rows", (P, 2 * CARRY), F32).ap()

    with ExitStack() as ctx:
        def sb(name, shape, dt=F32, stack=ctx):
            return stack.enter_context(nc.sbuf_tensor(name, shape, dt))

        def bank(name, shape=(P, 512)):
            return ctx.enter_context(nc.psum_tensor(name, list(shape), F32))

        def sem(name):
            return ctx.enter_context(nc.semaphore(name))

        Ts = [bank(f"T{i}") for i in range(2)]
        HP = [bank(f"HP{i}") for i in range(2)]
        Ys = [[bank(f"Y{i}{k}", (P, 4, D)) for k in range(2)] for i in range(2)]
        T4s = [T[:, :].rearrange("p (g d) -> p g d", g=4) for T in Ts]
        T, T4, Y = Ts[0], T4s[0], Ys[0]
        KEYS, NEXT = HP, Ts[1][:, 0:P]
        LOOK = [bank_[:, :, :].rearrange("p k d -> p (k d)") for bank_ in Ys[0]]
        TURNED = [bank_[:, 0:2, :].rearrange("p k d -> p (k d)").bitcast(BF16) for bank_ in Ys[1]]

        consts = sb("consts", [P, CONST_TOTAL])
        at = 0
        const = {}
        for name, n in CONSTS:
            const[name] = consts[:, at:at + n]
            at += n
        ident, iota, before, earlier, falling, cut_row = (
            const[n] for n in ("ident", "iota", "before", "earlier", "falling", "cut_row"))
        member = const["member"][0:GJ, :].rearrange("p (k n) -> p k n", k=GROUPS)
        row_tile = sb("row_tile", [P, ROW_TOTAL])

        def row(name):
            a, n = ROW_AT[name]
            return row_tile[:, a:a + n]

        mat = {name: sb(name, [P, n]) for name, n in MATS}
        (wt0, wg0, w1_0, w2_0, w_rel, w_root, w1_1, wg1, wd_1, w_self, w_neigh, wr, w1_2, w2_2, w1_3, w2_3, w_gat,
         w1_4, w2_4, b1_0, b1_1, b1_2, b1_3, b1_4) = (mat[name] for name, _ in MATS)
        b2_0 = sb("b2_0", [G * 8, G * D])
        b2_1 = sb("b2_1", [G * 8, G * D])
        b2_4 = sb("b2_4", [G * EXPERTS, G * D])
        wr_wide = sb("wr_wide", [P, P])
        ident_b, ident128_b = sb("ident_b", [P, P], BF16), sb("ident128_b", [P, P], BF16)
        zeros_b = sb("zeros_b", [P, P], BF16)
        ones = sb("ones", [P, P])
        zeros = sb("zeros", [P, P])
        eps = sb("eps", [P, 1])
        one = sb("one", [P, 1])
        gate_bias0 = sb("gate_bias0", [P, 8])
        share = sb("share", [P, GROUPS])
        share_sum = sb("share_sum", [P, 1])

        count = sb("count", [P, P])
        totals = sb("totals", [P, P])
        base_high = sb("base_high", [P, P])
        first_place, last_place = sb("first_place", [P, P]), sb("last_place", [P, P])

        def pair(name, shape, stack=ctx):
            return [sb(f"{name}{i}", shape, F32, stack) for i in range(2)]

        XINs, As, ATs, Xs = (pair(n, [P, G, D]) for n in ("XIN", "A", "AT", "X"))
        ABINs, TABs = pair("ABIN", [GJ, GJ]), pair("TAB", [P, G, ROW])
        ZTs = pair("ZT", [P, G * N])
        HT = sb("HT", [P, 4, G * N])
        deviation, rstd, peak, first, gap_exp = (
            sb(n, [P, G]) for n in ("deviation", "rstd", "peak", "first", "gap_exp"))
        top = sb("top", [P, 2, G])
        logits, chosen, second = (sb(n, [P, G, 8]) for n in ("logits", "chosen", "second"))
        CT = sb("CT", [G * 8, P])
        gat_part = sb("gat_part", [P, G, HE])
        bits = sb("bits", [P, CHUNK], I32)
        bitsf = bits[:, :].bitcast(F32)
        XIN, X, ZT = XINs[0], Xs[0], ZTs[0]

        with ExitStack() as sorting:
            POS_t = sb("POS", [P, TILES], F32, sorting)
            VAL_t = sb("VAL", [P, TILES], F32, sorting)
            POS, VAL = POS_t[:, :], VAL_t[:, :]
            loop_ids = sb("loop_ids", [P, LOOPS], I32, sorting)
            place16, equal16, skip16, key16 = (sb(n, [P, 16], F32, sorting)
                                               for n in ("place16", "equal16", "skip16", "key16"))
            stage_place = sb("stage_place", [P, 2, 16], I32, sorting)
            stage_value = sb("stage_value", [P, 2, 16], I32, sorting)
            with ExitStack() as ranking:
                digit = sb("digit", [P, TILES + 4], BF16, ranking)
                high = sb("high", [P, TILES + 4], BF16, ranking)
                OH = sb("OH", [P, 2, P, 4], BF16, ranking)
                OH2 = sb("OH2", [P, 2, P, 4], BF16, ranking)
                iota4 = sb("iota4", [P, P, 4], BF16, ranking)
                OHT = sb("OHT", [P, 4 * P], F32, ranking)
                picked = sb("picked", [P, 8, P], F32, ranking)
                next_place = sb("next_place", [P, 8, P], F32, ranking)
            Zs, Hs, XSs, NBs, SPs = (pair(n, [P, G, D], sorting) for n in ("Z", "H", "XS", "NB", "SP"))
            gates, scales_io, weights = (pair(n, s, sorting) for n, s in (
                ("gate", [P, G, 8]), ("scale_io", [P, 2 * G]), ("weight", [P, G])))
            A5s, NT5s = (pair(n, [GJ, GROUPS, GJ], sorting) for n in ("A5", "NT5"))
            inv5s, ZSs, Fs, FBs = (pair(n, s, sorting) for n, s in (
                ("inv5", [GJ, GROUPS]), ("ZS", [GJ, D]), ("F", [GJ, D]), ("FB", [JOINTS, G, D])))
            R, W = (sb(n, [P, G, D], F32, sorting) for n in ("R", "W"))
            NBT, AGT = (sb(n, [P, G * N], F32, sorting) for n in ("NBT", "AGT"))
            stats, moments = sb("stats", [P, G, 6], F32, sorting), sb("moments", [P, G, 2], F32, sorting)
            degree, no_edge, degree_root = (sb(n, [P, 2 * G], F32, sorting)
                                            for n in ("degree", "no_edge", "degree_root"))
            probs = sb("probs", [P, G, 8], F32, sorting)
            AB = sb("AB", [GJ, GJ], F32, sorting)
            deg5, no5, root5 = (sb(n, [GJ, GROUPS], F32, sorting) for n in ("deg5", "no5", "root5"))
            UT = sb("UT", [P, GROUPS * GJ], F32, sorting)
            H3 = sb("H3", [P, 2, GROUPS, GJ], F32, sorting)
            V5, F5 = sb("V5", [GJ, GROUPS * D], F32, sorting), sb("F5", [GJ, GROUPS, D], F32, sorting)
        begun = sb("begun", [P, OWN, P], BF16)
        begun_sum = sb("begun_sum", [P, P])
        owner = sb("owner", [P, 1], I32)
        owner_row = sb("owner_row", [P, ROW])
        end_place, end_part = sb("end_place", [P, P], I32), sb("end_part", [P, P], I32)
        node_a, node_b, node_c, uncut = (sb(n, [P, P]) for n in ("node_a", "node_b", "node_c", "uncut"))
        indices, source = sb("indices", [P, 2, SPAN], I32), sb("source", [P, 2, SPAN], I32)
        loop_here = sb("loop_here", [P, 2, SPAN])
        going, restart = sb("going", [P, SPAN]), sb("restart", [P, SPAN])
        loop_any, loops_seen = sb("loop_any", [P, 1]), sb("loops_seen", [P, 1])
        rows_in = sb("rows_in", [P, 2, SPAN * ROW])
        states = sb("states", [P, 2, SPAN, ROW])
        adst_run = sb("adst_run", [P, 2, HEADS, SPAN])
        high_run = sb("high_run", [P, 2, HEADS, SPAN + 1])
        adst, score, decay, mass = (sb(n, [P, HEADS, SPAN]) for n in ("adst", "score", "decay", "mass"))
        weighed = sb("weighed", [P, HE, SPAN])
        chain_in, chain = sb("chain_in", [P, 3, CARRY]), sb("chain", [CARRY, 3, P])
        chain_high, chain_sum = sb("chain_high", [CARRY, P + 1]), sb("chain_sum", [CARRY, P + 1])
        carry_out = sb("carry_out", [P, 2 * CARRY])
        tail_index = sb("tail_index", [P, 2, G], I32)
        node_states, node_carry = sb("node_states", [P, G * ROW]), sb("node_carry", [P, G * 2 * CARRY])
        own_high, taken_high, both_high = (sb(n, [P, G, CARRY]) for n in ("own_high", "taken_high", "both_high"))
        denominator = sb("denominator", [P, G, HEADS])
        agg = sb("agg", [P, G, HE])
        tail_gate = sb("tail_gate", [P, G, EXPERTS])

        variance_ready = [sem(f"variance_ready{i}") for i in range(2)]
        deviation_ready = [sem(f"deviation_ready{i}") for i in range(2)]
        outputs_ready = [sem(f"outputs_ready{i}") for i in range(2)]
        outputs_used = [sem(f"outputs_used{i}") for i in range(2)]
        adj_loaded = [sem(f"adj_loaded{i}") for i in range(2)]
        x_loaded = [sem(f"x_loaded{i}") for i in range(2)]
        results_stored = [sem(f"results_stored{i}") for i in range(2)]
        blocks_loaded = [sem(f"blocks_loaded{i}") for i in range(2)]
        fused_back = [sem(f"fused_back{i}") for i in range(2)]
        hidden_ready = [sem(f"hidden_ready{i}") for i in range(2)]
        hidden_done = [sem(f"hidden_done{i}") for i in range(2)]
        joints_stacked = [sem(f"joints_stacked{i}") for i in range(2)]
        scattered = [sem(f"scattered{i}") for i in range(2)]
        indices_loaded = [sem(f"indices_loaded{i}") for i in range(2)]
        gathered = [sem(f"gathered{i}") for i in range(2)]
        states_stored = [sem(f"states_stored{i}") for i in range(2)]
        vector_ticks, vector_steps, adj_rows_used, degrees_ready = (
            sem(n) for n in ("vector_ticks", "vector_steps", "adj_rows_used", "degrees_ready"))
        degree_roots_ready, h0_ready, h_ready, mixed0_ready = (
            sem(n) for n in ("degree_roots_ready", "h0_ready", "h_ready", "mixed0_ready"))
        x_used, gates_ready, gate_gap_ready, gate_exp_ready = (
            sem(n) for n in ("x_used", "gates_ready", "gate_gap_ready", "gate_exp_ready"))
        gate_ready, bias_sum_ready, z_ready, conv1_ready = (
            sem(n) for n in ("gate_ready", "bias_sum_ready", "z_ready", "conv1_ready"))
        shifted_ready, probs_ready, mixed2_ready, softplus_ready = (
            sem(n) for n in ("shifted_ready", "probs_ready", "mixed2_ready", "softplus_ready"))
        weights_ready, deep_ready, joint_degrees_ready, joint_roots_ready = (
            sem(n) for n in ("weights_ready", "deep_ready", "joint_degrees_ready", "joint_roots_ready"))
        joint_adj_ready, joint_turned, joint_norm_ready, joint_out_ready = (
            sem(n) for n in ("joint_adj_ready", "joint_turned", "joint_norm_ready", "joint_out_ready"))
        fused_ready, gat_ready, table_ready, turned = (
            sem(n) for n in ("fused_ready", "gat_ready", "table_ready", "turned"))
        turned_copied, gates_turned, gate_columns_ready, mixed1_ready = (
            sem(n) for n in ("turned_copied", "gates_turned", "gate_columns_ready", "mixed1_ready"))
        mixed1_copied, pre_ready, softplus_steps, joint_mixed_ready = (
            sem(n) for n in ("mixed1_copied", "pre_ready", "softplus_steps", "joint_mixed_ready"))
        joint_mixed_copied, joint_hidden_ready, joint_hidden_done, joint_values_ready = (
            sem(n) for n in ("joint_mixed_copied", "joint_hidden_ready", "joint_hidden_done", "joint_values_ready"))
        joint_values_copied, joints_ready, edges_loaded, loops_made = (
            sem(n) for n in ("joint_values_copied", "joints_ready", "edges_loaded", "loops_made"))
        pairs_counted, pairs_ready, counts_ready, count_copied = (
            sem(n) for n in ("pairs_counted", "pairs_ready", "counts_ready", "count_copied"))
        sums_ready, places_begun, rank_steps, ranks_taken = (
            sem(n) for n in ("sums_ready", "places_begun", "rank_steps", "ranks_taken"))
        tile_counted, keys_ready, lookups_ready, places_ready = (
            sem(n) for n in ("tile_counted", "keys_ready", "lookups_ready", "places_ready"))
        onehots_ready, next_copied, onehots_turned, turned_onehots_copied = (
            sem(n) for n in ("onehots_ready", "next_copied", "onehots_turned", "turned_onehots_copied"))
        staged, begun_ready, owner_ready, owner_written = (
            sem(n) for n in ("staged", "begun_ready", "owner_ready", "owner_written"))
        ends_ready, owner_row_loaded, states_ready, sources_ready = (
            sem(n) for n in ("ends_ready", "owner_row_loaded", "states_ready", "sources_ready"))
        exponents_ready, exps_ready, scan_steps, chain_in_ready = (
            sem(n) for n in ("exponents_ready", "exps_ready", "scan_steps", "chain_in_ready"))
        chain_turned, chain_exponents_ready, chain_exps_ready, chain_ready = (
            sem(n) for n in ("chain_turned", "chain_exponents_ready", "chain_exps_ready", "chain_ready"))
        chain_back, carry_ready, node_rows_used, tail_staged = (
            sem(n) for n in ("chain_back", "carry_ready", "node_rows_used", "tail_staged"))
        node_rows_loaded, tail_steps, node_exponents_ready, node_exps_ready = (
            sem(n) for n in ("node_rows_loaded", "tail_steps", "node_exponents_ready", "node_exps_ready"))
        agg_variance_ready, agg_deviation_ready, tail_gap_ready, tail_gap_exp_ready = (
            sem(n) for n in ("agg_variance_ready", "agg_deviation_ready", "tail_gap_ready", "tail_gap_exp_ready"))
        tail_gate_ready, tail_x_loaded, tail_outputs_ready, tail_outputs_used = (
            sem(n) for n in ("tail_gate_ready", "tail_x_loaded", "tail_outputs_ready", "tail_outputs_used"))
        tail_bias_ready, out_stored, out_ready, tail_hidden_ready = (
            sem(n) for n in ("tail_bias_ready", "out_stored", "out_ready", "tail_hidden_ready"))
        tail_hidden_done, tail_gates_turned, tail_gate_columns_ready, tail_z_loaded = (
            sem(n) for n in ("tail_hidden_done", "tail_gates_turned", "tail_gate_columns_ready", "tail_z_loaded"))
        consts_loaded, weights_loaded, cleared, places_blanked = (
            sem(n) for n in ("consts_loaded", "weights_loaded", "cleared", "places_blanked"))
        bf_consts_ready, fusion_shifted, fusion_exp_ready, weights_ready0 = (
            sem(n) for n in ("bf_consts_ready", "fusion_shifted", "fusion_exp_ready", "weights_ready0"))
        carry_stored, vector_links, sync_ticks, pool_ticks = (
            sem(n) for n in ("carry_stored", "vector_links", "sync_ticks", "pool_ticks"))

        def nth(t, i, k, each):
            return t * (2 * each) + (2 * (k - 1) + i + 1)

        def vector_norms(eng, t, i, src, dst, k, link, last_signal=None):
            for g in range(G):
                ins = eng.bn_stats(stats[:, g, :], src[:, g, :])
            link(ins)
            eng.sem_inc(vector_ticks, 1)
            for g in range(G):
                ins = eng.bn_aggr(moments[:, g, :], stats[:, g, :])
            ins.then_inc(variance_ready[i], 1)
            eng.wait_ge(deviation_ready[i], t * NORMS + k)
            link(eng.reciprocal(rstd[:, :], deviation[:, :]))
            for g in range(G):
                ins = eng.tensor_scalar(dst[:, g, :], src[:, g, :], moments[:, g, 0:1], rstd[:, g:g + 1],
                                        ALU.subtract, ALU.mult)
            if last_signal is None:
                link(ins)
            else:
                ins.then_inc(last_signal, 1)

        def first_largest(eng, link, onehot, values, n):
            link(eng.tensor_reduce(peak[:, :], values, AX.X, ALU.max))
            link(eng.tensor_tensor(onehot, values, peak[:, :].unsqueeze(2).broadcast_to([P, G, n]), ALU.is_equal))
            link(eng.tensor_tensor(onehot, onehot, falling[:, 0:n].unsqueeze(1).broadcast_to([P, G, n]), ALU.mult))
            link(eng.tensor_reduce(first[:, :], onehot, AX.X, ALU.max))
            link(eng.tensor_tensor(onehot, onehot, first[:, :].unsqueeze(2).broadcast_to([P, G, n]), ALU.is_equal))

        def vector_network(eng, t, i, count):
            n = t * 2 + i
            XIN, A, AT, X, Z, H, XS, NB, SP, T4 = (both[i] for both in (XINs, As, ATs, Xs, Zs, Hs, XSs, NBs, SPs, T4s))
            gate, scale_io, weight, inv5, ABIN = (both[i] for both in (gates, scales_io, weights, inv5s, ABINs))
            A5, NT5, F, FB, TAB, T, Y = (both[i] for both in (A5s, NT5s, Fs, FBs, TABs, Ts, Ys))

            def link(ins):
                ins.then_inc(vector_steps, 1)
                count[0] += 1
                eng.wait_ge(vector_steps, t * (2 * NET_STEPS) + count[0])

            def wide(row, width=D):
                return row.unsqueeze(1).broadcast_to([P, G, width])

            def per_token(cols, width=D):
                return cols.unsqueeze(2).broadcast_to([P, G, width])

            def expert_sum(first_y, experts):
                for e in range(experts):
                    eng.wait_ge(outputs_ready[i], t * YS + first_y + e + 1)
                    for g in range(G):
                        ins = eng.scalar_tensor_tensor(X[:, g, :], Y[(first_y + e) % 2][:, g, :], gate[:, g, e:e + 1],
                                                       X[:, g, :], ALU.mult, ALU.add)
                    ins.then_inc(outputs_used[i], 1)
                    eng.wait_ge(outputs_used[i], t * YS + first_y + e + 1)

            eng.wait_ge(adj_loaded[i], t * 32 + 32)
            link(eng.tensor_reduce(degree[:, 0:G], AT[:, :, :], AX.X, ALU.add))
            eng.tensor_reduce(degree[:, G:2 * G], A[:, :, :], AX.X, ALU.add).then_inc(adj_rows_used, 1)
            eng.wait_ge(adj_rows_used, n + 1)
            link(eng.tensor_scalar(no_edge[:, :], degree[:, :], 0.0, None, ALU.is_equal))
            eng.tensor_tensor(degree[:, :], degree[:, :], no_edge[:, :], ALU.add).then_inc(degrees_ready, 1)
            eng.wait_ge(degree_roots_ready, n + 1)
            link(eng.tensor_scalar(no_edge[:, :], no_edge[:, :], -1.0, 1.0, ALU.mult, ALU.add))
            link(eng.reciprocal(scale_io[:, :], degree_root[:, :]))
            link(eng.tensor_tensor(scale_io[:, :], scale_io[:, :], no_edge[:, :], ALU.mult))

            eng.wait_ge(x_loaded[i], t * 16 + 16)
            eng.wait_ge(results_stored[i], t * 48 + FREE)
            vector_norms(eng, t, i, XIN, Z, 1, link, z_ready)
            yield
            eng.wait_ge(h0_ready, n + 1)
            eng.tensor_tensor(H[:, :, :], Y[0][:, :, :], wide(row("L0_gnn_b")), ALU.add).then_inc(h_ready, 1)
            yield
            eng.wait_ge(mixed0_ready, n + 1)
            link(eng.tensor_scalar(R[:, :, :], Y[1][:, :, :], 0.0, row("L0_gnn_alpha"), ALU.min, ALU.mult))
            link(eng.scalar_tensor_tensor(R[:, :, :], Y[1][:, :, :], 0.0, R[:, :, :], ALU.max, ALU.add))
            eng.tensor_tensor(X[:, :, :], XIN[:, :, :], R[:, :, :], ALU.add).then_inc(x_used, 1)
            eng.wait_ge(x_used, n + 1)

            vector_norms(eng, t, i, X, Z, 2, link, z_ready)
            yield
            eng.wait_ge(gates_ready, nth(t, i, 1, 2))
            link(eng.tensor_tensor(logits[:, :, :], T[:, 0:G * 8].rearrange("p (g e) -> p g e", g=G),
                                   wide(gate_bias0[:, :], 8), ALU.add))
            first_largest(eng, link, chosen[:, :, :], logits[:, :, :], 8)
            link(eng.tensor_copy(top[:, 0, :], peak[:, :]))
            link(eng.scalar_tensor_tensor(logits[:, :, :], chosen[:, :, :], -BIG, logits[:, :, :], ALU.mult, ALU.add))
            first_largest(eng, link, second[:, :, :], logits[:, :, :], 8)
            eng.tensor_tensor(top[:, 1, :], peak[:, :], top[:, 0, :], ALU.subtract).then_inc(gate_gap_ready, 1)
            eng.wait_ge(gate_exp_ready, n + 1)
            link(eng.tensor_scalar(top[:, 0, :], gap_exp[:, :], 1.0, None, ALU.add))
            link(eng.reciprocal(top[:, 1, :], top[:, 0, :]))
            link(eng.tensor_tensor(top[:, 0, :], gap_exp[:, :], top[:, 1, :], ALU.mult))
            link(eng.tensor_tensor(chosen[:, :, :], chosen[:, :, :], per_token(top[:, 1, :], 8), ALU.mult))
            link(eng.tensor_tensor(second[:, :, :], second[:, :, :], per_token(top[:, 0, :], 8), ALU.mult))
            eng.tensor_tensor(gate[:, :, :], chosen[:, :, :], second[:, :, :], ALU.add).then_inc(gate_ready, 1)
            eng.wait_ge(gate_ready, nth(t, i, 1, 2))
            expert_sum(0, 8)
            eng.wait_ge(bias_sum_ready, nth(t, i, 1, 2))
            link(eng.tensor_tensor(X[:, :, :], X[:, :, :], T4[:, :, :], ALU.add))

            vector_norms(eng, t, i, X, Z, 3, link)
            vector_norms(eng, t, i, Z, H, 4, link)
            link(eng.tensor_tensor(H[:, :, :], H[:, :, :], wide(row("L1_gnn_ln_gamma")), ALU.mult))
            eng.tensor_tensor(H[:, :, :], H[:, :, :], wide(row("L1_gnn_ln_beta")), ALU.add).then_inc(z_ready, 1)
            yield
            eng.wait_ge(conv1_ready, n + 1)
            link(eng.tensor_tensor(R[:, :, :], Y[1][:, :, :], wide(row("L1_gnn_b_rel")), ALU.add))
            link(eng.scalar_tensor_tensor(R[:, :, :], R[:, :, :], 0.0, Z[:, :, :], ALU.max, ALU.add))
            link(eng.tensor_tensor(X[:, :, :], X[:, :, :], R[:, :, :], ALU.add))

            vector_norms(eng, t, i, X, Z, 5, link, z_ready)
            yield
            eng.wait_ge(gates_ready, nth(t, i, 2, 2))
            link(eng.tensor_tensor(logits[:, :, :], T[:, 0:G * 8].rearrange("p (g e) -> p g e", g=G),
                                   wide(row("L1_ffn_bg"), 8), ALU.add))
            link(eng.tensor_reduce(peak[:, :], logits[:, :, :], AX.X, ALU.max))
            eng.tensor_tensor(logits[:, :, :], logits[:, :, :], per_token(peak[:, :], 8),
                              ALU.subtract).then_inc(shifted_ready, 1)
            eng.wait_ge(probs_ready, n + 1)
            link(eng.tensor_reduce(top[:, 0, :], probs[:, :, :], AX.X, ALU.add))
            link(eng.reciprocal(top[:, 1, :], top[:, 0, :]))
            first_largest(eng, link, chosen[:, :, :], probs[:, :, :], 8)
            link(eng.tensor_tensor(chosen[:, :, :], chosen[:, :, :], probs[:, :, :], ALU.mult))
            eng.tensor_tensor(gate[:, :, :], chosen[:, :, :], per_token(top[:, 1, :], 8), ALU.mult).then_inc(gate_ready, 1)
            eng.wait_ge(gate_ready, nth(t, i, 2, 2))
            expert_sum(8, 8)
            eng.wait_ge(bias_sum_ready, nth(t, i, 2, 2))
            link(eng.tensor_tensor(X[:, :, :], X[:, :, :], T4[:, :, :], ALU.add))

            vector_norms(eng, t, i, X, Z, 6, link)
            vector_norms(eng, t, i, Z, H, 7, link)
            link(eng.tensor_tensor(H[:, :, :], H[:, :, :], wide(row("L2_gnn_gamma")), ALU.mult))
            eng.tensor_tensor(H[:, :, :], H[:, :, :], wide(row("L2_gnn_beta")), ALU.add).then_inc(z_ready, 1)
            eng.wait_ge(z_ready, nth(t, i, 5, 8))
            eng.tensor_tensor(XS[:, :, :], H[:, :, :], per_token(scale_io[:, G:2 * G]), ALU.mult).then_inc(h_ready, 1)
            yield
            eng.wait_ge(mixed2_ready, n + 1)
            link(eng.tensor_tensor(R[:, :, :], Y[0][:, :, :], per_token(scale_io[:, 0:G]), ALU.mult))
            eng.tensor_tensor(NB[:, :, :], H[:, :, :], R[:, :, :], ALU.subtract).then_inc(z_ready, 1)
            eng.wait_ge(z_ready, nth(t, i, 6, 8))
            yield
            eng.wait_ge(softplus_ready, n + 1)
            link(eng.scalar_tensor_tensor(R[:, :, :], Y[1][:, :, :], 0.0, SP[:, :, :], ALU.max, ALU.add))
            link(eng.tensor_tensor(X[:, :, :], X[:, :, :], R[:, :, :], ALU.add))

            vector_norms(eng, t, i, X, Z, 8, link, z_ready)
            yield
            eng.wait_ge(weights_ready, n + 1)
            link(eng.tensor_scalar(W[:, :, :], T[:, 0:G * N].rearrange("p (g n) -> p g n", g=G),
                                   row("L2_ffn_br"), None, ALU.add))
            link(eng.tensor_tensor(R[:, :, :], W[:, :, :], wide(ident[:, :], N), ALU.mult))
            link(eng.tensor_reduce(weight[:, :], R[:, :, :], AX.X, ALU.add))
            link(eng.tensor_tensor(R[:, :, :], W[:, :, :], per_token(weight[:, :], N), ALU.is_equal))
            link(eng.tensor_tensor(R[:, :, :], R[:, :, :], wide(earlier[:, :], N), ALU.mult))
            link(eng.tensor_tensor(W[:, :, :], W[:, :, :], per_token(weight[:, :], N), ALU.is_gt))
            link(eng.tensor_tensor(W[:, :, :], W[:, :, :], R[:, :, :], ALU.add))
            link(eng.tensor_reduce(peak[:, :], W[:, :, :], AX.X, ALU.add))
            link(eng.scalar_tensor_tensor(weight[:, :], peak[:, :], float(KEPT), weight[:, :], ALU.is_lt, ALU.mult))
            link(eng.tensor_tensor(X[:, :, :], X[:, :, :], Z[:, :, :], ALU.add))
            eng.wait_ge(deep_ready, n + 1)
            link(eng.tensor_tensor(R[:, :, :], Y[0][:, :, :], wide(row("L2_ffn_b2")), ALU.add))
            for g in range(G):
                ins = eng.scalar_tensor_tensor(X[:, g, :], R[:, g, :], weight[:, g:g + 1], X[:, g, :], ALU.mult, ALU.add)
            link(ins)

            vector_norms(eng, t, i, X, Z, 9, link, joints_ready)
            eng.wait_ge(blocks_loaded[i], t * 16 * G + 16 * G)
            link(eng.tensor_tensor(AB[:, :], ABIN[:, :], ident[0:GJ, 0:GJ], ALU.add))
            link(eng.tensor_tensor(A5[:, :, :], AB[:, :].unsqueeze(1).broadcast_to([GJ, GROUPS, GJ]), member[:, :, :],
                                   ALU.mult))
            link(eng.tensor_reduce(deg5[:, :], A5[:, :, :], AX.X, ALU.add))
            link(eng.tensor_scalar(no5[:, :], deg5[:, :], 0.0, None, ALU.is_equal))
            eng.tensor_tensor(deg5[:, :], deg5[:, :], no5[:, :], ALU.add).then_inc(joint_degrees_ready, 1)
            eng.wait_ge(joint_roots_ready, n + 1)
            link(eng.tensor_scalar(no5[:, :], no5[:, :], -1.0, 1.0, ALU.mult, ALU.add))
            link(eng.reciprocal(inv5[:, :], root5[:, :]))
            link(eng.tensor_tensor(inv5[:, :], inv5[:, :], no5[:, :], ALU.mult))
            inv_wide = inv5[:, :].unsqueeze(2).broadcast_to([GJ, GROUPS, GJ])
            eng.tensor_tensor(A5[:, :, :], A5[:, :, :], inv_wide, ALU.mult).then_inc(joint_adj_ready, 1)
            yield
            eng.wait_ge(joint_turned, n + 1)
            eng.tensor_tensor(NT5[:, :, :], T[0:GJ, 0:GROUPS * GJ].rearrange("p (k n) -> p k n", k=GROUPS), inv_wide,
                              ALU.mult).then_inc(joint_norm_ready, 1)
            yield
            eng.wait_ge(joint_out_ready, n + 1)
            bias5 = row("L3_gnn_b2")[0:GJ, :].rearrange("p (k d) -> p k d", k=GROUPS)
            eng.tensor_tensor(F5[:, 0:4, :], Y[0][0:GJ, :, :], bias5[:, 0:4, :], ALU.add)
            link(eng.tensor_tensor(F5[:, 4, :], Y[1][0:GJ, 0, :], bias5[:, 4, :], ALU.add))
            for k in range(GROUPS):
                ins = eng.tensor_scalar(F5[:, k, :], F5[:, k, :], 0.0, share[0:GJ, k:k + 1], ALU.max, ALU.mult)
            link(ins)
            eng.tensor_reduce(F[:, :], F5[:, :, :].rearrange("p k d -> p d k"), AX.X, ALU.add).then_inc(fused_ready, 1)
            eng.wait_ge(fused_ready, n + 1)
            yield
            eng.wait_ge(fused_back[i], t * 16 * G + 16 * G)
            link(eng.tensor_tensor(X[0:JOINTS, :, :], X[0:JOINTS, :, :], FB[:, :, :], ALU.add))

            vector_norms(eng, t, i, X, Z, 10, link, z_ready)
            yield
            eng.wait_ge(gat_ready, n + 1)
            gat = T[:, 0:G * HE].rearrange("p (g c) -> p g c", g=G)
            link(eng.tensor_copy(TAB[:, :, 0:HE], gat))
            for k, name in enumerate(("L3_ffn_att_src", "L3_ffn_att_dst")):
                link(eng.tensor_tensor(gat_part[:, :, :], TAB[:, :, 0:HE], wide(row(name), HE), ALU.mult))
                ins = eng.tensor_reduce(TAB[:, :, HE + HEADS * k:HE + HEADS * (k + 1)],
                                        gat_part[:, :, :].rearrange("p g (h e) -> p g h e", h=HEADS), AX.X, ALU.add)
                if k == 0:
                    link(ins)
                else:
                    ins.then_inc(table_ready, 1)

        def scalar_network(eng, t, i):
            turn = t * 2 + i
            SP, ZT, T, Y = SPs[i], ZTs[i], Ts[i], Ys[i]

            def root(k):
                eng.wait_ge(variance_ready[i], t * NORMS + k)
                eng.activation(deviation[:, :], moments[:, :, 1], ACT.Sqrt, bias=eps[:, 0:1]).then_inc(deviation_ready[i], 1)

            def evacuate(k, dst):
                eng.wait_ge(turned, nth(t, i, k, 8))
                eng.activation(dst[:, :], T[:, :], ACT.Copy).then_inc(turned_copied, 1)

            def hidden(n, func, bias):
                eng.wait_ge(hidden_ready[i], t * HIDS + n + 1)
                eng.activation(HT[:, n % 4, :], HP[n % 2][:, :], func, bias=bias).then_inc(hidden_done[i], 1)

            def gate_columns(k):
                eng.wait_ge(gates_turned, nth(t, i, k, 2))
                eng.activation(CT[:, :], T[0:G * 8, 0:P], ACT.Copy).then_inc(gate_columns_ready, 1)

            eng.wait_ge(degrees_ready, turn + 1)
            eng.activation(degree_root[:, :], degree[:, :], ACT.Sqrt).then_inc(degree_roots_ready, 1)
            root(1)
            yield
            evacuate(1, ZT)
            yield
            root(2)
            yield
            evacuate(2, ZT)
            for n in range(4):
                hidden(n, ACT.Relu, b1_0[:, n:n + 1])
            eng.wait_ge(gate_gap_ready, turn + 1)
            eng.activation(gap_exp[:, :], top[:, 1, :], ACT.Exp).then_inc(gate_exp_ready, 1)
            for n in range(4, 16):
                eng.wait_ge(outputs_ready[i], t * YS + n // 2 - 1)
                hidden(n, ACT.Relu, b1_0[:, n:n + 1])
            gate_columns(1)
            root(3)
            root(4)
            yield
            evacuate(3, ZT)
            eng.wait_ge(mixed1_ready, turn + 1)
            eng.activation(AGT[:, :], Y[0][:, :, :].rearrange("p g n -> p (g n)"), ACT.Copy).then_inc(mixed1_copied, 1)
            root(5)
            yield
            evacuate(4, ZT)
            for n in range(4):
                hidden(16 + n, ACT.Gelu, b1_1[:, n:n + 1])
            eng.wait_ge(shifted_ready, turn + 1)
            eng.activation(probs[:, :, :], logits[:, :, :], ACT.Exp).then_inc(probs_ready, 1)
            gate_columns(2)
            root(6)
            root(7)
            yield
            evacuate(5, ZT)
            yield
            evacuate(6, NBT)
            eng.wait_ge(pre_ready, turn + 1)
            pre = Y[1][:, :, :].rearrange("p g n -> p (g n)")
            soft = SP[:, :, :].rearrange("p g n -> p (g n)")
            eng.activation(soft, pre, ACT.Abs).then_inc(softplus_steps, 1)
            eng.wait_ge(softplus_steps, turn * 2 + 1)
            eng.activation(soft, soft, ACT.Exp, scale=-1.0).then_inc(softplus_steps, 1)
            eng.wait_ge(softplus_steps, turn * 2 + 2)
            eng.activation(soft, soft, ACT.Ln, bias=one[:, 0:1]).then_inc(softplus_ready, 1)
            root(8)
            yield
            evacuate(7, ZT)
            for n in range(4):
                hidden(20 + n, ACT.Gelu_apprx_tanh, b1_2[:, n:n + 1])
            root(9)
            eng.wait_ge(joint_degrees_ready, turn + 1)
            eng.activation(root5[:, :], deg5[:, :], ACT.Sqrt).then_inc(joint_roots_ready, 1)
            yield
            yield
            eng.wait_ge(joint_mixed_ready, turn + 1)
            eng.activation(UT[:, :], T[:, 0:GROUPS * GJ], ACT.Copy).then_inc(joint_mixed_copied, 1)
            eng.wait_ge(joint_hidden_ready, turn + 1)
            for c in range(2):
                for k in range(GROUPS):
                    ins = eng.activation(H3[:, c, k, :], HP[c][:, k * GJ:(k + 1) * GJ], ACT.Relu,
                                         bias=b1_3[:, 2 * k + c:2 * k + c + 1])
            ins.then_inc(joint_hidden_done, 1)
            eng.wait_ge(joint_values_ready, turn + 1)
            eng.activation(V5[:, 0:4 * D], Y[0][0:GJ, :, :].rearrange("p g n -> p (g n)"), ACT.Copy)
            eng.activation(V5[:, 4 * D:5 * D], Y[1][0:GJ, 0, :], ACT.Copy).then_inc(joint_values_copied, 1)
            yield
            root(10)
            yield
            evacuate(8, ZT)

        def tensor_network(eng, t, i):
            n = t * 2 + i
            AT, Z, H, XS, NB, ZT, T, Y = (both[i] for both in (ATs, Zs, Hs, XSs, NBs, ZTs, Ts, Ys))
            gate, A5, NT5, ZS = gates[i], A5s[i], NT5s[i], ZSs[i]

            def turn(k, src):
                eng.wait_ge(z_ready, nth(t, i, k, 8))
                for g in range(G):
                    ins = eng.transpose(T[:, g * N:(g + 1) * N], src[:, g, :], ident[:, :])
                ins.then_inc(turned, 1)

            def cols(buf, g):
                return buf[:, g * N:(g + 1) * N]

            def hidden(c, w, src):
                if c >= 2:
                    eng.wait_ge(hidden_done[i], t * HIDS + c - 1)
                eng.matmul(HP[c % 2][:, :], w, src[:, :], start=True, stop=True).then_inc(hidden_ready[i], 1)

            def second(y, slots, ws):
                for g in range(G):
                    for i, (s, w) in enumerate(zip(slots, ws)):
                        ins = eng.matmul(Y[y % 2][:, g, :], HT[:, s, g * N:(g + 1) * N], w,
                                         start=(i == 0), stop=(i == len(slots) - 1))
                return ins

            def bias_sum(k, b2):
                eng.wait_ge(gate_ready, nth(t, i, k, 2))
                eng.transpose(T[0:G * 8, 0:P], gate[:, :, :].rearrange("p g e -> p (g e)"),
                              ident[:, :]).then_inc(gates_turned, 1)
                eng.wait_ge(gate_columns_ready, nth(t, i, k, 2))
                eng.matmul(T[:, :], CT[:, :], b2[:, :], start=True,
                           stop=True).then_inc(bias_sum_ready, 1)

            turn(1, Z)
            eng.wait_ge(turned_copied, nth(t, i, 1, 8))
            for g in range(G):
                ins = eng.matmul(Y[0][:, g, :], cols(ZT, g), wt0[:, :], start=True, stop=True)
            ins.then_inc(h0_ready, 1)
            yield
            eng.wait_ge(h_ready, nth(t, i, 1, 2))
            for g in range(G):
                ins = eng.matmul(Y[1][:, g, :], AT[:, g, :], H[:, g, :], start=True, stop=True)
            ins.then_inc(mixed0_ready, 1)
            yield
            turn(2, Z)
            eng.wait_ge(turned_copied, nth(t, i, 2, 8))
            for g in range(G):
                ins = eng.matmul(T[:, g * 8:(g + 1) * 8], cols(ZT, g), wg0[:, :], start=True, stop=True)
            ins.then_inc(gates_ready, 1)
            for c in range(2):
                hidden(c, w1_0[:, c * D:(c + 1) * D], ZT)
            for e in range(8):
                if e + 1 < 8:
                    for c in (2 * e + 2, 2 * e + 3):
                        hidden(c, w1_0[:, c * D:(c + 1) * D], ZT)
                eng.wait_ge(hidden_done[i], t * HIDS + 2 * e + 2)
                if e >= 2:
                    eng.wait_ge(outputs_used[i], t * YS + e - 1)
                slots = [(2 * e) % 4, (2 * e + 1) % 4]
                second(e, slots, [w2_0[:, (2 * e + c) * D:(2 * e + c + 1) * D] for c in range(2)]).then_inc(outputs_ready[i], 1)
            bias_sum(1, b2_0)
            yield
            turn(3, H)
            for g in range(G):
                ins = eng.matmul(Y[0][:, g, :], H[:, g, :], AT[:, g, :], start=True, stop=True)
            ins.then_inc(mixed1_ready, 1)
            eng.wait_ge(turned_copied, nth(t, i, 3, 8))
            eng.wait_ge(mixed1_copied, n + 1)
            for g in range(G):
                eng.matmul(Y[1][:, g, :], cols(AGT, g), w_rel[:, :], start=True, stop=False)
                ins = eng.matmul(Y[1][:, g, :], cols(ZT, g), w_root[:, :], start=False, stop=True)
            ins.then_inc(conv1_ready, 1)
            yield
            turn(4, Z)
            eng.wait_ge(turned_copied, nth(t, i, 4, 8))
            for c in range(4):
                hidden(16 + c, w1_1[:, c * D:(c + 1) * D], ZT)
            eng.wait_ge(hidden_done[i], t * HIDS + 20)
            for g in range(G):
                for c in range(4):
                    ins = eng.matmul(T[:, g * 8:(g + 1) * 8], HT[:, c, g * N:(g + 1) * N], wg1[:, c * 8:(c + 1) * 8],
                                     start=(c == 0), stop=(c == 3))
            ins.then_inc(gates_ready, 1)
            for e in range(8):
                if e >= 2:
                    eng.wait_ge(outputs_used[i], t * YS + 8 + e - 1)
                if e == 2:
                    bias_sum(2, b2_1)
                second(8 + e, range(4), [wd_1[:, (4 * e + c) * D:(4 * e + c + 1) * D] for c in range(4)])\
                    .then_inc(outputs_ready[i], 1)
            yield
            turn(5, H)
            eng.wait_ge(h_ready, nth(t, i, 2, 2))
            for g in range(G):
                ins = eng.matmul(Y[0][:, g, :], AT[:, g, :], XS[:, g, :], start=True, stop=True)
            ins.then_inc(mixed2_ready, 1)
            eng.wait_ge(turned_copied, nth(t, i, 5, 8))
            yield
            turn(6, NB)
            eng.wait_ge(turned_copied, nth(t, i, 6, 8))
            for g in range(G):
                eng.matmul(Y[1][:, g, :], cols(ZT, g), w_self[:, :], start=True, stop=False)
                ins = eng.matmul(Y[1][:, g, :], cols(NBT, g), w_neigh[:, :], start=False, stop=True)
            ins.then_inc(pre_ready, 1)
            yield
            turn(7, Z)
            eng.wait_ge(turned_copied, nth(t, i, 7, 8))
            eng.matmul(T[:, :], wr_wide[:, :], ZT[:, :], start=True, stop=True).then_inc(weights_ready, 1)
            for c in range(4):
                hidden(20 + c, w1_2[:, c * D:(c + 1) * D], ZT)
            eng.wait_ge(hidden_done[i], t * HIDS + 24)
            second(0, range(4), [w2_2[:, c * D:(c + 1) * D] for c in range(4)]).then_inc(deep_ready, 1)
            yield
            eng.wait_ge(joint_adj_ready, n + 1)
            for k in range(GROUPS):
                ins = eng.transpose(T[0:GJ, k * GJ:(k + 1) * GJ], A5[:, k, :], ident[0:GJ, 0:GJ])
            ins.then_inc(joint_turned, 1)
            yield
            eng.wait_ge(joint_norm_ready, n + 1)
            eng.wait_ge(joints_stacked[i], t * 16 * G + 16 * G)
            eng.matmul(T[:, 0:GROUPS * GJ], ZS[:, :], NT5[:, :, :].rearrange("p k n -> p (k n)"), start=True,
                       stop=True).then_inc(joint_mixed_ready, 1)
            eng.wait_ge(joint_mixed_copied, n + 1)
            for c in range(2):
                for k in range(GROUPS):
                    ins = eng.matmul(HP[c][:, k * GJ:(k + 1) * GJ], w1_3[:, (2 * k + c) * D:(2 * k + c + 1) * D],
                                     UT[:, k * GJ:(k + 1) * GJ], start=True, stop=True)
            ins.then_inc(joint_hidden_ready, 1)
            eng.wait_ge(joint_hidden_done, n + 1)

            def joint_bank(k):
                return Y[0][0:GJ, k, :] if k < 4 else Y[1][0:GJ, 0, :]

            for k in range(GROUPS):
                for c in range(2):
                    ins = eng.matmul(joint_bank(k), H3[:, c, k, :], w2_3[:, (2 * k + c) * D:(2 * k + c + 1) * D],
                                     start=(c == 0), stop=(c == 1))
            ins.then_inc(joint_values_ready, 1)
            eng.wait_ge(joint_values_copied, n + 1)
            for k in range(GROUPS):
                ins = eng.matmul(joint_bank(k), NT5[:, k, :], V5[:, k * D:(k + 1) * D], start=True, stop=True)
            ins.then_inc(joint_out_ready, 1)
            yield
            yield
            turn(8, Z)
            eng.wait_ge(turned_copied, nth(t, i, 8, 8))
            for g in range(G):
                ins = eng.matmul(T[:, g * HE:(g + 1) * HE], cols(ZT, g), w_gat[:, :], start=True, stop=True)
            ins.then_inc(gat_ready, 1)

        def hold(eng, sem, value, ticks):
            eng.wait_ge(sem, value)
            eng.sem_inc(ticks, 1)

        def load_x(eng, t, i):
            eng.dma_start(XINs[i][:, :, :], x_in[bass.ds((t * 2 + i) * G, G)].rearrange("g n d -> n g d"))\
                .then_inc(x_loaded[i], 16)

        def load_adj(eng, t, i):
            eng.dma_start(As[i][:, :, :], adj_in[bass.ds((t * 2 + i) * G, G)].rearrange("g n m -> n g m"))\
                .then_inc(adj_loaded[i], 16)

        def load_adjT(eng, t, i):
            eng.dma_start(ATs[i][:, :, :], adjT_in[bass.ds((t * 2 + i) * G, G)].rearrange("g n m -> n g m"))\
                .then_inc(adj_loaded[i], 16)

        def load_blocks(eng, t, i):
            for g in range(G):
                eng.dma_start(ABINs[i][g * JOINTS:(g + 1) * JOINTS, g * JOINTS:(g + 1) * JOINTS],
                              adj_in[bass.ds((t * 2 + i) * G + g, 1), 0:JOINTS, 0:JOINTS].rearrange("g n m -> n (g m)"))\
                    .then_inc(blocks_loaded[i], 16)

        def sync_network(eng, t, i, more):
            n = t * 2 + i
            if more:
                hold(eng, adj_rows_used, n + 1, sync_ticks)
                load_adj(eng, t + 1, i)
                yield
                hold(eng, x_used, n + 1, sync_ticks)
                load_x(eng, t + 1, i)
                yield
                hold(eng, mixed2_ready, n + 1, sync_ticks)
                load_adjT(eng, t + 1, i)
                yield
            hold(eng, joints_ready, n + 1, sync_ticks)
            for g in range(G):
                eng.dma_start(ZSs[i][g * JOINTS:(g + 1) * JOINTS, :], Zs[i][0:JOINTS, g, :]).then_inc(joints_stacked[i], 16)
            if more:
                hold(eng, joint_degrees_ready, n + 1, sync_ticks)
                load_blocks(eng, t + 1, i)
            yield
            hold(eng, fused_ready, n + 1, sync_ticks)
            for g in range(G):
                eng.dma_start(FBs[i][:, g, :], Fs[i][g * JOINTS:(g + 1) * JOINTS, :]).then_inc(fused_back[i], 16)
            yield
            hold(eng, table_ready, n + 1, sync_ticks)
            eng.dma_start(table[bass.ds(n * (G * N), G * N), :].rearrange("(g n) c -> n g c", g=G),
                          TABs[i][:, :, :]).then_inc(results_stored[i], 16)
            eng.dma_start(x_mid[bass.ds(n, 1)].rearrange("t p c -> p (t c)"),
                          Xs[i][:, :, :].rearrange("p g d -> p (g d)")).then_inc(results_stored[i], 16)
            eng.dma_start(zT_mid[bass.ds(n, 1)].rearrange("t p c -> p (t c)"), ZTs[i][:, :])\
                .then_inc(results_stored[i], 16)

        def vector_prepare(eng, link):
            eng.wait_ge(edges_loaded, 32)
            eng.wait_ge(loops_made, 1)
            link(eng.tensor_copy(POS.bitcast(I32)[:, 0:LOOPS], loop_ids[:, :]))
            link(eng.tensor_copy(VAL.bitcast(I32)[:, 0:LOOPS], loop_ids[:, :]))
            for c in range(0, TILES, CHUNK):
                cs = slice(c, c + CHUNK)
                link(eng.tensor_scalar(bits[:, :], POS.bitcast(I32)[:, cs], 7, None, ALU.logical_shift_right))
                link(eng.tensor_copy(high[:, cs], bits[:, :]))
                link(eng.tensor_scalar(bits[:, :], POS.bitcast(I32)[:, cs], 127, None, ALU.bitwise_and))
                link(eng.tensor_copy(digit[:, cs], bits[:, :]))
                link(eng.tensor_scalar(bitsf, high[:, cs], 127.5, 128.0, ALU.is_gt, ALU.mult))
                link(eng.tensor_tensor(digit[:, cs], digit[:, cs], bitsf, ALU.add))
            link(eng.tensor_scalar(VAL.bitcast(I32)[:, :], VAL.bitcast(I32)[:, :], NODES - 1, None, ALU.min))
            link(eng.tensor_scalar(VAL.bitcast(I32)[:, :], VAL.bitcast(I32)[:, :], NODES - 1, None, ALU.bitwise_and))
            link(eng.tensor_scalar(VAL.bitcast(I32)[:, 0:LOOPS], VAL.bitcast(I32)[:, 0:LOOPS], NODES, None, ALU.add))

        def onehot_of(eng, out, digits, column):
            return eng.tensor_tensor(out, iota4[:, :, :], digits[:, bass.ds(column, 4)].unsqueeze(1).broadcast_to([P, P, 4]),
                                     ALU.is_equal)

        def vector_count(eng, t):
            for u in range(UNROLL):
                b = u % 2
                eng.wait_ge(pairs_counted, t * UNROLL + max(u - 1, 0) + FREE)
                onehot_of(eng, OH[:, b, :, :], digit, t * (4 * UNROLL) + 4 * u)
                onehot_of(eng, OH2[:, b, :, :], high, t * (4 * UNROLL) + 4 * u).then_inc(pairs_ready, 1)

        def tensor_count(eng, t):
            for u in range(UNROLL):
                b = u % 2
                eng.wait_ge(pairs_ready, t * UNROLL + u + 1)
                for k in range(4):
                    ins = eng.matmul(T[:, 0:P], OH[:, b, :, k], OH2[:, b, :, k], start=False, stop=False,
                                     skip_group_check=True)
                ins.then_inc(pairs_counted, 1)

        def vector_bases(eng, link):
            eng.wait_ge(counts_ready, 1)
            eng.tensor_copy(count[:, :], T[:, 0:P]).then_inc(count_copied, 1)
            eng.wait_ge(sums_ready, 1)
            link(eng.tensor_copy(totals[:, :], Y[1][:, 0, :]))
            link(eng.tensor_tensor_scan(base_high[:, :], totals[:, :], zeros[:, :], 0.0, ALU.add, ALU.add))
            link(eng.tensor_tensor(base_high[:, :], base_high[:, :], totals[:, :], ALU.subtract))
            link(eng.tensor_tensor(first_place[:, :], Y[0][:, 1, :], base_high[:, :], ALU.add))
            link(eng.tensor_tensor(last_place[:, :], first_place[:, :], count[:, :], ALU.add))
            link(eng.tensor_scalar(last_place[:, :], last_place[:, :], -1.0, None, ALU.add))
            eng.tensor_copy(next_place[:, 0, :], first_place[:, :]).then_inc(places_begun, 1)
            eng.wait_ge(places_begun, 1)

        def tensor_bases(eng):
            eng.wait_ge(count_copied, 1)
            eng.matmul(Y[1][:, 0, :], ones[:, :], count[:, :], start=True, stop=True)
            eng.matmul(Y[0][:, 1, :], before[:, :], count[:, :], start=True, stop=True).then_inc(sums_ready, 1)
            eng.wait_ge(places_begun, 1)
            eng.matmul(NEXT, ident[:, :], first_place[:, :], start=True, stop=False, skip_group_check=True)

        def vector_rank(eng, t):
            q = t * UNROLL
            here = bass.ds(t * (4 * UNROLL), 4 * UNROLL)
            steps = [0]

            def link(ins):
                ins.then_inc(rank_steps, 1)
                steps[0] += 1
                eng.wait_ge(rank_steps, t * RANK_STEPS + steps[0])

            link(eng.scalar_tensor_tensor(key16[:, :], high[:, here], float(P), digit[:, here], ALU.mult, ALU.add))
            eng.tensor_scalar(skip16[:, :], digit[:, here], 127.5, float(FAR), ALU.is_gt, ALU.mult)
            for u in range(UNROLL):
                b = u % 2
                eng.wait_ge(ranks_taken, q + (u + FREE))
                eng.wait_ge(tile_counted, 4 * (q + u) + FREE)
                group_onehots(eng, t, u + 1)
                eng.wait_ge(keys_ready, q + u + 1)
                for k in range(4):
                    eng.scalar_tensor_tensor(picked[:, k, :], KEYS[b][:, k * P:(k + 1) * P],
                                             key16[:, 4 * u + k:4 * u + k + 1], earlier[:, :], ALU.is_equal,
                                             ALU.mult, accum_out=equal16[:, 4 * u + k:4 * u + k + 1])
                eng.wait_ge(lookups_ready, q + u + 1)
                for k in range(4):
                    ins = eng.tensor_tensor_reduce(picked[:, 4 + k, :], LOOK[b][:, k * P:(k + 1) * P], OH2[:, b, :, k],
                                                   1.0, 0.0, ALU.mult, ALU.add, place16[:, 4 * u + k:4 * u + k + 1])
                ins.then_inc(ranks_taken, 1)
            eng.wait_ge(ranks_taken, q + (UNROLL + FREE))
            link(eng.tensor_tensor(place16[:, :], place16[:, :], equal16[:, :], ALU.add))
            eng.tensor_tensor(POS.bitcast(I32)[:, here], place16[:, :], skip16[:, :], ALU.add).then_inc(places_ready, 1)
            assert steps[0] == RANK_STEPS, steps[0]

        def group_onehots(eng, t, u):
            onehot_of(eng, OH[:, u % 2, :, :], digit, t * (4 * UNROLL) + 4 * u)
            onehot_of(eng, OH2[:, u % 2, :, :], high, t * (4 * UNROLL) + 4 * u).then_inc(onehots_ready, 1)

        def tensor_rank(eng, t):
            q = t * UNROLL
            for u in range(UNROLL):
                b = u % 2

                def count_in(k):
                    eng.wait_ge(next_copied, 4 * (q + u) + (k + FREE))
                    eng.matmul(NEXT, OH[:, b, :, k], OH2[:, b, :, k], start=False, stop=False,
                               skip_group_check=True).then_inc(tile_counted, 1)

                def look_up(k):
                    return eng.matmul(LOOK[b][:, k * P:(k + 1) * P], OHT[:, k * P:(k + 1) * P],
                                      next_place[:, 4 * b + k, :], start=True, stop=True)

                eng.wait_ge(onehots_ready, q + u + 1)
                for k in range(4):
                    ins = eng.transpose(TURNED[b][:, k * P:(k + 1) * P], OH[:, b, :, k], ident_b[:, :])
                ins.then_inc(onehots_turned, 1)
                count_in(0)
                for k in range(4):
                    column = bass.ds(t * (4 * UNROLL) + (4 * u + k), 1)
                    eng.matmul(KEYS[b][:, k * P:(k + 1) * P], digit[:, column].broadcast_to([P, P]), ident_b[:, :],
                               start=True, stop=False)
                    ins = eng.matmul(KEYS[b][:, k * P:(k + 1) * P], high[:, column].broadcast_to([P, P]),
                                     ident128_b[:, :], start=False, stop=True)
                ins.then_inc(keys_ready, 1)
                eng.wait_ge(turned_onehots_copied, q + u + 1)
                for k in range(1, 4):
                    count_in(k)
                    look_up(k - 1)
                look_up(3).then_inc(lookups_ready, 1)

        def scalar_rank(eng, t):
            q = t * UNROLL
            for u in range(UNROLL):
                eng.wait_ge(onehots_turned, q + u + 1)
                eng.activation(OHT[:, :], TURNED[u % 2], ACT.Copy).then_inc(turned_onehots_copied, 1)
                for k in range(4):
                    eng.wait_ge(tile_counted, 4 * (q + u) + (k + 1 + FREE))
                    eng.activation(next_place[:, (4 * (u % 2) + k + 1) % 8, :], NEXT, ACT.Copy).then_inc(next_copied, 1)

        def pool_scatter(eng, t):
            for half in range(2):
                here = bass.ds(t * 32 + 16 * half, 16)
                hold(eng, places_ready, t * 2 + half + 1, pool_ticks)
                if not (isinstance(t, int) and t == 0):
                    hold(eng, scattered[half], t * 256, pool_ticks)
                eng.tensor_copy(stage_place[:, half, :], POS.bitcast(I32)[:, here])
                eng.tensor_copy(stage_value[:, half, :], VAL.bitcast(I32)[:, here]).then_inc(staged, 1)
                hold(eng, staged, t * 2 + half + 1, pool_ticks)
                for j in range(16):
                    eng.indirect_dma_start(order, bass.IndirectOffsetOnAxis(stage_place[:, half, j:j + 1].bitcast(U32), 0),
                                           stage_value[:, half, j:j + 1], None,
                                           bounds_check=PLACES - 1, oob_is_err=False).then_inc(scattered[half], 16)

        def vector_owner(eng, link):
            for c in range(0, P, OWN):
                cuts = cut_row[:, c:c + OWN].unsqueeze(2).broadcast_to([P, OWN, P])
                link(eng.tensor_tensor(begun[:, :, :], first_place[:, :].unsqueeze(1).broadcast_to([P, OWN, P]), cuts,
                                       ALU.is_le))
                ins = eng.tensor_reduce(begun_sum[:, c:c + OWN], begun[:, :, :], AX.X, ALU.add)
                if c + OWN < P:
                    link(ins)
            ins.then_inc(begun_ready, 1)
            eng.wait_ge(owner_ready, 1)
            eng.tensor_scalar(owner[:, :], T[:, 0:1], -1.0, None, ALU.add).then_inc(owner_written, 1)
            link(eng.tensor_copy(end_place[:, :], last_place[:, :]))
            link(eng.tensor_scalar(node_a[:, :], last_place[:, :], 1.0 / WIDTH, None, ALU.mult))
            link(eng.tensor_copy(end_part[:, :], node_a[:, :]))
            link(eng.tensor_copy(node_a[:, :], end_part[:, :]))
            link(eng.scalar_tensor_tensor(node_b[:, :], node_a[:, :], -float(WIDTH), last_place[:, :], ALU.mult, ALU.add))
            link(eng.tensor_scalar(node_c[:, :], node_b[:, :], 0.0, None, ALU.is_lt))
            link(eng.tensor_tensor(node_a[:, :], node_a[:, :], node_c[:, :], ALU.subtract))
            link(eng.tensor_scalar(node_c[:, :], node_b[:, :], float(WIDTH), None, ALU.is_ge))
            link(eng.tensor_tensor(node_a[:, :], node_a[:, :], node_c[:, :], ALU.add))
            link(eng.tensor_copy(end_part[:, :], node_a[:, :]))
            link(eng.scalar_tensor_tensor(node_b[:, :], node_a[:, :], float(WIDTH), first_place[:, :], ALU.mult,
                                          ALU.is_le))
            eng.tensor_scalar(uncut[:, :], node_b[:, :], -HUGE, None, ALU.mult).then_inc(ends_ready, 1)

        def vector_scan_start(eng, link):
            eng.memset(adst_run[:, 1, :, :], 0.0)
            eng.memset(high_run[:, 1, :, :], -BIG)
            eng.memset(loops_seen[:, :], 0.0)
            link(eng.memset(states[:, 1, :, :], 0.0))
            eng.wait_ge(owner_row_loaded, 16)
            eng.tensor_copy(adst_run[:, 1, :, SPAN - 1], owner_row[:, HE + HEADS:ROW]).then_inc(states_ready, 1)
            eng.wait_ge(states_ready, 1 + FREE)

        def vector_sources(eng, t, h, link):
            eng.wait_ge(indices_loaded[h], t * 16 + 16)
            link(eng.tensor_scalar(bits[:, 0:SPAN], indices[:, h, :], 14, None, ALU.logical_shift_right))
            link(eng.tensor_copy(loop_here[:, h, :], bits[:, 0:SPAN]))
            eng.tensor_scalar(source[:, h, :], indices[:, h, :], NODES - 1, None, ALU.bitwise_and)\
                .then_inc(sources_ready, 1)

        def vector_scan(eng, t, h, link):
            o = 1 - h
            n = t * 2 + h
            loops = loop_here[:, h, :]
            link(eng.tensor_scalar(going[:, :], loops, -1.0, 1.0, ALU.mult, ALU.add))
            link(eng.tensor_scalar(restart[:, :], loops, -HUGE, None, ALU.mult))
            link(eng.tensor_reduce(loop_any[:, :], loops, AX.X, ALU.max))
            link(eng.tensor_tensor(loops_seen[:, :], loops_seen[:, :], loop_any[:, :], ALU.max))
            eng.wait_ge(gathered[h], (t + 1) * (SPAN * 16))
            rows = rows_in[:, h, :].rearrange("p (c f) -> p c f", f=ROW)

            def each_head(x):
                return x.unsqueeze(1).broadcast_to([P, HEADS, SPAN])

            link(eng.tensor_tensor(adst[:, :, :], rows[:, :, HE + HEADS:ROW].rearrange("p c h -> p h c"),
                                   each_head(loops), ALU.mult))
            for k in range(HEADS):
                ins = eng.tensor_tensor_scan(adst_run[:, h, k, :], going[:, :], adst[:, k, :],
                                             adst_run[:, o, k, SPAN - 1:SPAN], ALU.mult, ALU.add)
            link(ins)
            link(eng.tensor_tensor(score[:, :, :], rows[:, :, HE:HE + HEADS].rearrange("p c h -> p h c"),
                                   adst_run[:, h, :, :], ALU.add))
            link(eng.scalar_tensor_tensor(score[:, :, :], score[:, :, :], 0.2, score[:, :, :], ALU.mult, ALU.max))
            link(eng.tensor_copy(high_run[:, h, :, 0], high_run[:, o, :, SPAN]))
            for k in range(HEADS):
                ins = eng.tensor_tensor_scan(high_run[:, h, k, 1:SPAN + 1], restart[:, :], score[:, k, :],
                                             high_run[:, h, k, 0:1], ALU.add, ALU.max)
            link(ins)
            link(eng.tensor_tensor(decay[:, :, :], high_run[:, h, :, 0:SPAN], each_head(restart[:, :]), ALU.add))
            link(eng.tensor_tensor(decay[:, :, :], decay[:, :, :], high_run[:, h, :, 1:SPAN + 1], ALU.subtract))
            eng.tensor_tensor(mass[:, :, :], score[:, :, :], high_run[:, h, :, 1:SPAN + 1],
                              ALU.subtract).then_inc(exponents_ready, 1)
            eng.wait_ge(exps_ready, n + 1)
            for k in range(HEADS):
                ins = eng.tensor_tensor(weighed[:, EXPERTS * k:EXPERTS * (k + 1), :],
                                        rows[:, :, EXPERTS * k:EXPERTS * (k + 1)].rearrange("p c e -> p e c"),
                                        mass[:, k, :].unsqueeze(1).broadcast_to([P, EXPERTS, SPAN]), ALU.mult)
            link(ins)
            eng.wait_ge(states_stored[h], t * 16 + FREE)
            for k in range(HEADS):
                eng.tensor_tensor_scan(states[:, h, :, HEADS + k], decay[:, k, :], mass[:, k, :],
                                       states[:, o, SPAN - 1:SPAN, HEADS + k], ALU.mult, ALU.add)
            for k in range(HE):
                eng.tensor_tensor_scan(states[:, h, :, 2 * HEADS + k], decay[:, k // EXPERTS, :], weighed[:, k, :],
                                       states[:, o, SPAN - 1:SPAN, 2 * HEADS + k], ALU.mult, ALU.add)
            eng.tensor_copy(states[:, h, :, 0:HEADS], high_run[:, h, :, 1:SPAN + 1].rearrange("p h c -> p c h"))\
                .then_inc(states_ready, 1)
            eng.wait_ge(states_ready, n + 2 + FREE)

        def vector_scan_turn(eng, t, more=True):
            count = [0]

            def link(ins):
                ins.then_inc(scan_steps, 1)
                count[0] += 1
                eng.wait_ge(scan_steps, t * SCAN_STEPS + count[0] + 2)

            vector_sources(eng, t, 1, link)
            vector_scan(eng, t, 0, link)
            if more:
                vector_sources(eng, t + 1, 0, link)
            vector_scan(eng, t, 1, link)
            assert count[0] == SCAN_STEPS - (0 if more else 2), count[0]

        def scalar_scan(eng, t):
            for h in range(2):
                eng.wait_ge(exponents_ready, t * 2 + h + 1)
                eng.activation(decay[:, :, :], decay[:, :, :], ACT.Exp)
                eng.activation(mass[:, :, :], mass[:, :, :], ACT.Exp).then_inc(exps_ready, 1)

        def pool_gather(eng, t):
            for h in range(2):
                hold(eng, sources_ready, t * 2 + h + 1, pool_ticks)
                hold(eng, states_ready, t * 2 + h + FREE, pool_ticks)
                for j in range(SPAN):
                    eng.indirect_dma_start(rows_in[:, h, j * ROW:(j + 1) * ROW], None, table,
                                           bass.IndirectOffsetOnAxis(source[:, h, j:j + 1].bitcast(U32), 0),
                                           bounds_check=NODES - 1, oob_is_err=False).then_inc(gathered[h], 16)

        def load_indices(eng, t, h):
            eng.dma_start(indices[:, h, :], order_rows[:, bass.ds((t * 2 + h) * SPAN, SPAN)]).then_inc(indices_loaded[h], 16)

        def sync_scan(eng, t, more=True):
            for h in range(2):
                if more:
                    hold(eng, sources_ready, t * 2 + h + 1, sync_ticks)
                    load_indices(eng, t + 1, h)
                hold(eng, states_ready, t * 2 + h + 2 + FREE, sync_ticks)
                eng.dma_start(state_rows[:, bass.ds((t * 2 + h) * (SPAN * ROW), SPAN * ROW)],
                              states[:, h, :, :].rearrange("p c f -> p (c f)")).then_inc(states_stored[h], 16)

        def vector_chain(eng, link):
            link(eng.tensor_copy(chain_in[:, 0, 0:HEADS], states[:, 1, SPAN - 1, 0:HEADS]))
            link(eng.tensor_copy(chain_in[:, 0, HEADS:CARRY].rearrange("p (h e) -> p h e", h=HEADS),
                                 states[:, 1, SPAN - 1, 0:HEADS].unsqueeze(2).broadcast_to([P, HEADS, EXPERTS])))
            link(eng.tensor_copy(chain_in[:, 1, :], states[:, 1, SPAN - 1, HEADS:ROW]))
            eng.tensor_copy(chain_in[:, 2, :], loops_seen[:, 0:1].broadcast_to([P, CARRY])).then_inc(chain_in_ready, 1)
            eng.wait_ge(chain_turned, 1)
            for k in range(3):
                ins = eng.tensor_copy(chain[:, k, :], T[0:CARRY, k * P:(k + 1) * P])
            link(ins)
            maximum, sums, loop = chain[:, 0, :], chain[:, 1, :], chain[:, 2, :]
            link(eng.tensor_scalar(loop, loop, -HUGE, None, ALU.mult))
            link(eng.memset(chain_high[:, 0:1], -BIG))
            link(eng.tensor_tensor_scan(chain_high[:, 1:P + 1], loop, maximum, chain_high[:, 0:1], ALU.add, ALU.max))
            link(eng.tensor_tensor(loop, loop, chain_high[:, 0:P], ALU.add))
            link(eng.tensor_tensor(loop, loop, chain_high[:, 1:P + 1], ALU.subtract))
            eng.tensor_tensor(maximum, maximum, chain_high[:, 1:P + 1], ALU.subtract).then_inc(chain_exponents_ready, 1)
            eng.wait_ge(chain_exps_ready, 1)
            link(eng.tensor_tensor(sums, sums, maximum, ALU.mult))
            link(eng.memset(chain_sum[:, 0:1], 0.0))
            eng.tensor_tensor_scan(chain_sum[:, 1:P + 1], loop, sums, chain_sum[:, 0:1], ALU.mult, ALU.add)\
                .then_inc(chain_ready, 1)
            eng.wait_ge(chain_back, 1)
            eng.tensor_copy(carry_out[:, 0:CARRY], T[:, 0:CARRY])
            eng.tensor_copy(carry_out[:, CARRY:2 * CARRY], T[:, CARRY:2 * CARRY]).then_inc(carry_ready, 1)

        def tensor_chain(eng):
            eng.wait_ge(chain_in_ready, 1)
            for k in range(3):
                ins = eng.transpose(T[0:CARRY, k * P:(k + 1) * P], chain_in[:, k, :], ident[:, :])
            ins.then_inc(chain_turned, 1)
            eng.wait_ge(chain_ready, 1)
            eng.transpose(T[:, 0:CARRY], chain_high[:, 0:P], ident[0:CARRY, 0:CARRY])
            eng.transpose(T[:, CARRY:2 * CARRY], chain_sum[:, 0:P], ident[0:CARRY, 0:CARRY]).then_inc(chain_back, 1)

        def pool_tail(eng, t):
            hold(eng, node_rows_used, t + FREE, pool_ticks)
            eng.tensor_copy(tail_index[:, 0, :], end_place.bitcast(I32)[:, bass.ds(t * G, G)])
            eng.tensor_copy(tail_index[:, 1, :], end_part.bitcast(I32)[:, bass.ds(t * G, G)]).then_inc(tail_staged, 1)
            hold(eng, tail_staged, t + 1, pool_ticks)
            for g in range(G):
                eng.indirect_dma_start(node_states[:, g * ROW:(g + 1) * ROW], None,
                                       state_rows.rearrange("p (c f) -> (p c) f", f=ROW),
                                       bass.IndirectOffsetOnAxis(tail_index[:, 0, g:g + 1].bitcast(U32), 0),
                                       bounds_check=PLACES - 1, oob_is_err=False).then_inc(node_rows_loaded, 16)
                eng.indirect_dma_start(node_carry[:, g * 2 * CARRY:(g + 1) * 2 * CARRY], None, carry_rows,
                                       bass.IndirectOffsetOnAxis(tail_index[:, 1, g:g + 1].bitcast(U32), 0),
                                       bounds_check=P - 1, oob_is_err=False).then_inc(node_rows_loaded, 16)

        def vector_tail(eng, t):
            count = [0]

            def link(ins):
                ins.then_inc(tail_steps, 1)
                count[0] += 1
                eng.wait_ge(tail_steps, t * TAIL_STEPS + count[0])

            eng.wait_ge(node_rows_loaded, t * 32 * G + 32 * G)
            own = node_states[:, :].rearrange("p (g f) -> p g f", g=G)
            taken = node_carry[:, :].rearrange("p (g f) -> p g f", g=G)
            link(eng.tensor_copy(own_high[:, :, 0:HEADS], own[:, :, 0:HEADS]))
            for g in range(G):
                ins = eng.tensor_copy(own_high[:, g, HEADS:CARRY].rearrange("p (h e) -> p h e", h=HEADS),
                                      own[:, g, 0:HEADS].unsqueeze(2).broadcast_to([P, HEADS, EXPERTS]))
            link(ins)
            link(eng.tensor_tensor(taken_high[:, :, :], taken[:, :, 0:CARRY],
                                   uncut[:, bass.ds(t * G, G)].unsqueeze(2).broadcast_to([P, G, CARRY]), ALU.add))
            link(eng.tensor_tensor(both_high[:, :, :], own_high[:, :, :], taken_high[:, :, :], ALU.max))
            link(eng.tensor_tensor(own_high[:, :, :], own_high[:, :, :], both_high[:, :, :], ALU.subtract))
            eng.tensor_tensor(taken_high[:, :, :], taken_high[:, :, :], both_high[:, :, :],
                              ALU.subtract).then_inc(node_exponents_ready, 1)
            eng.wait_ge(node_exps_ready, t + 1)
            link(eng.tensor_tensor(own_high[:, :, :], own_high[:, :, :], own[:, :, HEADS:ROW], ALU.mult))
            link(eng.tensor_tensor(taken_high[:, :, :], taken_high[:, :, :], taken[:, :, CARRY:2 * CARRY], ALU.mult))
            eng.tensor_tensor(own_high[:, :, :], own_high[:, :, :], taken_high[:, :, :], ALU.add)\
                .then_inc(node_rows_used, 1)
            eng.wait_ge(node_rows_used, t + 1 + FREE)
            link(eng.tensor_scalar(denominator[:, :, :], own_high[:, :, 0:HEADS], 1e-16, None, ALU.add))
            link(eng.reciprocal(denominator[:, :, :], denominator[:, :, :]))
            for g in range(G):
                ins = eng.tensor_tensor(agg[:, g, :].rearrange("p (h e) -> p h e", h=HEADS),
                                        own_high[:, g, HEADS:CARRY].rearrange("p (h e) -> p h e", h=HEADS),
                                        denominator[:, g, :].unsqueeze(2).broadcast_to([P, HEADS, EXPERTS]), ALU.mult)
            link(ins)

            def wide(x):
                return x.unsqueeze(1).broadcast_to([P, G, HE])

            def over(x, n=HE):
                return x.unsqueeze(2).broadcast_to([P, G, n])

            link(eng.tensor_tensor(agg[:, :, :], agg[:, :, :], wide(row("L3_ffn_b_gat")), ALU.add))
            link(eng.tensor_reduce(peak[:, :], agg[:, :, :], AX.X, ALU.add))
            link(eng.tensor_scalar(peak[:, :], peak[:, :], 1.0 / HE, None, ALU.mult))
            link(eng.tensor_tensor(agg[:, :, :], agg[:, :, :], over(peak[:, :]), ALU.subtract))
            link(eng.tensor_tensor(gat_part[:, :, :], agg[:, :, :], agg[:, :, :], ALU.mult))
            link(eng.tensor_reduce(peak[:, :], gat_part[:, :, :], AX.X, ALU.add))
            eng.tensor_scalar(peak[:, :], peak[:, :], 1.0 / HE, None, ALU.mult).then_inc(agg_variance_ready, 1)
            eng.wait_ge(agg_deviation_ready, t + 1)
            link(eng.reciprocal(rstd[:, :], deviation[:, :]))
            link(eng.tensor_tensor(agg[:, :, :], agg[:, :, :], over(rstd[:, :]), ALU.mult))
            link(eng.tensor_tensor(agg[:, :, :], agg[:, :, :], wide(row("L3_ffn_ln_gamma")), ALU.mult))
            link(eng.tensor_tensor(agg[:, :, :], agg[:, :, :], wide(row("L3_ffn_ln_beta")), ALU.add))
            link(eng.tensor_reduce(logits[:, :, 0:EXPERTS], agg[:, :, :].rearrange("p g (h e) -> p g e h", h=HEADS),
                                   AX.X, ALU.add))
            link(eng.tensor_scalar(logits[:, :, 0:EXPERTS], logits[:, :, 0:EXPERTS], 1.0 / HEADS, None, ALU.mult))
            small = logits[:, :, 0:EXPERTS]
            ch, se = chosen[:, :, 0:EXPERTS], second[:, :, 0:EXPERTS]
            first_largest(eng, link, ch, small, EXPERTS)
            link(eng.tensor_copy(top[:, 0, :], peak[:, :]))
            link(eng.scalar_tensor_tensor(small, ch, -BIG, small, ALU.mult, ALU.add))
            first_largest(eng, link, se, small, EXPERTS)
            eng.tensor_tensor(top[:, 1, :], peak[:, :], top[:, 0, :], ALU.subtract).then_inc(tail_gap_ready, 1)
            eng.wait_ge(tail_gap_exp_ready, t + 1)
            link(eng.tensor_scalar(top[:, 0, :], gap_exp[:, :], 1.0, None, ALU.add))
            link(eng.reciprocal(top[:, 1, :], top[:, 0, :]))
            link(eng.tensor_tensor(top[:, 0, :], gap_exp[:, :], top[:, 1, :], ALU.mult))
            link(eng.tensor_tensor(ch, ch, over(top[:, 1, :], EXPERTS), ALU.mult))
            link(eng.tensor_tensor(se, se, over(top[:, 0, :], EXPERTS), ALU.mult))
            eng.tensor_tensor(tail_gate[:, :, :], ch, se, ALU.add).then_inc(tail_gate_ready, 1)
            eng.wait_ge(tail_gate_ready, t + 1)
            eng.wait_ge(tail_x_loaded, t * 16 + 16)
            for e in range(EXPERTS):
                eng.wait_ge(tail_outputs_ready, t * EXPERTS + e + 1)
                for g in range(G):
                    ins = eng.scalar_tensor_tensor(X[:, g, :], Y[e % 2][:, g, :], tail_gate[:, g, e:e + 1], X[:, g, :],
                                                   ALU.mult, ALU.add)
                ins.then_inc(tail_outputs_used, 1)
                eng.wait_ge(tail_outputs_used, t * EXPERTS + e + 1 + FREE)
            eng.wait_ge(tail_bias_ready, t + 1)
            eng.wait_ge(out_stored, t * 16 + FREE)
            eng.tensor_tensor(XIN[:, :, :], X[:, :, :], T4[:, :, :], ALU.add).then_inc(out_ready, 1)
            assert count[0] == TAIL_STEPS, count[0]

        def scalar_tail(eng, t):
            for n in range(8):
                eng.wait_ge(tail_hidden_ready, t * 8 + n + 1)
                if n >= 4:
                    eng.wait_ge(tail_outputs_ready, t * EXPERTS + n // 2 - 1)
                eng.activation(HT[:, n % 4, :], HP[n % 2][:, :], ACT.Gelu, bias=b1_4[:, n:n + 1])\
                    .then_inc(tail_hidden_done, 1)
                if n == 3:
                    eng.wait_ge(node_exponents_ready, t + 1)
                    eng.activation(own_high[:, :, :], own_high[:, :, :], ACT.Exp)
                    eng.activation(taken_high[:, :, :], taken_high[:, :, :], ACT.Exp).then_inc(node_exps_ready, 1)
                    eng.wait_ge(agg_variance_ready, t + 1)
                    eng.activation(deviation[:, :], peak[:, :], ACT.Sqrt, bias=eps[:, 0:1])\
                        .then_inc(agg_deviation_ready, 1)
                    eng.wait_ge(tail_gap_ready, t + 1)
                    eng.activation(gap_exp[:, :], top[:, 1, :], ACT.Exp).then_inc(tail_gap_exp_ready, 1)
            eng.wait_ge(tail_gates_turned, t + 1)
            eng.activation(CT[0:G * EXPERTS, :], T[0:G * EXPERTS, 0:P], ACT.Copy).then_inc(tail_gate_columns_ready, 1)

        def tensor_tail(eng, t):
            def hidden(n):
                if n >= 2:
                    eng.wait_ge(tail_hidden_done, t * 8 + n - 1 + FREE)
                eng.matmul(HP[n % 2][:, :], w1_4[:, n * D:(n + 1) * D], ZT[:, :], start=True, stop=True)\
                    .then_inc(tail_hidden_ready, 1)

            eng.wait_ge(tail_z_loaded, t * 16 + 16)
            eng.wait_ge(tail_hidden_done, t * 8 + FREE)
            hidden(0)
            hidden(1)
            for e in range(EXPERTS):
                if e + 1 < EXPERTS:
                    hidden(2 * e + 2)
                    hidden(2 * e + 3)
                eng.wait_ge(tail_hidden_done, t * 8 + 2 * e + 2 + FREE)
                eng.wait_ge(tail_outputs_used, t * EXPERTS + max(e - 1, 0) + FREE)
                for g in range(G):
                    for c in range(2):
                        n = 2 * e + c
                        ins = eng.matmul(Y[e % 2][:, g, :], HT[:, n % 4, g * N:(g + 1) * N], w2_4[:, n * D:(n + 1) * D],
                                         start=(c == 0), stop=(c == 1))
                ins.then_inc(tail_outputs_ready, 1)
            eng.wait_ge(tail_gate_ready, t + 1)
            eng.transpose(T[0:G * EXPERTS, 0:P], tail_gate[:, :, :].rearrange("p g e -> p (g e)"),
                          ident[:, :]).then_inc(tail_gates_turned, 1)
            eng.wait_ge(tail_gate_columns_ready, t + 1)
            eng.wait_ge(out_ready, t + FREE)
            eng.matmul(T[:, :], CT[0:G * EXPERTS, :], b2_4[:, :], start=True,
                       stop=True).then_inc(tail_bias_ready, 1)

        def load_tail_z(eng, t):
            eng.dma_start(ZT[:, :], zT_mid[bass.ds(t, 1)].rearrange("t p c -> p (t c)")).then_inc(tail_z_loaded, 16)

        def load_tail_x(eng, t):
            eng.dma_start(X[:, :, :].rearrange("p g d -> p (g d)"),
                          x_mid[bass.ds(t, 1)].rearrange("t p c -> p (t c)")).then_inc(tail_x_loaded, 16)

        def sync_tail(eng, t, more=True):
            if more:
                hold(eng, tail_outputs_ready, (t + 1) * EXPERTS, sync_ticks)
                load_tail_z(eng, t + 1)
            hold(eng, out_ready, t + 1 + FREE, sync_ticks)
            if more:
                load_tail_x(eng, t + 1)
            eng.dma_start(out[bass.ds(t * G, G)].rearrange("g n d -> n g d"), XIN[:, :, :]).then_inc(out_stored, 16)

        def pool_setup(eng):
            eng.iota(loop_ids[:, :], [[P, LOOPS]], base=0, channel_multiplier=1).then_inc(loops_made, 1)

        def sync_setup(eng):
            for free in (pairs_counted, *results_stored, states_ready, *states_stored, node_rows_used,
                         tail_outputs_used, tail_hidden_done, out_stored, out_ready, next_copied,
                         ranks_taken):
                eng.sem_inc(free, FREE)
            eng.sem_inc(tile_counted, FREE)
            eng.dma_start(consts[:, :], consts_in).then_inc(consts_loaded, 16)
            eng.dma_start(row_tile[:, :], rows_in_dram.partition_broadcast(P)).then_inc(consts_loaded, 16)
            eng.dma_start(POS.bitcast(I32)[:, LOOPS:TILES], edges[1].rearrange("(p c) -> p c", p=P))\
                .then_inc(edges_loaded, 16)
            eng.dma_start(VAL.bitcast(I32)[:, LOOPS:TILES], edges[0].rearrange("(p c) -> p c", p=P))\
                .then_inc(edges_loaded, 16)
            for i in range(2):
                load_x(eng, 0, i)
                load_adj(eng, 0, i)
                load_adjT(eng, 0, i)
            for name, _ in MATS:
                eng.dma_start(mat[name][:, :], mats[name]).then_inc(weights_loaded, 16)
            eng.wait_ge(cleared, 1)
            for tile, bias, n in ((b2_0, 0, 8), (b2_1, 1, 8), (b2_4, 2, EXPERTS)):
                for g in range(G):
                    eng.dma_start(tile[g * n:(g + 1) * n, g * D:(g + 1) * D], expert_biases[bias])\
                        .then_inc(weights_loaded, 16)
            for i in range(2):
                load_blocks(eng, 0, i)
            for c in range(4):
                eng.dma_start(order_rows[:, c * CHUNK:(c + 1) * CHUNK], high[:, 0:2 * CHUNK].bitcast(I32))\
                    .then_inc(places_blanked, 16)

        def vector_setup(eng, link):
            eng.memset(b2_0[:, :], 0.0)
            eng.memset(b2_1[:, :], 0.0)
            eng.memset(b2_4[:, :], 0.0)
            for i in range(2):
                eng.memset(ABINs[i][:, :], 0.0)
            eng.memset(digit[:, :], 0.0)
            eng.memset(high[:, :], 0.0).then_inc(cleared, 1)
            eng.memset(zeros_b[:, :], 0.0)
            eng.memset(ones[:, :], 1.0)
            eng.memset(zeros[:, :], 0.0)
            eng.memset(eps[:, :], EPS)
            link(eng.memset(one[:, :], 1.0))
            eng.wait_ge(consts_loaded, 32)
            link(eng.tensor_copy(iota4[:, :, :], iota[:, :].unsqueeze(2).broadcast_to([P, P, 4])))
            eng.tensor_copy(ident_b[:, :], ident)
            eng.tensor_scalar(ident128_b[:, :], ident, float(P), None, ALU.mult).then_inc(bf_consts_ready, 1)
            link(eng.tensor_tensor(gate_bias0[:, :], row("L0_ffn_bg"), row("L0_ffn_bias"), ALU.add))
            fusion = row("L3_gnn_fusion_w")
            link(eng.tensor_reduce(share_sum[:, :], fusion, AX.X, ALU.max))
            eng.tensor_scalar(share[:, :], fusion, share_sum[:, 0:1], None, ALU.subtract).then_inc(fusion_shifted, 1)
            eng.wait_ge(fusion_exp_ready, 1)
            link(eng.tensor_reduce(share_sum[:, :], share[:, :], AX.X, ALU.add))
            link(eng.reciprocal(share_sum[:, :], share_sum[:, :]))
            link(eng.tensor_scalar(share[:, :], share[:, :], share_sum[:, 0:1], None, ALU.mult))
            link(eng.tensor_tensor(share[:, :], share[:, :], const["joint_share"], ALU.mult))
            eng.wait_ge(weights_loaded, 16 * (len(MATS) + 3 * G))
            eng.tensor_copy(wr_wide[:, :], wr[:, 0:1].broadcast_to([P, P])).then_inc(weights_ready0, 1)

        block = ctx.enter_context(nc.Block())
        PAIRS = NET_TURNS // 2

        def both(part, *args):
            streams = [part(i, *args) for i in range(2)]
            for pieces in zip_longest(*streams):
                assert len(pieces) == 2

        @block.sync
        def _(sp):
            sync_setup(sp)
            with sp.Fori(0, PAIRS - 1) as t:
                both(lambda i: sync_network(sp, t, i, True))
            both(lambda i: sync_network(sp, PAIRS - 1, i, False))
            for half in range(2):
                sp.wait_ge(scattered[half], SCATTERS * 256)
            load_indices(sp, 0, 0)
            load_indices(sp, 0, 1)
            with sp.Fori(0, SCAN_TURNS - 1) as t:
                sync_scan(sp, t)
            sync_scan(sp, SCAN_TURNS - 1, more=False)
            load_tail_z(sp, 0)
            load_tail_x(sp, 0)
            sp.wait_ge(carry_ready, 1)
            sp.dma_start(carry_rows, carry_out[:, :]).then_inc(carry_stored, 16)
            with sp.Fori(0, NET_TURNS - 1) as t:
                sync_tail(sp, t)
            sync_tail(sp, NET_TURNS - 1, more=False)
            sp.wait_ge(out_stored, NET_TURNS * 16 + FREE)
            for i in range(2):
                sp.wait_ge(results_stored[i], PAIRS * 48 + FREE)
            for h in range(2):
                sp.wait_ge(states_stored[h], SCAN_TURNS * 16 + FREE)

        @block.gpsimd
        def _(pool):
            pool_setup(pool)
            pool.wait_ge(places_blanked, 64)
            pool_scatter(pool, 0)
            with pool.Fori(1, SCATTERS) as t:
                pool_scatter(pool, t)
            pool.wait_ge(owner_written, 1)
            for i in range(2):
                pool.wait_ge(results_stored[i], PAIRS * 48 + FREE)
            pool.indirect_dma_start(owner_row[:, :], None, table, bass.IndirectOffsetOnAxis(owner[:, :].bitcast(U32), 0),
                                    bounds_check=NODES - 1, oob_is_err=False).then_inc(owner_row_loaded, 16)
            with pool.Fori(0, SCAN_TURNS) as t:
                pool_gather(pool, t)
            for h in range(2):
                pool.wait_ge(states_stored[h], SCAN_TURNS * 16 + FREE)
            pool.wait_ge(carry_stored, 16)
            with pool.Fori(0, NET_TURNS) as t:
                pool_tail(pool, t)

        @block.scalar
        def _(act):
            act.wait_ge(fusion_shifted, 1)
            act.activation(share[:, :], share[:, :], ACT.Exp).then_inc(fusion_exp_ready, 1)
            with act.Fori(0, TURNS) as t:
                scalar_rank(act, t)
            with act.Fori(0, PAIRS) as t:
                both(lambda i: scalar_network(act, t, i))
            with act.Fori(0, SCAN_TURNS) as t:
                scalar_scan(act, t)
            act.wait_ge(chain_exponents_ready, 1)
            act.activation(chain[:, 0, :], chain[:, 0, :], ACT.Exp)
            act.activation(chain[:, 2, :], chain[:, 2, :], ACT.Exp).then_inc(chain_exps_ready, 1)
            with act.Fori(0, NET_TURNS) as t:
                scalar_tail(act, t)

        @block.vector
        def _(dve):
            chain_count = [0]

            def link(ins):
                ins.then_inc(vector_links, 1)
                chain_count[0] += 1
                dve.wait_ge(vector_links, chain_count[0])

            def first_link(ins, n=[0]):
                ins.then_inc(scan_steps, 1)
                n[0] += 1
                dve.wait_ge(scan_steps, n[0])

            vector_setup(dve, link)
            dve.wait_ge(places_blanked, 64)
            vector_prepare(dve, link)
            with dve.Fori(0, TURNS) as t:
                vector_count(dve, t)
            vector_bases(dve, link)
            group_onehots(dve, 0, 0)
            with dve.Fori(0, TURNS) as t:
                vector_rank(dve, t)
            dve.wait_ge(next_copied, 4 * UNROLL * TURNS + FREE)
            with dve.Fori(0, PAIRS) as t:
                steps = [0]
                both(lambda i: vector_network(dve, t, i, steps))
            assert steps[0] == 2 * NET_STEPS, steps[0]
            for half in range(2):
                dve.wait_ge(scattered[half], SCATTERS * 256)
            vector_owner(dve, link)
            vector_scan_start(dve, link)
            vector_sources(dve, 0, 0, first_link)
            with dve.Fori(0, SCAN_TURNS - 1) as t:
                vector_scan_turn(dve, t)
            vector_scan_turn(dve, SCAN_TURNS - 1, more=False)
            vector_chain(dve, link)
            with dve.Fori(0, NET_TURNS) as t:
                vector_tail(dve, t)

        @block.tensor
        def _(pe):
            pe.wait_ge(bf_consts_ready, 1)
            pe.matmul(T[:, 0:P], zeros_b[:, :], zeros_b[:, :], start=True, stop=False, skip_group_check=True)
            with pe.Fori(0, TURNS) as t:
                tensor_count(pe, t)
            pe.matmul(T[:, 0:P], zeros_b[:, :], zeros_b[:, :], start=False, stop=True,
                      skip_group_check=True).then_inc(counts_ready, 1)
            tensor_bases(pe)
            pe.wait_ge(weights_ready0, 1)
            with pe.Fori(0, TURNS) as t:
                tensor_rank(pe, t)
            pe.wait_ge(next_copied, 4 * UNROLL * TURNS + FREE)
            pe.matmul(NEXT, zeros_b[:, :], zeros_b[:, :], start=False, stop=True, skip_group_check=True)
            with pe.Fori(0, PAIRS) as t:
                both(lambda i: tensor_network(pe, t, i))
            pe.wait_ge(begun_ready, 1)
            pe.matmul(T[:, 0:1], begun_sum[:, :], ones[:, 0:1], start=True, stop=True).then_inc(owner_ready, 1)
            tensor_chain(pe)
            with pe.Fori(0, NET_TURNS) as t:
                tensor_tail(pe, t)

def kernel(**inputs):
    import concourse.bacc as bacc
    from concourse.bass_utils import run_bass_kernel_spmd

    a = {k: np.asarray(v) for k, v in inputs.items()}

    def hidden_major(w):
        e, h, d = w.shape
        return w.reshape(e, h // P, P, d).transpose(2, 0, 1, 3).reshape(P, -1)

    def feature_major(w):
        return w.transpose(1, 0, 2).reshape(P, -1)

    def bias_columns(b):
        return b.reshape(-1, P).transpose(1, 0)

    mats = {
        "wt0": a["L0_gnn_W"].T, "wg0": a["L0_ffn_Wg"], "w1_0": feature_major(a["L0_ffn_W1"]),
        "w2_0": hidden_major(a["L0_ffn_W2"]), "w_rel": a["L1_gnn_W_rel"], "w_root": a["L1_gnn_W_root"],
        "w1_1": a["L1_ffn_W1"], "wg1": hidden_major(a["L1_ffn_Wg"][None]), "wd_1": hidden_major(a["L1_ffn_Wd"]),
        "w_self": a["L2_gnn_W_self"], "w_neigh": a["L2_gnn_W_neigh"], "wr": a["L2_ffn_wr"], "w1_2": a["L2_ffn_w1"],
        "w2_2": hidden_major(a["L2_ffn_w2"][None]), "w1_3": feature_major(a["L3_gnn_W1"]),
        "w2_3": hidden_major(a["L3_gnn_W2"]), "w_gat": a["L3_ffn_W_gat"], "w1_4": feature_major(a["L3_ffn_W1"]),
        "w2_4": hidden_major(a["L3_ffn_W2"]), "b1_0": bias_columns(a["L0_ffn_b1"]),
        "b1_1": bias_columns(a["L1_ffn_b1"]), "b1_2": bias_columns(a["L2_ffn_b1"]),
        "b1_3": bias_columns(a["L3_gnn_b1"]), "b1_4": bias_columns(a["L3_ffn_b1"]),
    }
    lower = np.tril(np.ones((P, P), np.float32), -1)
    groups_of = np.zeros((GROUPS, JOINTS), np.float32)
    for k, nodes in enumerate(JOINT_GROUPS):
        groups_of[k, nodes] = 1.0
    one_of = np.tile(groups_of, (1, G))
    member = np.zeros((P, GROUPS, GJ), np.float32)
    member[:GJ] = one_of.T[:, :, None] * one_of[None]
    joint_share = np.zeros((P, GROUPS), np.float32)
    joint_share[:GJ] = one_of.T
    tables = {
        "ident": np.eye(P, dtype=np.float32), "iota": np.tile(np.arange(P, dtype=np.float32), (P, 1)),
        "before": lower.T, "earlier": lower, "falling": np.tile(np.arange(8, 0, -1, dtype=np.float32), (P, 1)),
        "cut_row": np.tile(np.arange(P, dtype=np.float32) * WIDTH, (P, 1)), "member": member.reshape(P, -1),
        "joint_share": joint_share,
    }
    data = {
        "x_in": a["x"], "adj_in": a["adj"], "adjT_in": a["adj"].transpose(0, 2, 1), "edges": a["L3_ffn_edge_index"],
        "rows_in_dram": np.concatenate([a[name].reshape(-1) for name, _ in ROWS]),
        "consts_in": np.concatenate([tables[name] for name, _ in CONSTS], axis=1),
        "bias0": a["L0_ffn_b2"], "bias1": a["L1_ffn_bd"], "bias2": a["L3_ffn_b2"],
    }
    data.update({f"m_{name}": w for name, w in mats.items()})
    data = {name: np.ascontiguousarray(v) for name, v in data.items()}

    nc = bacc.Bacc("TRN2", target_bir_lowering=False, num_devices=1)
    t = {name: nc.dram_tensor(name, v.shape, mybir.dt.from_np(v.dtype), kind="ExternalInput").ap()
         for name, v in data.items()}
    out = nc.dram_tensor("out", (B, N, D), F32, kind="ExternalOutput").ap()
    build(nc, t["x_in"], t["adj_in"], t["adjT_in"], t["edges"], t["rows_in_dram"], t["consts_in"],
          [t["bias0"], t["bias1"], t["bias2"]], {name: t[f"m_{name}"] for name, _ in MATS}, out)
    return run_bass_kernel_spmd(nc, [data], core_ids=[0]).results[0]["out"]
```

```python
from contextlib import ExitStack
from itertools import zip_longest

import concourse.bass as bass
import numpy as np
from concourse import mybir

F32, BF16 = mybir.dt.float32, mybir.dt.bfloat16
I32, U32 = mybir.dt.int32, mybir.dt.uint32
ALU, ACT, AX = mybir.AluOpType, mybir.ActivationFunctionType, mybir.AxisListType

P = 128
B, N, D = 128, 128, 128
NODES = B * N
EDGES = 524288
G = 4
NET_TURNS = B // G
NORMS = 10
HIDS, YS = 24, 16
JOINTS, GJ = 25, G * 25
JOINT_GROUPS = [list(range(25)), [0, 1, 2, 3, 4, 5, 6, 7, 8], [0, 9, 10, 11, 12, 13, 14], [6, 7, 8, 12, 13, 14],
                [3, 4, 5, 9, 10, 11]]
GROUPS = len(JOINT_GROUPS)
KEPT = max(1, N // 2) - 1
HEADS, EXPERTS = 4, 4
HE = HEADS * EXPERTS
ROW = HE + 2 * HEADS
CARRY = HEADS + HE
EPS = 1e-5
BIG, HUGE = 1e30, 3e38

LOOPS = NODES // P
TILES = LOOPS + EDGES // P
PLACES = TILES * P
WIDTH = PLACES // P
CHUNK = TILES // 4
UNROLL = 4
TURNS = TILES // (4 * UNROLL)
SCATTERS = TILES // 32
FAR = 1 << 20
SPAN = 64
SCAN_TURNS = WIDTH // (2 * SPAN)
OWN = 32
TWO_FREE = 2
FREE = 1

NET_STEPS, RANK_STEPS, SCAN_STEPS, TAIL_STEPS = 90, 2, 30, 40

ROWS = [("L0_gnn_b", D), ("L0_gnn_alpha", 1), ("L0_ffn_bg", 8), ("L0_ffn_bias", 8), ("L1_gnn_ln_gamma", D),
        ("L1_gnn_ln_beta", D), ("L1_gnn_b_rel", D), ("L1_ffn_bg", 8), ("L2_gnn_gamma", D), ("L2_gnn_beta", D),
        ("L2_ffn_br", 1), ("L2_ffn_b2", D), ("L3_gnn_b2", GROUPS * D), ("L3_gnn_fusion_w", GROUPS),
        ("L3_ffn_att_src", HE), ("L3_ffn_att_dst", HE), ("L3_ffn_b_gat", HE), ("L3_ffn_ln_gamma", HE),
        ("L3_ffn_ln_beta", HE)]
ROW_AT = {}
for _name, _n in ROWS:
    ROW_AT[_name] = (sum(n for _, n in ROWS[:len(ROW_AT)]), _n)
ROW_TOTAL = sum(n for _, n in ROWS)

MATS = [("wt0", D), ("wg0", 8), ("w1_0", 8 * 256), ("w2_0", 8 * 256), ("w_rel", D), ("w_root", D), ("w1_1", 512),
        ("wg1", 4 * 8), ("wd_1", 8 * 512), ("w_self", D), ("w_neigh", D), ("wr", 1), ("w1_2", 512), ("w2_2", 512),
        ("w1_3", GROUPS * 256), ("w2_3", GROUPS * 256), ("w_gat", HE), ("w1_4", EXPERTS * 256),
        ("w2_4", EXPERTS * 256), ("b1_0", 16), ("b1_1", 4), ("b1_2", 4), ("b1_3", 2 * GROUPS), ("b1_4", 8)]
CONSTS = [("ident", P), ("iota", P), ("before", P), ("earlier", P), ("falling", 8), ("cut_row", P),
          ("member", GROUPS * GJ), ("joint_share", GROUPS)]
CONST_TOTAL = sum(n for _, n in CONSTS)

def build(nc, x_in, adj_in, adjT_in, edges, rows_in_dram, consts_in, expert_biases, mats, out):
    table = nc.dram_tensor("table", (NODES, ROW), F32).ap()
    x_mid = nc.dram_tensor("x_mid", (NET_TURNS, P, G * D), F32).ap()
    zT_mid = nc.dram_tensor("zT_mid", (NET_TURNS, P, G * D), F32).ap()
    order = nc.dram_tensor("order", (PLACES, 1), I32).ap()
    order_rows = order.rearrange("(p c) o -> p (c o)", p=P)
    state_rows = nc.dram_tensor("state_rows", (P, WIDTH * ROW), F32).ap()
    carry_rows = nc.dram_tensor("carry_rows", (P, 2 * CARRY), F32).ap()

    with ExitStack() as ctx:
        def sb(name, shape, dt=F32, stack=ctx):
            return stack.enter_context(nc.sbuf_tensor(name, shape, dt))

        def bank(name, shape=(P, 512)):
            return ctx.enter_context(nc.psum_tensor(name, list(shape), F32))

        def sem(name):
            return ctx.enter_context(nc.semaphore(name))

        Ts = [bank(f"T{i}") for i in range(2)]
        HP = [bank(f"HP{i}") for i in range(2)]
        Ys = [[bank(f"Y{i}{k}", (P, 4, D)) for k in range(2)] for i in range(2)]
        T4s = [T[:, :].rearrange("p (g d) -> p g d", g=4) for T in Ts]
        T, T4, Y = Ts[0], T4s[0], Ys[0]
        KEYS, NEXT = HP, Ts[1][:, 0:P]
        LOOK = [bank_[:, :, :].rearrange("p k d -> p (k d)") for bank_ in Ys[0]]
        TURNED = [bank_[:, 0:2, :].rearrange("p k d -> p (k d)").bitcast(BF16) for bank_ in Ys[1]]

        consts = sb("consts", [P, CONST_TOTAL])
        at = 0
        const = {}
        for name, n in CONSTS:
            const[name] = consts[:, at:at + n]
            at += n
        ident, iota, before, earlier, falling, cut_row = (
            const[n] for n in ("ident", "iota", "before", "earlier", "falling", "cut_row"))
        member = const["member"][0:GJ, :].rearrange("p (k n) -> p k n", k=GROUPS)
        row_tile = sb("row_tile", [P, ROW_TOTAL])

        def row(name):
            a, n = ROW_AT[name]
            return row_tile[:, a:a + n]

        mat = {name: sb(name, [P, n]) for name, n in MATS}
        (wt0, wg0, w1_0, w2_0, w_rel, w_root, w1_1, wg1, wd_1, w_self, w_neigh, wr, w1_2, w2_2, w1_3, w2_3, w_gat,
         w1_4, w2_4, b1_0, b1_1, b1_2, b1_3, b1_4) = (mat[name] for name, _ in MATS)
        b2_0 = sb("b2_0", [G * 8, G * D])
        b2_1 = sb("b2_1", [G * 8, G * D])
        b2_4 = sb("b2_4", [G * EXPERTS, G * D])
        wr_wide = sb("wr_wide", [P, P])
        ident_b, ident128_b = sb("ident_b", [P, P], BF16), sb("ident128_b", [P, P], BF16)
        zeros_b = sb("zeros_b", [P, P], BF16)
        ones = sb("ones", [P, P])
        zeros = sb("zeros", [P, P])
        eps = sb("eps", [P, 1])
        one = sb("one", [P, 1])
        gate_bias0 = sb("gate_bias0", [P, 8])
        share = sb("share", [P, GROUPS])
        share_sum = sb("share_sum", [P, 1])

        count = sb("count", [P, P])
        totals = sb("totals", [P, P])
        base_high = sb("base_high", [P, P])
        first_place, last_place = sb("first_place", [P, P]), sb("last_place", [P, P])

        def pair(name, shape, stack=ctx):
            return [sb(f"{name}{i}", shape, F32, stack) for i in range(2)]

        XINs, As, ATs, Xs = (pair(n, [P, G, D]) for n in ("XIN", "A", "AT", "X"))
        ABINs, TABs = pair("ABIN", [GJ, GJ]), pair("TAB", [P, G, ROW])
        ZTs = pair("ZT", [P, G * N])
        HT = sb("HT", [P, 4, G * N])
        deviation, rstd, peak, first, gap_exp = (
            sb(n, [P, G]) for n in ("deviation", "rstd", "peak", "first", "gap_exp"))
        top = sb("top", [P, 2, G])
        logits, chosen, second = (sb(n, [P, G, 8]) for n in ("logits", "chosen", "second"))
        CT = sb("CT", [G * 8, P])
        gat_part = sb("gat_part", [P, G, HE])
        bits = sb("bits", [P, CHUNK], I32)
        bitsf = bits[:, :].bitcast(F32)
        with ExitStack() as sorting:
            POS_t = sb("POS", [P, TILES], F32, sorting)
            VAL_t = sb("VAL", [P, TILES], F32, sorting)
            POS, VAL = POS_t[:, :], VAL_t[:, :]
            loop_ids = sb("loop_ids", [P, LOOPS], I32, sorting)
            place16, equal16, skip16, key16 = (sb(n, [P, 16], F32, sorting)
                                               for n in ("place16", "equal16", "skip16", "key16"))
            stage_place = sb("stage_place", [P, 2, 16], I32, sorting)
            stage_value = sb("stage_value", [P, 2, 16], I32, sorting)
            with ExitStack() as ranking:
                digit = sb("digit", [P, TILES + 4], BF16, ranking)
                high = sb("high", [P, TILES + 4], BF16, ranking)
                OH = sb("OH", [P, 2, P, 4], BF16, ranking)
                OH2 = sb("OH2", [P, 2, P, 4], BF16, ranking)
                iota4 = sb("iota4", [P, P, 4], BF16, ranking)
                OHT = sb("OHT", [P, 4 * P], F32, ranking)
                picked = sb("picked", [P, 8, P], F32, ranking)
                next_place = sb("next_place", [P, 8, P], F32, ranking)
            Zs, Hs, XSs, NBs, SPs = (pair(n, [P, G, D], sorting) for n in ("Z", "H", "XS", "NB", "SP"))
            gates, scales_io, weights = (pair(n, s, sorting) for n, s in (
                ("gate", [P, G, 8]), ("scale_io", [P, 2 * G]), ("weight", [P, G])))
            A5s, NT5s = (pair(n, [GJ, GROUPS, GJ], sorting) for n in ("A5", "NT5"))
            inv5s, ZSs, Fs, FBs = (pair(n, s, sorting) for n, s in (
                ("inv5", [GJ, GROUPS]), ("ZS", [GJ, D]), ("F", [GJ, D]), ("FB", [JOINTS, G, D])))
            R, W = (sb(n, [P, G, D], F32, sorting) for n in ("R", "W"))
            NBT, AGT = (sb(n, [P, G * N], F32, sorting) for n in ("NBT", "AGT"))
            stats, moments = sb("stats", [P, G, 6], F32, sorting), sb("moments", [P, G, 2], F32, sorting)
            degree, no_edge, degree_root = (sb(n, [P, 2 * G], F32, sorting)
                                            for n in ("degree", "no_edge", "degree_root"))
            probs = sb("probs", [P, G, 8], F32, sorting)
            AB = sb("AB", [GJ, GJ], F32, sorting)
            deg5, no5, root5 = (sb(n, [GJ, GROUPS], F32, sorting) for n in ("deg5", "no5", "root5"))
            UT = sb("UT", [P, GROUPS * GJ], F32, sorting)
            H3 = sb("H3", [P, 2, GROUPS, GJ], F32, sorting)
            V5, F5 = sb("V5", [GJ, GROUPS * D], F32, sorting), sb("F5", [GJ, GROUPS, D], F32, sorting)
        begun = sb("begun", [P, OWN, P], BF16)
        begun_sum = sb("begun_sum", [P, P])
        owner = sb("owner", [P, 1], I32)
        owner_row = sb("owner_row", [P, ROW])
        end_place, end_part = sb("end_place", [P, P], I32), sb("end_part", [P, P], I32)
        node_a, node_b, node_c, uncut = (sb(n, [P, P]) for n in ("node_a", "node_b", "node_c", "uncut"))
        indices, source = sb("indices", [P, 2, SPAN], I32), sb("source", [P, 2, SPAN], I32)
        loop_here = sb("loop_here", [P, 2, SPAN])
        going, restart = sb("going", [P, SPAN]), sb("restart", [P, SPAN])
        loop_any, loops_seen = sb("loop_any", [P, 1]), sb("loops_seen", [P, 1])
        rows_in = sb("rows_in", [P, 2, SPAN * ROW])
        states = sb("states", [P, 2, SPAN, ROW])
        adst_run = sb("adst_run", [P, 2, HEADS, SPAN])
        high_run = sb("high_run", [P, 2, HEADS, SPAN + 1])
        adst, score, decay, mass = (sb(n, [P, HEADS, SPAN]) for n in ("adst", "score", "decay", "mass"))
        weighed = sb("weighed", [P, HE, SPAN])
        chain_in, chain = sb("chain_in", [P, 3, CARRY]), sb("chain", [CARRY, 3, P])
        chain_high, chain_sum = sb("chain_high", [CARRY, P + 1]), sb("chain_sum", [CARRY, P + 1])
        carry_out = sb("carry_out", [P, 2 * CARRY])
        tail_index = sb("tail_index", [P, 2, 2 * G], I32)
        node_states, node_carry = sb("node_states", [P, 2 * G * ROW]), sb("node_carry", [P, 2 * G * 2 * CARRY])
        own_high, taken_high, both_high = (sb(n, [P, 2 * G, CARRY]) for n in ("own_high", "taken_high", "both_high"))
        denominator = sb("denominator", [P, 2 * G, HEADS])
        agg, tail_part = sb("agg", [P, 2 * G, HE]), sb("tail_part", [P, 2 * G, HE])
        tail_peak, tail_first, tail_deviation, tail_rstd, tail_gap_exp = (
            sb(n, [P, 2 * G]) for n in ("tail_peak", "tail_first", "tail_deviation", "tail_rstd", "tail_gap_exp"))
        tail_top = sb("tail_top", [P, 2, 2 * G])
        tail_logits, tail_chosen, tail_second, next_gate, tail_gate = (
            sb(n, [P, 2 * G, EXPERTS])
            for n in ("tail_logits", "tail_chosen", "tail_second", "next_gate", "tail_gate"))

        variance_ready = [sem(f"variance_ready{i}") for i in range(2)]
        deviation_ready = [sem(f"deviation_ready{i}") for i in range(2)]
        outputs_ready = [sem(f"outputs_ready{i}") for i in range(2)]
        outputs_used = [sem(f"outputs_used{i}") for i in range(2)]
        adj_loaded = [sem(f"adj_loaded{i}") for i in range(2)]
        x_loaded = [sem(f"x_loaded{i}") for i in range(2)]
        results_stored = [sem(f"results_stored{i}") for i in range(2)]
        blocks_loaded = [sem(f"blocks_loaded{i}") for i in range(2)]
        fused_back = [sem(f"fused_back{i}") for i in range(2)]
        hidden_ready = [sem(f"hidden_ready{i}") for i in range(2)]
        hidden_done = [sem(f"hidden_done{i}") for i in range(2)]
        joints_stacked = [sem(f"joints_stacked{i}") for i in range(2)]
        scattered = [sem(f"scattered{i}") for i in range(2)]
        indices_loaded = [sem(f"indices_loaded{i}") for i in range(2)]
        gathered = [sem(f"gathered{i}") for i in range(2)]
        states_stored = [sem(f"states_stored{i}") for i in range(2)]
        tail_x_loaded = [sem(f"tail_x_loaded{i}") for i in range(2)]
        out_stored = [sem(f"out_stored{i}") for i in range(2)]
        tail_z_loaded = [sem(f"tail_z_loaded{i}") for i in range(2)]
        vector_ticks, vector_steps, adj_rows_used, degrees_ready = (
            sem(n) for n in ("vector_ticks", "vector_steps", "adj_rows_used", "degrees_ready"))
        degree_roots_ready, h0_ready, h_ready, mixed0_ready = (
            sem(n) for n in ("degree_roots_ready", "h0_ready", "h_ready", "mixed0_ready"))
        x_used, gates_ready, gate_gap_ready, gate_exp_ready = (
            sem(n) for n in ("x_used", "gates_ready", "gate_gap_ready", "gate_exp_ready"))
        gate_ready, bias_sum_ready, z_ready, conv1_ready = (
            sem(n) for n in ("gate_ready", "bias_sum_ready", "z_ready", "conv1_ready"))
        shifted_ready, probs_ready, mixed2_ready, softplus_ready = (
            sem(n) for n in ("shifted_ready", "probs_ready", "mixed2_ready", "softplus_ready"))
        weights_ready, deep_ready, joint_degrees_ready, joint_roots_ready = (
            sem(n) for n in ("weights_ready", "deep_ready", "joint_degrees_ready", "joint_roots_ready"))
        joint_adj_ready, joint_turned, joint_norm_ready, joint_out_ready = (
            sem(n) for n in ("joint_adj_ready", "joint_turned", "joint_norm_ready", "joint_out_ready"))
        fused_ready, gat_ready, table_ready, turned = (
            sem(n) for n in ("fused_ready", "gat_ready", "table_ready", "turned"))
        turned_copied, gates_turned, gate_columns_ready, mixed1_ready = (
            sem(n) for n in ("turned_copied", "gates_turned", "gate_columns_ready", "mixed1_ready"))
        mixed1_copied, pre_ready, softplus_steps, joint_mixed_ready = (
            sem(n) for n in ("mixed1_copied", "pre_ready", "softplus_steps", "joint_mixed_ready"))
        joint_mixed_copied, joint_hidden_ready, joint_hidden_done, joint_values_ready = (
            sem(n) for n in ("joint_mixed_copied", "joint_hidden_ready", "joint_hidden_done", "joint_values_ready"))
        joint_values_copied, joints_ready, edges_loaded, loops_made = (
            sem(n) for n in ("joint_values_copied", "joints_ready", "edges_loaded", "loops_made"))
        pairs_counted, pairs_ready, counts_ready, count_copied = (
            sem(n) for n in ("pairs_counted", "pairs_ready", "counts_ready", "count_copied"))
        sums_ready, places_begun, rank_steps, ranks_taken = (
            sem(n) for n in ("sums_ready", "places_begun", "rank_steps", "ranks_taken"))
        tile_counted, keys_ready, lookups_ready, places_ready = (
            sem(n) for n in ("tile_counted", "keys_ready", "lookups_ready", "places_ready"))
        onehots_ready, next_copied, onehots_turned, turned_onehots_copied = (
            sem(n) for n in ("onehots_ready", "next_copied", "onehots_turned", "turned_onehots_copied"))
        staged, begun_ready, owner_ready, owner_written = (
            sem(n) for n in ("staged", "begun_ready", "owner_ready", "owner_written"))
        ends_ready, owner_row_loaded, states_ready, sources_ready = (
            sem(n) for n in ("ends_ready", "owner_row_loaded", "states_ready", "sources_ready"))
        exponents_ready, exps_ready, scan_steps, chain_in_ready = (
            sem(n) for n in ("exponents_ready", "exps_ready", "scan_steps", "chain_in_ready"))
        chain_turned, chain_exponents_ready, chain_exps_ready, chain_ready = (
            sem(n) for n in ("chain_turned", "chain_exponents_ready", "chain_exps_ready", "chain_ready"))
        chain_back, carry_ready, node_rows_used, tail_staged = (
            sem(n) for n in ("chain_back", "carry_ready", "node_rows_used", "tail_staged"))
        node_rows_loaded, tail_steps, node_exponents_ready, node_exps_ready = (
            sem(n) for n in ("node_rows_loaded", "tail_steps", "node_exponents_ready", "node_exps_ready"))
        agg_variance_ready, agg_deviation_ready, tail_gap_ready, tail_gap_exp_ready = (
            sem(n) for n in ("agg_variance_ready", "agg_deviation_ready", "tail_gap_ready", "tail_gap_exp_ready"))
        tail_gate_ready, tail_outputs_ready, tail_outputs_used, tail_bias_ready = (
            sem(n) for n in ("tail_gate_ready", "tail_outputs_ready", "tail_outputs_used", "tail_bias_ready"))
        out_ready, tail_hidden_ready, tail_hidden_done, tail_gates_turned = (
            sem(n) for n in ("out_ready", "tail_hidden_ready", "tail_hidden_done", "tail_gates_turned"))
        tail_gate_columns_ready, consts_loaded, weights_loaded, cleared = (
            sem(n) for n in ("tail_gate_columns_ready", "consts_loaded", "weights_loaded", "cleared"))
        places_blanked, bf_consts_ready, fusion_shifted, fusion_exp_ready = (
            sem(n) for n in ("places_blanked", "bf_consts_ready", "fusion_shifted", "fusion_exp_ready"))
        weights_ready0, carry_stored, vector_links, sync_ticks = (
            sem(n) for n in ("weights_ready0", "carry_stored", "vector_links", "sync_ticks"))
        pool_ticks = sem("pool_ticks")

        def nth(t, i, k, each):
            return t * (2 * each) + (2 * (k - 1) + i + 1)

        def vector_norms(eng, t, i, src, dst, k, link, last_signal=None):
            for g in range(G):
                ins = eng.bn_stats(stats[:, g, :], src[:, g, :])
            link(ins)
            eng.sem_inc(vector_ticks, 1)
            for g in range(G):
                ins = eng.bn_aggr(moments[:, g, :], stats[:, g, :])
            ins.then_inc(variance_ready[i], 1)
            eng.wait_ge(deviation_ready[i], t * NORMS + k)
            link(eng.reciprocal(rstd[:, :], deviation[:, :]))
            for g in range(G):
                ins = eng.tensor_scalar(dst[:, g, :], src[:, g, :], moments[:, g, 0:1], rstd[:, g:g + 1],
                                        ALU.subtract, ALU.mult)
            if last_signal is None:
                link(ins)
            else:
                ins.then_inc(last_signal, 1)

        def first_largest(eng, link, onehot, values, n, peak, first):
            graphs = peak.shape[1]
            link(eng.tensor_reduce(peak[:, :], values, AX.X, ALU.max))
            link(eng.tensor_tensor(onehot, values, peak[:, :].unsqueeze(2).broadcast_to([P, graphs, n]), ALU.is_equal))
            link(eng.tensor_tensor(onehot, onehot, falling[:, 0:n].unsqueeze(1).broadcast_to([P, graphs, n]), ALU.mult))
            link(eng.tensor_reduce(first[:, :], onehot, AX.X, ALU.max))
            link(eng.tensor_tensor(onehot, onehot, first[:, :].unsqueeze(2).broadcast_to([P, graphs, n]), ALU.is_equal))

        def vector_network(eng, t, i, count):
            n = t * 2 + i
            XIN, A, AT, X, Z, H, XS, NB, SP, T4 = (both[i] for both in (XINs, As, ATs, Xs, Zs, Hs, XSs, NBs, SPs, T4s))
            gate, scale_io, weight, inv5, ABIN = (both[i] for both in (gates, scales_io, weights, inv5s, ABINs))
            A5, NT5, F, FB, TAB, T, Y = (both[i] for both in (A5s, NT5s, Fs, FBs, TABs, Ts, Ys))

            def link(ins):
                ins.then_inc(vector_steps, 1)
                count[0] += 1
                eng.wait_ge(vector_steps, t * (2 * NET_STEPS) + count[0])

            def wide(row, width=D):
                return row.unsqueeze(1).broadcast_to([P, G, width])

            def per_token(cols, width=D):
                return cols.unsqueeze(2).broadcast_to([P, G, width])

            def expert_sum(first_y, experts):
                for e in range(experts):
                    eng.wait_ge(outputs_ready[i], t * YS + first_y + e + 1)
                    for g in range(G):
                        ins = eng.scalar_tensor_tensor(X[:, g, :], Y[(first_y + e) % 2][:, g, :], gate[:, g, e:e + 1],
                                                       X[:, g, :], ALU.mult, ALU.add)
                    ins.then_inc(outputs_used[i], 1)
                    eng.wait_ge(outputs_used[i], t * YS + first_y + e + 1)

            eng.wait_ge(adj_loaded[i], t * 32 + 32)
            link(eng.tensor_reduce(degree[:, 0:G], AT[:, :, :], AX.X, ALU.add))
            eng.tensor_reduce(degree[:, G:2 * G], A[:, :, :], AX.X, ALU.add).then_inc(adj_rows_used, 1)
            eng.wait_ge(adj_rows_used, n + 1)
            link(eng.tensor_scalar(no_edge[:, :], degree[:, :], 0.0, None, ALU.is_equal))
            eng.tensor_tensor(degree[:, :], degree[:, :], no_edge[:, :], ALU.add).then_inc(degrees_ready, 1)
            eng.wait_ge(degree_roots_ready, n + 1)
            link(eng.tensor_scalar(no_edge[:, :], no_edge[:, :], -1.0, 1.0, ALU.mult, ALU.add))
            link(eng.reciprocal(scale_io[:, :], degree_root[:, :]))
            link(eng.tensor_tensor(scale_io[:, :], scale_io[:, :], no_edge[:, :], ALU.mult))
            eng.tensor_scalar(scale_io[:, 0:G], scale_io[:, 0:G], -1.0, None, ALU.mult)

            eng.wait_ge(x_loaded[i], t * 16 + 16)
            eng.wait_ge(results_stored[i], t * 48 + FREE)
            vector_norms(eng, t, i, XIN, Z, 1, link, z_ready)
            yield
            eng.wait_ge(h0_ready, n + 1)
            eng.tensor_tensor(H[:, :, :], Y[0][:, :, :], wide(row("L0_gnn_b")), ALU.add).then_inc(h_ready, 1)
            yield
            eng.wait_ge(mixed0_ready, n + 1)
            link(eng.tensor_scalar(R[:, :, :], Y[1][:, :, :], 0.0, row("L0_gnn_alpha"), ALU.min, ALU.mult))
            link(eng.scalar_tensor_tensor(R[:, :, :], Y[1][:, :, :], 0.0, R[:, :, :], ALU.max, ALU.add))
            eng.tensor_tensor(X[:, :, :], XIN[:, :, :], R[:, :, :], ALU.add).then_inc(x_used, 1)
            eng.wait_ge(x_used, n + 1)

            vector_norms(eng, t, i, X, Z, 2, link, z_ready)
            yield
            eng.wait_ge(gates_ready, nth(t, i, 1, 2))
            link(eng.tensor_tensor(logits[:, :, :], T[:, 0:G * 8].rearrange("p (g e) -> p g e", g=G),
                                   wide(gate_bias0[:, :], 8), ALU.add))
            first_largest(eng, link, chosen[:, :, :], logits[:, :, :], 8, peak, first)
            link(eng.tensor_copy(top[:, 0, :], peak[:, :]))
            link(eng.scalar_tensor_tensor(logits[:, :, :], chosen[:, :, :], -BIG, logits[:, :, :], ALU.mult, ALU.add))
            first_largest(eng, link, second[:, :, :], logits[:, :, :], 8, peak, first)
            eng.tensor_tensor(top[:, 1, :], peak[:, :], top[:, 0, :], ALU.subtract).then_inc(gate_gap_ready, 1)
            eng.wait_ge(gate_exp_ready, n + 1)
            link(eng.tensor_scalar(top[:, 0, :], gap_exp[:, :], 1.0, None, ALU.add))
            link(eng.reciprocal(top[:, 1, :], top[:, 0, :]))
            link(eng.tensor_tensor(top[:, 0, :], gap_exp[:, :], top[:, 1, :], ALU.mult))
            link(eng.tensor_tensor(chosen[:, :, :], chosen[:, :, :], per_token(top[:, 1, :], 8), ALU.mult))
            link(eng.tensor_tensor(second[:, :, :], second[:, :, :], per_token(top[:, 0, :], 8), ALU.mult))
            eng.tensor_tensor(gate[:, :, :], chosen[:, :, :], second[:, :, :], ALU.add).then_inc(gate_ready, 1)
            eng.wait_ge(gate_ready, nth(t, i, 1, 2))
            expert_sum(0, 8)
            eng.wait_ge(bias_sum_ready, nth(t, i, 1, 2))
            link(eng.tensor_tensor(X[:, :, :], X[:, :, :], T4[:, :, :], ALU.add))

            vector_norms(eng, t, i, X, Z, 3, link)
            vector_norms(eng, t, i, Z, H, 4, link)
            link(eng.tensor_tensor(H[:, :, :], H[:, :, :], wide(row("L1_gnn_ln_gamma")), ALU.mult))
            eng.tensor_tensor(H[:, :, :], H[:, :, :], wide(row("L1_gnn_ln_beta")), ALU.add).then_inc(z_ready, 1)
            yield
            eng.wait_ge(conv1_ready, n + 1)
            link(eng.tensor_tensor(R[:, :, :], Y[1][:, :, :], wide(row("L1_gnn_b_rel")), ALU.add))
            link(eng.scalar_tensor_tensor(R[:, :, :], R[:, :, :], 0.0, Z[:, :, :], ALU.max, ALU.add))
            link(eng.tensor_tensor(X[:, :, :], X[:, :, :], R[:, :, :], ALU.add))

            vector_norms(eng, t, i, X, Z, 5, link, z_ready)
            yield
            eng.wait_ge(gates_ready, nth(t, i, 2, 2))
            link(eng.tensor_tensor(logits[:, :, :], T[:, 0:G * 8].rearrange("p (g e) -> p g e", g=G),
                                   wide(row("L1_ffn_bg"), 8), ALU.add))
            link(eng.tensor_reduce(peak[:, :], logits[:, :, :], AX.X, ALU.max))
            eng.tensor_tensor(logits[:, :, :], logits[:, :, :], per_token(peak[:, :], 8),
                              ALU.subtract).then_inc(shifted_ready, 1)
            eng.wait_ge(probs_ready, n + 1)
            link(eng.tensor_reduce(top[:, 0, :], probs[:, :, :], AX.X, ALU.add))
            link(eng.reciprocal(top[:, 1, :], top[:, 0, :]))
            first_largest(eng, link, chosen[:, :, :], probs[:, :, :], 8, peak, first)
            link(eng.tensor_tensor(chosen[:, :, :], chosen[:, :, :], probs[:, :, :], ALU.mult))
            eng.tensor_tensor(gate[:, :, :], chosen[:, :, :], per_token(top[:, 1, :], 8), ALU.mult).then_inc(gate_ready, 1)
            eng.wait_ge(gate_ready, nth(t, i, 2, 2))
            expert_sum(8, 8)
            eng.wait_ge(bias_sum_ready, nth(t, i, 2, 2))
            link(eng.tensor_tensor(X[:, :, :], X[:, :, :], T4[:, :, :], ALU.add))

            vector_norms(eng, t, i, X, Z, 6, link)
            vector_norms(eng, t, i, Z, H, 7, link)
            link(eng.tensor_tensor(H[:, :, :], H[:, :, :], wide(row("L2_gnn_gamma")), ALU.mult))
            eng.tensor_tensor(H[:, :, :], H[:, :, :], wide(row("L2_gnn_beta")), ALU.add).then_inc(z_ready, 1)
            eng.wait_ge(z_ready, nth(t, i, 5, 8))
            eng.tensor_tensor(XS[:, :, :], H[:, :, :], per_token(scale_io[:, G:2 * G]), ALU.mult).then_inc(h_ready, 1)
            yield
            eng.wait_ge(mixed2_ready, n + 1)
            for g in range(G):
                ins = eng.scalar_tensor_tensor(NB[:, g, :], Y[0][:, g, :], scale_io[:, g:g + 1], H[:, g, :], ALU.mult,
                                               ALU.add)
            ins.then_inc(z_ready, 1)
            yield
            eng.wait_ge(softplus_ready, n + 1)
            link(eng.scalar_tensor_tensor(R[:, :, :], Y[1][:, :, :], 0.0, SP[:, :, :], ALU.max, ALU.add))
            link(eng.tensor_tensor(X[:, :, :], X[:, :, :], R[:, :, :], ALU.add))

            vector_norms(eng, t, i, X, Z, 8, link, z_ready)
            yield
            eng.wait_ge(weights_ready, n + 1)
            link(eng.tensor_scalar(W[:, :, :], T[:, 0:G * N].rearrange("p (g n) -> p g n", g=G),
                                   row("L2_ffn_br"), None, ALU.add))
            for g in range(G):
                ins = eng.tensor_tensor_reduce(R[:, g, :], W[:, g, :], ident[:, :], 1.0, 0.0, ALU.mult, ALU.add,
                                               weight[:, g:g + 1])
            link(ins)
            for g in range(G):
                ins = eng.scalar_tensor_tensor(R[:, g, :], W[:, g, :], weight[:, g:g + 1], earlier[:, :], ALU.is_equal,
                                               ALU.mult)
            link(ins)
            for g in range(G):
                ins = eng.scalar_tensor_tensor(W[:, g, :], W[:, g, :], weight[:, g:g + 1], R[:, g, :], ALU.is_gt,
                                               ALU.add, accum_out=peak[:, g:g + 1])
            link(ins)
            link(eng.scalar_tensor_tensor(weight[:, :], peak[:, :], float(KEPT), weight[:, :], ALU.is_lt, ALU.mult))
            link(eng.tensor_tensor(X[:, :, :], X[:, :, :], Z[:, :, :], ALU.add))
            eng.wait_ge(deep_ready, n + 1)
            link(eng.tensor_tensor(R[:, :, :], Y[0][:, :, :], wide(row("L2_ffn_b2")), ALU.add))
            for g in range(G):
                ins = eng.scalar_tensor_tensor(X[:, g, :], R[:, g, :], weight[:, g:g + 1], X[:, g, :], ALU.mult, ALU.add)
            link(ins)

            vector_norms(eng, t, i, X, Z, 9, link, joints_ready)
            eng.wait_ge(blocks_loaded[i], t * 16 * G + 16 * G)
            link(eng.tensor_tensor(AB[:, :], ABIN[:, :], ident[0:GJ, 0:GJ], ALU.add))
            link(eng.tensor_tensor(A5[:, :, :], AB[:, :].unsqueeze(1).broadcast_to([GJ, GROUPS, GJ]), member[:, :, :],
                                   ALU.mult))
            link(eng.tensor_reduce(deg5[:, :], A5[:, :, :], AX.X, ALU.add))
            link(eng.tensor_scalar(no5[:, :], deg5[:, :], 0.0, None, ALU.is_equal))
            eng.tensor_tensor(deg5[:, :], deg5[:, :], no5[:, :], ALU.add).then_inc(joint_degrees_ready, 1)
            eng.wait_ge(joint_roots_ready, n + 1)
            link(eng.tensor_scalar(no5[:, :], no5[:, :], -1.0, 1.0, ALU.mult, ALU.add))
            link(eng.reciprocal(inv5[:, :], root5[:, :]))
            link(eng.tensor_tensor(inv5[:, :], inv5[:, :], no5[:, :], ALU.mult))
            inv_wide = inv5[:, :].unsqueeze(2).broadcast_to([GJ, GROUPS, GJ])
            eng.tensor_tensor(A5[:, :, :], A5[:, :, :], inv_wide, ALU.mult).then_inc(joint_adj_ready, 1)
            yield
            eng.wait_ge(joint_turned, n + 1)
            eng.tensor_tensor(NT5[:, :, :], T[0:GJ, 0:GROUPS * GJ].rearrange("p (k n) -> p k n", k=GROUPS), inv_wide,
                              ALU.mult).then_inc(joint_norm_ready, 1)
            yield
            eng.wait_ge(joint_out_ready, n + 1)
            bias5 = row("L3_gnn_b2")[0:GJ, :].rearrange("p (k d) -> p k d", k=GROUPS)
            eng.tensor_tensor(F5[:, 0:4, :], Y[0][0:GJ, :, :], bias5[:, 0:4, :], ALU.add)
            link(eng.tensor_tensor(F5[:, 4, :], Y[1][0:GJ, 0, :], bias5[:, 4, :], ALU.add))
            for k in range(GROUPS):
                ins = eng.tensor_scalar(F5[:, k, :], F5[:, k, :], 0.0, share[0:GJ, k:k + 1], ALU.max, ALU.mult)
            link(ins)
            eng.tensor_reduce(F[:, :], F5[:, :, :].rearrange("p k d -> p d k"), AX.X, ALU.add).then_inc(fused_ready, 1)
            eng.wait_ge(fused_ready, n + 1)
            yield
            eng.wait_ge(fused_back[i], t * 16 * G + 16 * G)
            link(eng.tensor_tensor(X[0:JOINTS, :, :], X[0:JOINTS, :, :], FB[:, :, :], ALU.add))

            vector_norms(eng, t, i, X, Z, 10, link, z_ready)
            yield
            eng.wait_ge(gat_ready, n + 1)
            gat = T[:, 0:G * HE].rearrange("p (g c) -> p g c", g=G)
            link(eng.tensor_copy(TAB[:, :, 0:HE], gat))
            for k, name in enumerate(("L3_ffn_att_src", "L3_ffn_att_dst")):
                link(eng.tensor_tensor(gat_part[:, :, :], TAB[:, :, 0:HE], wide(row(name), HE), ALU.mult))
                ins = eng.tensor_reduce(TAB[:, :, HE + HEADS * k:HE + HEADS * (k + 1)],
                                        gat_part[:, :, :].rearrange("p g (h e) -> p g h e", h=HEADS), AX.X, ALU.add)
                if k == 0:
                    link(ins)
                else:
                    ins.then_inc(table_ready, 1)

        def scalar_network(eng, t, i):
            turn = t * 2 + i
            SP, ZT, T, Y = SPs[i], ZTs[i], Ts[i], Ys[i]

            def root(k):
                eng.wait_ge(variance_ready[i], t * NORMS + k)
                eng.activation(deviation[:, :], moments[:, :, 1], ACT.Sqrt, bias=eps[:, 0:1]).then_inc(deviation_ready[i], 1)

            def evacuate(k, dst):
                eng.wait_ge(turned, nth(t, i, k, 8))
                eng.activation(dst[:, :], T[:, :], ACT.Copy).then_inc(turned_copied, 1)

            def hidden(n, func, bias):
                eng.wait_ge(hidden_ready[i], t * HIDS + n + 1)
                eng.activation(HT[:, n % 4, :], HP[n % 2][:, :], func, bias=bias).then_inc(hidden_done[i], 1)

            def gate_columns(k):
                eng.wait_ge(gates_turned, nth(t, i, k, 2))
                eng.activation(CT[:, :], T[0:G * 8, 0:P], ACT.Copy).then_inc(gate_columns_ready, 1)

            eng.wait_ge(degrees_ready, turn + 1)
            eng.activation(degree_root[:, :], degree[:, :], ACT.Sqrt).then_inc(degree_roots_ready, 1)
            root(1)
            yield
            evacuate(1, ZT)
            for _ in range(5):
                yield
            root(2)
            yield
            evacuate(2, ZT)
            yield
            for n in range(4):
                hidden(n, ACT.Relu, b1_0[:, n:n + 1])
            eng.wait_ge(gate_gap_ready, turn + 1)
            eng.activation(gap_exp[:, :], top[:, 1, :], ACT.Exp).then_inc(gate_exp_ready, 1)
            for n in range(4, 16):
                eng.wait_ge(outputs_ready[i], t * YS + n // 2 - 1)
                hidden(n, ACT.Relu, b1_0[:, n:n + 1])
            gate_columns(1)
            yield
            root(3)
            root(4)
            yield
            evacuate(3, ZT)
            eng.wait_ge(mixed1_ready, turn + 1)
            eng.activation(AGT[:, :], Y[0][:, :, :].rearrange("p g n -> p (g n)"), ACT.Copy).then_inc(mixed1_copied, 1)
            for _ in range(2):
                yield
            root(5)
            yield
            evacuate(4, ZT)
            yield
            for n in range(4):
                hidden(16 + n, ACT.Gelu, b1_1[:, n:n + 1])
            eng.wait_ge(shifted_ready, turn + 1)
            eng.activation(probs[:, :, :], logits[:, :, :], ACT.Exp).then_inc(probs_ready, 1)
            gate_columns(2)
            yield
            root(6)
            root(7)
            yield
            evacuate(5, ZT)
            for _ in range(3):
                yield
            evacuate(6, NBT)
            yield
            eng.wait_ge(pre_ready, turn + 1)
            pre = Y[1][:, :, :].rearrange("p g n -> p (g n)")
            soft = SP[:, :, :].rearrange("p g n -> p (g n)")
            eng.activation(soft, pre, ACT.Abs).then_inc(softplus_steps, 1)
            eng.wait_ge(softplus_steps, turn * 2 + 1)
            eng.activation(soft, soft, ACT.Exp, scale=-1.0).then_inc(softplus_steps, 1)
            eng.wait_ge(softplus_steps, turn * 2 + 2)
            eng.activation(soft, soft, ACT.Ln, bias=one[:, 0:1]).then_inc(softplus_ready, 1)
            yield
            root(8)
            yield
            evacuate(7, ZT)
            yield
            for n in range(4):
                hidden(20 + n, ACT.Gelu_apprx_tanh, b1_2[:, n:n + 1])
            yield
            root(9)
            eng.wait_ge(joint_degrees_ready, turn + 1)
            eng.activation(root5[:, :], deg5[:, :], ACT.Sqrt).then_inc(joint_roots_ready, 1)
            for _ in range(4):
                yield
            eng.wait_ge(joint_mixed_ready, turn + 1)
            eng.activation(UT[:, :], T[:, 0:GROUPS * GJ], ACT.Copy).then_inc(joint_mixed_copied, 1)
            eng.wait_ge(joint_hidden_ready, turn + 1)
            for c in range(2):
                for k in range(GROUPS):
                    ins = eng.activation(H3[:, c, k, :], HP[c][:, k * GJ:(k + 1) * GJ], ACT.Relu,
                                         bias=b1_3[:, 2 * k + c:2 * k + c + 1])
            ins.then_inc(joint_hidden_done, 1)
            eng.wait_ge(joint_values_ready, turn + 1)
            eng.activation(V5[:, 0:4 * D], Y[0][0:GJ, :, :].rearrange("p g n -> p (g n)"), ACT.Copy)
            eng.activation(V5[:, 4 * D:5 * D], Y[1][0:GJ, 0, :], ACT.Copy).then_inc(joint_values_copied, 1)
            for _ in range(5):
                yield
            root(10)
            yield
            evacuate(8, ZT)

        def tensor_network(eng, t, i):
            n = t * 2 + i
            AT, Z, H, XS, NB, ZT, T, Y = (both[i] for both in (ATs, Zs, Hs, XSs, NBs, ZTs, Ts, Ys))
            gate, A5, NT5, ZS = gates[i], A5s[i], NT5s[i], ZSs[i]

            def turn(k, src):
                eng.wait_ge(z_ready, nth(t, i, k, 8))
                for g in range(G):
                    ins = eng.transpose(T[:, g * N:(g + 1) * N], src[:, g, :], ident[:, :])
                ins.then_inc(turned, 1)

            def cols(buf, g):
                return buf[:, g * N:(g + 1) * N]

            def hidden(c, w, src):
                if c >= 2:
                    eng.wait_ge(hidden_done[i], t * HIDS + c - 1)
                eng.matmul(HP[c % 2][:, :], w, src[:, :], start=True, stop=True).then_inc(hidden_ready[i], 1)

            def second(y, slots, ws):
                for g in range(G):
                    for i, (s, w) in enumerate(zip(slots, ws)):
                        ins = eng.matmul(Y[y % 2][:, g, :], HT[:, s, g * N:(g + 1) * N], w,
                                         start=(i == 0), stop=(i == len(slots) - 1))
                return ins

            def bias_sum(k, b2):
                eng.wait_ge(gate_ready, nth(t, i, k, 2))
                eng.transpose(T[0:G * 8, 0:P], gate[:, :, :].rearrange("p g e -> p (g e)"),
                              ident[:, :]).then_inc(gates_turned, 1)
                eng.wait_ge(gate_columns_ready, nth(t, i, k, 2))
                eng.matmul(T[:, :], CT[:, :], b2[:, :], start=True,
                           stop=True).then_inc(bias_sum_ready, 1)

            turn(1, Z)
            eng.wait_ge(turned_copied, nth(t, i, 1, 8))
            for g in range(G):
                ins = eng.matmul(Y[0][:, g, :], cols(ZT, g), wt0[:, :], start=True, stop=True)
            ins.then_inc(h0_ready, 1)
            yield
            eng.wait_ge(h_ready, nth(t, i, 1, 2))
            for g in range(G):
                ins = eng.matmul(Y[1][:, g, :], AT[:, g, :], H[:, g, :], start=True, stop=True)
            ins.then_inc(mixed0_ready, 1)
            yield
            turn(2, Z)
            eng.wait_ge(turned_copied, nth(t, i, 2, 8))
            for g in range(G):
                ins = eng.matmul(T[:, g * 8:(g + 1) * 8], cols(ZT, g), wg0[:, :], start=True, stop=True)
            ins.then_inc(gates_ready, 1)
            for c in range(2):
                hidden(c, w1_0[:, c * D:(c + 1) * D], ZT)
            for e in range(8):
                if e + 1 < 8:
                    for c in (2 * e + 2, 2 * e + 3):
                        hidden(c, w1_0[:, c * D:(c + 1) * D], ZT)
                eng.wait_ge(hidden_done[i], t * HIDS + 2 * e + 2)
                if e >= 2:
                    eng.wait_ge(outputs_used[i], t * YS + e - 1)
                slots = [(2 * e) % 4, (2 * e + 1) % 4]
                second(e, slots, [w2_0[:, (2 * e + c) * D:(2 * e + c + 1) * D] for c in range(2)]).then_inc(outputs_ready[i], 1)
            bias_sum(1, b2_0)
            yield
            turn(3, H)
            for g in range(G):
                ins = eng.matmul(Y[0][:, g, :], H[:, g, :], AT[:, g, :], start=True, stop=True)
            ins.then_inc(mixed1_ready, 1)
            eng.wait_ge(turned_copied, nth(t, i, 3, 8))
            eng.wait_ge(mixed1_copied, n + 1)
            for g in range(G):
                eng.matmul(Y[1][:, g, :], cols(AGT, g), w_rel[:, :], start=True, stop=False)
                ins = eng.matmul(Y[1][:, g, :], cols(ZT, g), w_root[:, :], start=False, stop=True)
            ins.then_inc(conv1_ready, 1)
            yield
            turn(4, Z)
            eng.wait_ge(turned_copied, nth(t, i, 4, 8))
            for c in range(4):
                hidden(16 + c, w1_1[:, c * D:(c + 1) * D], ZT)
            eng.wait_ge(hidden_done[i], t * HIDS + 20)
            for g in range(G):
                for c in range(4):
                    ins = eng.matmul(T[:, g * 8:(g + 1) * 8], HT[:, c, g * N:(g + 1) * N], wg1[:, c * 8:(c + 1) * 8],
                                     start=(c == 0), stop=(c == 3))
            ins.then_inc(gates_ready, 1)
            for e in range(8):
                if e >= 2:
                    eng.wait_ge(outputs_used[i], t * YS + 8 + e - 1)
                if e == 2:
                    bias_sum(2, b2_1)
                second(8 + e, range(4), [wd_1[:, (4 * e + c) * D:(4 * e + c + 1) * D] for c in range(4)])\
                    .then_inc(outputs_ready[i], 1)
            yield
            turn(5, H)
            eng.wait_ge(h_ready, nth(t, i, 2, 2))
            for g in range(G):
                ins = eng.matmul(Y[0][:, g, :], AT[:, g, :], XS[:, g, :], start=True, stop=True)
            ins.then_inc(mixed2_ready, 1)
            eng.wait_ge(turned_copied, nth(t, i, 5, 8))
            yield
            turn(6, NB)
            eng.wait_ge(turned_copied, nth(t, i, 6, 8))
            for g in range(G):
                eng.matmul(Y[1][:, g, :], cols(ZT, g), w_self[:, :], start=True, stop=False)
                ins = eng.matmul(Y[1][:, g, :], cols(NBT, g), w_neigh[:, :], start=False, stop=True)
            ins.then_inc(pre_ready, 1)
            yield
            turn(7, Z)
            eng.wait_ge(turned_copied, nth(t, i, 7, 8))
            eng.matmul(T[:, :], wr_wide[:, :], ZT[:, :], start=True, stop=True).then_inc(weights_ready, 1)
            for c in range(4):
                hidden(20 + c, w1_2[:, c * D:(c + 1) * D], ZT)
            eng.wait_ge(hidden_done[i], t * HIDS + 24)
            second(0, range(4), [w2_2[:, c * D:(c + 1) * D] for c in range(4)]).then_inc(deep_ready, 1)
            yield
            eng.wait_ge(joint_adj_ready, n + 1)
            for k in range(GROUPS):
                ins = eng.transpose(T[0:GJ, k * GJ:(k + 1) * GJ], A5[:, k, :], ident[0:GJ, 0:GJ])
            ins.then_inc(joint_turned, 1)
            yield
            eng.wait_ge(joint_norm_ready, n + 1)
            eng.wait_ge(joints_stacked[i], t * 16 * G + 16 * G)
            eng.matmul(T[:, 0:GROUPS * GJ], ZS[:, :], NT5[:, :, :].rearrange("p k n -> p (k n)"), start=True,
                       stop=True).then_inc(joint_mixed_ready, 1)
            eng.wait_ge(joint_mixed_copied, n + 1)
            for c in range(2):
                for k in range(GROUPS):
                    ins = eng.matmul(HP[c][:, k * GJ:(k + 1) * GJ], w1_3[:, (2 * k + c) * D:(2 * k + c + 1) * D],
                                     UT[:, k * GJ:(k + 1) * GJ], start=True, stop=True)
            ins.then_inc(joint_hidden_ready, 1)
            eng.wait_ge(joint_hidden_done, n + 1)

            def joint_bank(k):
                return Y[0][0:GJ, k, :] if k < 4 else Y[1][0:GJ, 0, :]

            for k in range(GROUPS):
                for c in range(2):
                    ins = eng.matmul(joint_bank(k), H3[:, c, k, :], w2_3[:, (2 * k + c) * D:(2 * k + c + 1) * D],
                                     start=(c == 0), stop=(c == 1))
            ins.then_inc(joint_values_ready, 1)
            eng.wait_ge(joint_values_copied, n + 1)
            for k in range(GROUPS):
                ins = eng.matmul(joint_bank(k), NT5[:, k, :], V5[:, k * D:(k + 1) * D], start=True, stop=True)
            ins.then_inc(joint_out_ready, 1)
            yield
            yield
            turn(8, Z)
            eng.wait_ge(turned_copied, nth(t, i, 8, 8))
            for g in range(G):
                ins = eng.matmul(T[:, g * HE:(g + 1) * HE], cols(ZT, g), w_gat[:, :], start=True, stop=True)
            ins.then_inc(gat_ready, 1)

        def hold(eng, sem, value, ticks):
            eng.wait_ge(sem, value)
            eng.sem_inc(ticks, 1)

        def load_x(eng, t, i):
            eng.dma_start(XINs[i][:, :, :], x_in[bass.ds((t * 2 + i) * G, G)].rearrange("g n d -> n g d"))\
                .then_inc(x_loaded[i], 16)

        def load_adj(eng, t, i):
            eng.dma_start(As[i][:, :, :], adj_in[bass.ds((t * 2 + i) * G, G)].rearrange("g n m -> n g m"))\
                .then_inc(adj_loaded[i], 16)

        def load_adjT(eng, t, i):
            eng.dma_start(ATs[i][:, :, :], adjT_in[bass.ds((t * 2 + i) * G, G)].rearrange("g n m -> n g m"))\
                .then_inc(adj_loaded[i], 16)

        def load_blocks(eng, t, i):
            for g in range(G):
                eng.dma_start(ABINs[i][g * JOINTS:(g + 1) * JOINTS, g * JOINTS:(g + 1) * JOINTS],
                              adj_in[bass.ds((t * 2 + i) * G + g, 1), 0:JOINTS, 0:JOINTS].rearrange("g n m -> n (g m)"))\
                    .then_inc(blocks_loaded[i], 16)

        def sync_network(eng, t, i, more):
            n = t * 2 + i
            if more:
                hold(eng, adj_rows_used, n + 1, sync_ticks)
                load_adj(eng, t + 1, i)
                yield
                hold(eng, x_used, n + 1, sync_ticks)
                load_x(eng, t + 1, i)
                yield
                hold(eng, mixed2_ready, n + 1, sync_ticks)
                load_adjT(eng, t + 1, i)
                yield
            hold(eng, joints_ready, n + 1, sync_ticks)
            for g in range(G):
                eng.dma_start(ZSs[i][g * JOINTS:(g + 1) * JOINTS, :], Zs[i][0:JOINTS, g, :]).then_inc(joints_stacked[i], 16)
            if more:
                hold(eng, joint_degrees_ready, n + 1, sync_ticks)
                load_blocks(eng, t + 1, i)
            yield
            hold(eng, fused_ready, n + 1, sync_ticks)
            for g in range(G):
                eng.dma_start(FBs[i][:, g, :], Fs[i][g * JOINTS:(g + 1) * JOINTS, :]).then_inc(fused_back[i], 16)
            yield
            hold(eng, table_ready, n + 1, sync_ticks)
            eng.dma_start(table[bass.ds(n * (G * N), G * N), :].rearrange("(g n) c -> n g c", g=G),
                          TABs[i][:, :, :]).then_inc(results_stored[i], 16)
            eng.dma_start(x_mid[bass.ds(n, 1)].rearrange("t p c -> p (t c)"),
                          Xs[i][:, :, :].rearrange("p g d -> p (g d)")).then_inc(results_stored[i], 16)
            eng.dma_start(zT_mid[bass.ds(n, 1)].rearrange("t p c -> p (t c)"), ZTs[i][:, :])\
                .then_inc(results_stored[i], 16)

        def vector_prepare(eng, link):
            eng.wait_ge(edges_loaded, 32)
            eng.wait_ge(loops_made, 1)
            link(eng.tensor_copy(POS.bitcast(I32)[:, 0:LOOPS], loop_ids[:, :]))
            link(eng.tensor_copy(VAL.bitcast(I32)[:, 0:LOOPS], loop_ids[:, :]))
            for c in range(0, TILES, CHUNK):
                cs = slice(c, c + CHUNK)
                link(eng.tensor_scalar(bits[:, :], POS.bitcast(I32)[:, cs], 7, None, ALU.logical_shift_right))
                link(eng.tensor_copy(high[:, cs], bits[:, :]))
                link(eng.tensor_scalar(bits[:, :], POS.bitcast(I32)[:, cs], 127, None, ALU.bitwise_and))
                link(eng.tensor_copy(digit[:, cs], bits[:, :]))
                link(eng.tensor_scalar(bitsf, high[:, cs], 127.5, 128.0, ALU.is_gt, ALU.mult))
                link(eng.tensor_tensor(digit[:, cs], digit[:, cs], bitsf, ALU.add))
            link(eng.tensor_scalar(VAL.bitcast(I32)[:, :], VAL.bitcast(I32)[:, :], NODES - 1, None, ALU.min))
            link(eng.tensor_scalar(VAL.bitcast(I32)[:, :], VAL.bitcast(I32)[:, :], NODES - 1, None, ALU.bitwise_and))
            link(eng.tensor_scalar(VAL.bitcast(I32)[:, 0:LOOPS], VAL.bitcast(I32)[:, 0:LOOPS], NODES, None, ALU.add))

        def onehot_of(eng, out, digits, column):
            return eng.tensor_tensor(out, iota4[:, :, :], digits[:, bass.ds(column, 4)].unsqueeze(1).broadcast_to([P, P, 4]),
                                     ALU.is_equal)

        def vector_count(eng, t):
            for u in range(UNROLL):
                b = u % 2
                eng.wait_ge(pairs_counted, t * UNROLL + (u - 1 + TWO_FREE))
                onehot_of(eng, OH[:, b, :, :], digit, t * (4 * UNROLL) + 4 * u)
                onehot_of(eng, OH2[:, b, :, :], high, t * (4 * UNROLL) + 4 * u).then_inc(pairs_ready, 1)

        def tensor_count(eng, t):
            for u in range(UNROLL):
                b = u % 2
                eng.wait_ge(pairs_ready, t * UNROLL + u + 1)
                for k in range(4):
                    ins = eng.matmul(T[:, 0:P], OH[:, b, :, k], OH2[:, b, :, k], start=False, stop=False,
                                     skip_group_check=True)
                ins.then_inc(pairs_counted, 1)

        def vector_bases(eng, link):
            eng.wait_ge(counts_ready, 1)
            eng.tensor_copy(count[:, :], T[:, 0:P]).then_inc(count_copied, 1)
            eng.wait_ge(sums_ready, 1)
            link(eng.tensor_copy(totals[:, :], Y[1][:, 0, :]))
            link(eng.tensor_tensor_scan(base_high[:, :], totals[:, :], zeros[:, :], 0.0, ALU.add, ALU.add))
            link(eng.tensor_tensor(base_high[:, :], base_high[:, :], totals[:, :], ALU.subtract))
            link(eng.tensor_tensor(first_place[:, :], Y[0][:, 1, :], base_high[:, :], ALU.add))
            link(eng.tensor_tensor(last_place[:, :], first_place[:, :], count[:, :], ALU.add))
            link(eng.tensor_scalar(last_place[:, :], last_place[:, :], -1.0, None, ALU.add))
            eng.tensor_copy(next_place[:, 0, :], first_place[:, :]).then_inc(places_begun, 1)
            eng.wait_ge(places_begun, 1)

        def tensor_bases(eng):
            eng.wait_ge(count_copied, 1)
            eng.matmul(Y[1][:, 0, :], ones[:, :], count[:, :], start=True, stop=True)
            eng.matmul(Y[0][:, 1, :], before[:, :], count[:, :], start=True, stop=True).then_inc(sums_ready, 1)
            eng.wait_ge(places_begun, 1)
            eng.matmul(NEXT, ident[:, :], first_place[:, :], start=True, stop=False, skip_group_check=True)

        def vector_rank(eng, t):
            q = t * UNROLL
            here = bass.ds(t * (4 * UNROLL), 4 * UNROLL)
            steps = [0]

            def link(ins):
                ins.then_inc(rank_steps, 1)
                steps[0] += 1
                eng.wait_ge(rank_steps, t * RANK_STEPS + steps[0])

            link(eng.scalar_tensor_tensor(key16[:, :], high[:, here], float(P), digit[:, here], ALU.mult, ALU.add))
            eng.tensor_scalar(skip16[:, :], digit[:, here], 127.5, float(FAR), ALU.is_gt, ALU.mult)
            for u in range(UNROLL):
                b = u % 2
                eng.wait_ge(ranks_taken, q + (u + FREE))
                eng.wait_ge(tile_counted, 4 * (q + u) + FREE)
                group_onehots(eng, t, u + 1)
                eng.wait_ge(keys_ready, q + u + 1)
                for k in range(4):
                    eng.scalar_tensor_tensor(picked[:, k, :], KEYS[b][:, k * P:(k + 1) * P],
                                             key16[:, 4 * u + k:4 * u + k + 1], earlier[:, :], ALU.is_equal,
                                             ALU.mult, accum_out=equal16[:, 4 * u + k:4 * u + k + 1])
                eng.wait_ge(lookups_ready, q + u + 1)
                for k in range(4):
                    ins = eng.tensor_tensor_reduce(picked[:, 4 + k, :], LOOK[b][:, k * P:(k + 1) * P], OH2[:, b, :, k],
                                                   1.0, 0.0, ALU.mult, ALU.add, place16[:, 4 * u + k:4 * u + k + 1])
                ins.then_inc(ranks_taken, 1)
            eng.wait_ge(ranks_taken, q + (UNROLL + FREE))
            link(eng.tensor_tensor(place16[:, :], place16[:, :], equal16[:, :], ALU.add))
            eng.tensor_tensor(POS.bitcast(I32)[:, here], place16[:, :], skip16[:, :], ALU.add).then_inc(places_ready, 1)
            assert steps[0] == RANK_STEPS, steps[0]

        def group_onehots(eng, t, u):
            onehot_of(eng, OH[:, u % 2, :, :], digit, t * (4 * UNROLL) + 4 * u)
            onehot_of(eng, OH2[:, u % 2, :, :], high, t * (4 * UNROLL) + 4 * u).then_inc(onehots_ready, 1)

        def tensor_rank(eng, t):
            q = t * UNROLL
            for u in range(UNROLL):
                b = u % 2

                def count_in(k):
                    eng.wait_ge(next_copied, 4 * (q + u) + (k + FREE))
                    eng.matmul(NEXT, OH[:, b, :, k], OH2[:, b, :, k], start=False, stop=False,
                               skip_group_check=True).then_inc(tile_counted, 1)

                def look_up(k):
                    return eng.matmul(LOOK[b][:, k * P:(k + 1) * P], OHT[:, k * P:(k + 1) * P],
                                      next_place[:, 4 * b + k, :], start=True, stop=True)

                eng.wait_ge(onehots_ready, q + u + 1)
                for k in range(4):
                    ins = eng.transpose(TURNED[b][:, k * P:(k + 1) * P], OH[:, b, :, k], ident_b[:, :])
                ins.then_inc(onehots_turned, 1)
                count_in(0)
                for k in range(4):
                    column = bass.ds(t * (4 * UNROLL) + (4 * u + k), 1)
                    eng.matmul(KEYS[b][:, k * P:(k + 1) * P], digit[:, column].broadcast_to([P, P]), ident_b[:, :],
                               start=True, stop=False)
                    ins = eng.matmul(KEYS[b][:, k * P:(k + 1) * P], high[:, column].broadcast_to([P, P]),
                                     ident128_b[:, :], start=False, stop=True)
                ins.then_inc(keys_ready, 1)
                eng.wait_ge(turned_onehots_copied, q + u + 1)
                for k in range(1, 4):
                    count_in(k)
                    look_up(k - 1)
                look_up(3).then_inc(lookups_ready, 1)

        def scalar_rank(eng, t):
            q = t * UNROLL
            for u in range(UNROLL):
                eng.wait_ge(onehots_turned, q + u + 1)
                eng.activation(OHT[:, :], TURNED[u % 2], ACT.Copy).then_inc(turned_onehots_copied, 1)
                for k in range(4):
                    eng.wait_ge(tile_counted, 4 * (q + u) + (k + 1 + FREE))
                    eng.activation(next_place[:, (4 * (u % 2) + k + 1) % 8, :], NEXT, ACT.Copy).then_inc(next_copied, 1)

        def pool_scatter(eng, t):
            for half in range(2):
                here = bass.ds(t * 32 + 16 * half, 16)
                hold(eng, places_ready, t * 2 + half + 1, pool_ticks)
                if not (isinstance(t, int) and t == 0):
                    hold(eng, scattered[half], t * 256, pool_ticks)
                eng.tensor_copy(stage_place[:, half, :], POS.bitcast(I32)[:, here])
                eng.tensor_copy(stage_value[:, half, :], VAL.bitcast(I32)[:, here]).then_inc(staged, 1)
                hold(eng, staged, t * 2 + half + 1, pool_ticks)
                for j in range(16):
                    eng.indirect_dma_start(order, bass.IndirectOffsetOnAxis(stage_place[:, half, j:j + 1].bitcast(U32), 0),
                                           stage_value[:, half, j:j + 1], None,
                                           bounds_check=PLACES - 1, oob_is_err=False).then_inc(scattered[half], 16)

        def vector_owner(eng, link):
            for c in range(0, P, OWN):
                cuts = cut_row[:, c:c + OWN].unsqueeze(2).broadcast_to([P, OWN, P])
                link(eng.tensor_tensor(begun[:, :, :], first_place[:, :].unsqueeze(1).broadcast_to([P, OWN, P]), cuts,
                                       ALU.is_le))
                ins = eng.tensor_reduce(begun_sum[:, c:c + OWN], begun[:, :, :], AX.X, ALU.add)
                if c + OWN < P:
                    link(ins)
            ins.then_inc(begun_ready, 1)
            eng.wait_ge(owner_ready, 1)
            eng.tensor_scalar(owner[:, :], T[:, 0:1], -1.0, None, ALU.add).then_inc(owner_written, 1)
            link(eng.tensor_copy(end_place[:, :], last_place[:, :]))
            link(eng.tensor_scalar(node_a[:, :], last_place[:, :], 1.0 / WIDTH, None, ALU.mult))
            link(eng.tensor_copy(end_part[:, :], node_a[:, :]))
            link(eng.tensor_copy(node_a[:, :], end_part[:, :]))
            link(eng.scalar_tensor_tensor(node_b[:, :], node_a[:, :], -float(WIDTH), last_place[:, :], ALU.mult, ALU.add))
            link(eng.tensor_scalar(node_c[:, :], node_b[:, :], 0.0, None, ALU.is_lt))
            link(eng.tensor_tensor(node_a[:, :], node_a[:, :], node_c[:, :], ALU.subtract))
            link(eng.tensor_scalar(node_c[:, :], node_b[:, :], float(WIDTH), None, ALU.is_ge))
            link(eng.tensor_tensor(node_a[:, :], node_a[:, :], node_c[:, :], ALU.add))
            link(eng.tensor_copy(end_part[:, :], node_a[:, :]))
            link(eng.scalar_tensor_tensor(node_b[:, :], node_a[:, :], float(WIDTH), first_place[:, :], ALU.mult,
                                          ALU.is_le))
            eng.tensor_scalar(uncut[:, :], node_b[:, :], -HUGE, None, ALU.mult).then_inc(ends_ready, 1)

        def vector_scan_start(eng, link):
            eng.memset(adst_run[:, 1, :, :], 0.0)
            eng.memset(high_run[:, 1, :, :], -BIG)
            eng.memset(loops_seen[:, :], 0.0)
            link(eng.memset(states[:, 1, :, :], 0.0))
            eng.wait_ge(owner_row_loaded, 16)
            eng.tensor_copy(adst_run[:, 1, :, SPAN - 1], owner_row[:, HE + HEADS:ROW]).then_inc(states_ready, 1)
            eng.wait_ge(states_ready, 1 + FREE)

        def vector_sources(eng, t, h, link):
            eng.wait_ge(indices_loaded[h], t * 16 + 16)
            link(eng.tensor_scalar(bits[:, 0:SPAN], indices[:, h, :], 14, None, ALU.logical_shift_right))
            link(eng.tensor_copy(loop_here[:, h, :], bits[:, 0:SPAN]))
            eng.tensor_scalar(source[:, h, :], indices[:, h, :], NODES - 1, None, ALU.bitwise_and)\
                .then_inc(sources_ready, 1)

        def vector_scan(eng, t, h, link):
            o = 1 - h
            n = t * 2 + h
            loops = loop_here[:, h, :]
            link(eng.tensor_scalar(going[:, :], loops, -1.0, 1.0, ALU.mult, ALU.add))
            link(eng.tensor_scalar(restart[:, :], loops, -HUGE, None, ALU.mult))
            link(eng.tensor_reduce(loop_any[:, :], loops, AX.X, ALU.max))
            link(eng.tensor_tensor(loops_seen[:, :], loops_seen[:, :], loop_any[:, :], ALU.max))
            eng.wait_ge(gathered[h], (t + 1) * (SPAN * 16))
            rows = rows_in[:, h, :].rearrange("p (c f) -> p c f", f=ROW)

            def each_head(x):
                return x.unsqueeze(1).broadcast_to([P, HEADS, SPAN])

            link(eng.tensor_tensor(adst[:, :, :], rows[:, :, HE + HEADS:ROW].rearrange("p c h -> p h c"),
                                   each_head(loops), ALU.mult))
            for k in range(HEADS):
                ins = eng.tensor_tensor_scan(adst_run[:, h, k, :], going[:, :], adst[:, k, :],
                                             adst_run[:, o, k, SPAN - 1:SPAN], ALU.mult, ALU.add)
            link(ins)
            link(eng.tensor_tensor(score[:, :, :], rows[:, :, HE:HE + HEADS].rearrange("p c h -> p h c"),
                                   adst_run[:, h, :, :], ALU.add))
            link(eng.scalar_tensor_tensor(score[:, :, :], score[:, :, :], 0.2, score[:, :, :], ALU.mult, ALU.max))
            link(eng.tensor_copy(high_run[:, h, :, 0], high_run[:, o, :, SPAN]))
            for k in range(HEADS):
                ins = eng.tensor_tensor_scan(high_run[:, h, k, 1:SPAN + 1], restart[:, :], score[:, k, :],
                                             high_run[:, h, k, 0:1], ALU.add, ALU.max)
            link(ins)
            link(eng.tensor_tensor(decay[:, :, :], high_run[:, h, :, 0:SPAN], each_head(restart[:, :]), ALU.add))
            link(eng.tensor_tensor(decay[:, :, :], decay[:, :, :], high_run[:, h, :, 1:SPAN + 1], ALU.subtract))
            eng.tensor_tensor(mass[:, :, :], score[:, :, :], high_run[:, h, :, 1:SPAN + 1],
                              ALU.subtract).then_inc(exponents_ready, 1)
            eng.wait_ge(exps_ready, n + 1)
            for k in range(HEADS):
                ins = eng.tensor_tensor(weighed[:, EXPERTS * k:EXPERTS * (k + 1), :],
                                        rows[:, :, EXPERTS * k:EXPERTS * (k + 1)].rearrange("p c e -> p e c"),
                                        mass[:, k, :].unsqueeze(1).broadcast_to([P, EXPERTS, SPAN]), ALU.mult)
            link(ins)
            eng.wait_ge(states_stored[h], t * 16 + FREE)
            for k in range(HEADS):
                eng.tensor_tensor_scan(states[:, h, :, HEADS + k], decay[:, k, :], mass[:, k, :],
                                       states[:, o, SPAN - 1:SPAN, HEADS + k], ALU.mult, ALU.add)
            for k in range(HE):
                eng.tensor_tensor_scan(states[:, h, :, 2 * HEADS + k], decay[:, k // EXPERTS, :], weighed[:, k, :],
                                       states[:, o, SPAN - 1:SPAN, 2 * HEADS + k], ALU.mult, ALU.add)
            eng.tensor_copy(states[:, h, :, 0:HEADS], high_run[:, h, :, 1:SPAN + 1].rearrange("p h c -> p c h"))\
                .then_inc(states_ready, 1)
            eng.wait_ge(states_ready, n + 2 + FREE)

        def vector_scan_turn(eng, t, more=True):
            count = [0]

            def link(ins):
                ins.then_inc(scan_steps, 1)
                count[0] += 1
                eng.wait_ge(scan_steps, t * SCAN_STEPS + count[0] + 2)

            vector_sources(eng, t, 1, link)
            vector_scan(eng, t, 0, link)
            if more:
                vector_sources(eng, t + 1, 0, link)
            vector_scan(eng, t, 1, link)
            assert count[0] == SCAN_STEPS - (0 if more else 2), count[0]

        def scalar_scan(eng, t):
            for h in range(2):
                eng.wait_ge(exponents_ready, t * 2 + h + 1)
                eng.activation(decay[:, :, :], decay[:, :, :], ACT.Exp)
                eng.activation(mass[:, :, :], mass[:, :, :], ACT.Exp).then_inc(exps_ready, 1)

        def pool_gather(eng, t):
            for h in range(2):
                hold(eng, sources_ready, t * 2 + h + 1, pool_ticks)
                hold(eng, states_ready, t * 2 + h + FREE, pool_ticks)
                for j in range(SPAN):
                    eng.indirect_dma_start(rows_in[:, h, j * ROW:(j + 1) * ROW], None, table,
                                           bass.IndirectOffsetOnAxis(source[:, h, j:j + 1].bitcast(U32), 0),
                                           bounds_check=NODES - 1, oob_is_err=False).then_inc(gathered[h], 16)

        def load_indices(eng, t, h):
            eng.dma_start(indices[:, h, :], order_rows[:, bass.ds((t * 2 + h) * SPAN, SPAN)]).then_inc(indices_loaded[h], 16)

        def sync_scan(eng, t, more=True):
            for h in range(2):
                if more:
                    hold(eng, sources_ready, t * 2 + h + 1, sync_ticks)
                    load_indices(eng, t + 1, h)
                hold(eng, states_ready, t * 2 + h + 2 + FREE, sync_ticks)
                eng.dma_start(state_rows[:, bass.ds((t * 2 + h) * (SPAN * ROW), SPAN * ROW)],
                              states[:, h, :, :].rearrange("p c f -> p (c f)")).then_inc(states_stored[h], 16)

        def vector_chain(eng, link):
            link(eng.tensor_copy(chain_in[:, 0, 0:HEADS], states[:, 1, SPAN - 1, 0:HEADS]))
            link(eng.tensor_copy(chain_in[:, 0, HEADS:CARRY].rearrange("p (h e) -> p h e", h=HEADS),
                                 states[:, 1, SPAN - 1, 0:HEADS].unsqueeze(2).broadcast_to([P, HEADS, EXPERTS])))
            link(eng.tensor_copy(chain_in[:, 1, :], states[:, 1, SPAN - 1, HEADS:ROW]))
            eng.tensor_copy(chain_in[:, 2, :], loops_seen[:, 0:1].broadcast_to([P, CARRY])).then_inc(chain_in_ready, 1)
            eng.wait_ge(chain_turned, 1)
            for k in range(3):
                ins = eng.tensor_copy(chain[:, k, :], T[0:CARRY, k * P:(k + 1) * P])
            link(ins)
            maximum, sums, loop = chain[:, 0, :], chain[:, 1, :], chain[:, 2, :]
            link(eng.tensor_scalar(loop, loop, -HUGE, None, ALU.mult))
            link(eng.memset(chain_high[:, 0:1], -BIG))
            link(eng.tensor_tensor_scan(chain_high[:, 1:P + 1], loop, maximum, chain_high[:, 0:1], ALU.add, ALU.max))
            link(eng.tensor_tensor(loop, loop, chain_high[:, 0:P], ALU.add))
            link(eng.tensor_tensor(loop, loop, chain_high[:, 1:P + 1], ALU.subtract))
            eng.tensor_tensor(maximum, maximum, chain_high[:, 1:P + 1], ALU.subtract).then_inc(chain_exponents_ready, 1)
            eng.wait_ge(chain_exps_ready, 1)
            link(eng.tensor_tensor(sums, sums, maximum, ALU.mult))
            link(eng.memset(chain_sum[:, 0:1], 0.0))
            eng.tensor_tensor_scan(chain_sum[:, 1:P + 1], loop, sums, chain_sum[:, 0:1], ALU.mult, ALU.add)\
                .then_inc(chain_ready, 1)
            eng.wait_ge(chain_back, 1)
            eng.tensor_copy(carry_out[:, 0:CARRY], T[:, 0:CARRY])
            eng.tensor_copy(carry_out[:, CARRY:2 * CARRY], T[:, CARRY:2 * CARRY]).then_inc(carry_ready, 1)

        def tensor_chain(eng):
            eng.wait_ge(chain_in_ready, 1)
            for k in range(3):
                ins = eng.transpose(T[0:CARRY, k * P:(k + 1) * P], chain_in[:, k, :], ident[:, :])
            ins.then_inc(chain_turned, 1)
            eng.wait_ge(chain_ready, 1)
            eng.transpose(T[:, 0:CARRY], chain_high[:, 0:P], ident[0:CARRY, 0:CARRY])
            eng.transpose(T[:, CARRY:2 * CARRY], chain_sum[:, 0:P], ident[0:CARRY, 0:CARRY]).then_inc(chain_back, 1)

        def pool_tail(eng, pair):
            hold(eng, node_rows_used, pair + FREE, pool_ticks)
            eng.tensor_copy(tail_index[:, 0, :], end_place.bitcast(I32)[:, bass.ds(pair * (2 * G), 2 * G)])
            eng.tensor_copy(tail_index[:, 1, :],
                            end_part.bitcast(I32)[:, bass.ds(pair * (2 * G), 2 * G)]).then_inc(tail_staged, 1)
            hold(eng, tail_staged, pair + 1, pool_ticks)
            for g in range(2 * G):
                eng.indirect_dma_start(node_states[:, g * ROW:(g + 1) * ROW], None,
                                       state_rows.rearrange("p (c f) -> (p c) f", f=ROW),
                                       bass.IndirectOffsetOnAxis(tail_index[:, 0, g:g + 1].bitcast(U32), 0),
                                       bounds_check=PLACES - 1, oob_is_err=False).then_inc(node_rows_loaded, 16)
                eng.indirect_dma_start(node_carry[:, g * 2 * CARRY:(g + 1) * 2 * CARRY], None, carry_rows,
                                       bass.IndirectOffsetOnAxis(tail_index[:, 1, g:g + 1].bitcast(U32), 0),
                                       bounds_check=P - 1, oob_is_err=False).then_inc(node_rows_loaded, 16)

        def vector_gates(eng, pair):
            count = [0]

            def link(ins):
                ins.then_inc(tail_steps, 1)
                count[0] += 1
                eng.wait_ge(tail_steps, pair * TAIL_STEPS + count[0])

            eng.wait_ge(node_rows_loaded, pair * (64 * G) + 64 * G)
            own = node_states[:, :].rearrange("p (g f) -> p g f", g=2 * G)
            taken = node_carry[:, :].rearrange("p (g f) -> p g f", g=2 * G)
            link(eng.tensor_copy(own_high[:, :, 0:HEADS], own[:, :, 0:HEADS]))
            for g in range(2 * G):
                ins = eng.tensor_copy(own_high[:, g, HEADS:CARRY].rearrange("p (h e) -> p h e", h=HEADS),
                                      own[:, g, 0:HEADS].unsqueeze(2).broadcast_to([P, HEADS, EXPERTS]))
            link(ins)
            link(eng.tensor_tensor(taken_high[:, :, :], taken[:, :, 0:CARRY],
                                   uncut[:, bass.ds(pair * (2 * G), 2 * G)].unsqueeze(2).broadcast_to([P, 2 * G, CARRY]), ALU.add))
            link(eng.tensor_tensor(both_high[:, :, :], own_high[:, :, :], taken_high[:, :, :], ALU.max))
            link(eng.tensor_tensor(own_high[:, :, :], own_high[:, :, :], both_high[:, :, :], ALU.subtract))
            eng.tensor_tensor(taken_high[:, :, :], taken_high[:, :, :], both_high[:, :, :],
                              ALU.subtract).then_inc(node_exponents_ready, 1)
            eng.wait_ge(node_exps_ready, pair + 1)
            link(eng.tensor_tensor(own_high[:, :, :], own_high[:, :, :], own[:, :, HEADS:ROW], ALU.mult))
            link(eng.tensor_tensor(taken_high[:, :, :], taken_high[:, :, :], taken[:, :, CARRY:2 * CARRY], ALU.mult))
            eng.tensor_tensor(own_high[:, :, :], own_high[:, :, :], taken_high[:, :, :], ALU.add)\
                .then_inc(node_rows_used, 1)
            eng.wait_ge(node_rows_used, pair + (1 + FREE))
            link(eng.tensor_scalar(denominator[:, :, :], own_high[:, :, 0:HEADS], 1e-16, None, ALU.add))
            link(eng.reciprocal(denominator[:, :, :], denominator[:, :, :]))
            for g in range(2 * G):
                ins = eng.tensor_tensor(agg[:, g, :].rearrange("p (h e) -> p h e", h=HEADS),
                                        own_high[:, g, HEADS:CARRY].rearrange("p (h e) -> p h e", h=HEADS),
                                        denominator[:, g, :].unsqueeze(2).broadcast_to([P, HEADS, EXPERTS]), ALU.mult)
            link(ins)

            def wide(x):
                return x.unsqueeze(1).broadcast_to([P, 2 * G, HE])

            def over(x, n=HE):
                return x.unsqueeze(2).broadcast_to([P, 2 * G, n])

            link(eng.tensor_tensor(agg[:, :, :], agg[:, :, :], wide(row("L3_ffn_b_gat")), ALU.add))
            link(eng.tensor_reduce(tail_peak[:, :], agg[:, :, :], AX.X, ALU.add))
            link(eng.tensor_scalar(tail_peak[:, :], tail_peak[:, :], 1.0 / HE, None, ALU.mult))
            link(eng.tensor_tensor(agg[:, :, :], agg[:, :, :], over(tail_peak[:, :]), ALU.subtract))
            link(eng.tensor_tensor(tail_part[:, :, :], agg[:, :, :], agg[:, :, :], ALU.mult))
            link(eng.tensor_reduce(tail_peak[:, :], tail_part[:, :, :], AX.X, ALU.add))
            eng.tensor_scalar(tail_peak[:, :], tail_peak[:, :], 1.0 / HE, None, ALU.mult).then_inc(agg_variance_ready, 1)
            eng.wait_ge(agg_deviation_ready, pair + 1)
            link(eng.reciprocal(tail_rstd[:, :], tail_deviation[:, :]))
            link(eng.tensor_tensor(agg[:, :, :], agg[:, :, :], over(tail_rstd[:, :]), ALU.mult))
            link(eng.tensor_tensor(agg[:, :, :], agg[:, :, :], wide(row("L3_ffn_ln_gamma")), ALU.mult))
            link(eng.tensor_tensor(agg[:, :, :], agg[:, :, :], wide(row("L3_ffn_ln_beta")), ALU.add))
            link(eng.tensor_reduce(tail_logits[:, :, :], agg[:, :, :].rearrange("p g (h e) -> p g e h", h=HEADS),
                                   AX.X, ALU.add))
            link(eng.tensor_scalar(tail_logits[:, :, :], tail_logits[:, :, :], 1.0 / HEADS, None, ALU.mult))
            small, ch, se = tail_logits[:, :, :], tail_chosen[:, :, :], tail_second[:, :, :]
            first_largest(eng, link, ch, small, EXPERTS, tail_peak, tail_first)
            link(eng.tensor_copy(tail_top[:, 0, :], tail_peak[:, :]))
            link(eng.scalar_tensor_tensor(small, ch, -BIG, small, ALU.mult, ALU.add))
            first_largest(eng, link, se, small, EXPERTS, tail_peak, tail_first)
            eng.tensor_tensor(tail_top[:, 1, :], tail_peak[:, :], tail_top[:, 0, :], ALU.subtract).then_inc(tail_gap_ready, 1)
            eng.wait_ge(tail_gap_exp_ready, pair + 1)
            link(eng.tensor_scalar(tail_top[:, 0, :], tail_gap_exp[:, :], 1.0, None, ALU.add))
            link(eng.reciprocal(tail_top[:, 1, :], tail_top[:, 0, :]))
            link(eng.tensor_tensor(tail_top[:, 0, :], tail_gap_exp[:, :], tail_top[:, 1, :], ALU.mult))
            link(eng.tensor_tensor(ch, ch, over(tail_top[:, 1, :], EXPERTS), ALU.mult))
            link(eng.tensor_tensor(se, se, over(tail_top[:, 0, :], EXPERTS), ALU.mult))
            link(eng.tensor_tensor(next_gate[:, :, :], ch, se, ALU.add))
            assert count[0] == TAIL_STEPS, count[0]

        def vector_use_gates(eng, pair):
            eng.tensor_copy(tail_gate[:, :, :], next_gate[:, :, :]).then_inc(tail_gate_ready, 1)
            eng.wait_ge(tail_gate_ready, pair + 1)

        def vector_sum(eng, pair, i):
            t = pair * 2 + i
            X, XIN = Xs[i], XINs[i]
            eng.wait_ge(tail_x_loaded[i], pair * 16 + 16)
            for e in range(EXPERTS):
                eng.wait_ge(tail_outputs_ready, t * EXPERTS + e + 1)
                for g in range(G):
                    ins = eng.scalar_tensor_tensor(X[:, g, :], Ys[e // 2][e % 2][:, g, :],
                                                   tail_gate[:, i * G + g, e:e + 1], X[:, g, :], ALU.mult, ALU.add)
                ins.then_inc(tail_outputs_used, 1)
                eng.wait_ge(tail_outputs_used, t * EXPERTS + (e + 1 + EXPERTS))
            eng.wait_ge(tail_bias_ready, t + 1)
            eng.wait_ge(out_stored[i], pair * 16 + FREE)
            eng.tensor_tensor(XIN[:, :, :], X[:, :, :], T4[:, :, :], ALU.add).then_inc(out_ready, 1)

        def scalar_gates(eng, pair, step):
            if step == 0:
                eng.wait_ge(node_exponents_ready, pair + 1)
                eng.activation(own_high[:, :, :], own_high[:, :, :], ACT.Exp)
                eng.activation(taken_high[:, :, :], taken_high[:, :, :], ACT.Exp).then_inc(node_exps_ready, 1)
            elif step == 1:
                eng.wait_ge(agg_variance_ready, pair + 1)
                eng.activation(tail_deviation[:, :], tail_peak[:, :], ACT.Sqrt, bias=eps[:, 0:1])\
                    .then_inc(agg_deviation_ready, 1)
            else:
                eng.wait_ge(tail_gap_ready, pair + 1)
                eng.activation(tail_gap_exp[:, :], tail_top[:, 1, :], ACT.Exp).then_inc(tail_gap_exp_ready, 1)

        def scalar_tail(eng, pair, i, more):
            t = pair * 2 + i
            for n in range(8):
                eng.wait_ge(tail_hidden_ready, t * 8 + n + 1)
                if n >= 4:
                    eng.wait_ge(tail_outputs_ready, t * EXPERTS + n // 2 - 1)
                eng.activation(HT[:, n % 4, :], HP[n % 2][:, :], ACT.Gelu, bias=b1_4[:, n:n + 1])\
                    .then_inc(tail_hidden_done, 1)
                if more and i == 1 and n in (1, 3, 7):
                    scalar_gates(eng, pair + 1, n // 3)
            eng.wait_ge(tail_gates_turned, t + 1)
            eng.activation(CT[0:G * EXPERTS, :], T[0:G * EXPERTS, 0:P], ACT.Copy).then_inc(tail_gate_columns_ready, 1)

        def tensor_tail(eng, pair, i):
            t = pair * 2 + i
            ZT = ZTs[i]

            def hidden(n):
                if n >= 2:
                    eng.wait_ge(tail_hidden_done, t * 8 + n - 1 + FREE)
                eng.matmul(HP[n % 2][:, :], w1_4[:, n * D:(n + 1) * D], ZT[:, :], start=True, stop=True)\
                    .then_inc(tail_hidden_ready, 1)

            eng.wait_ge(tail_z_loaded[i], pair * 16 + 16)
            eng.wait_ge(tail_hidden_done, t * 8 + FREE)
            hidden(0)
            hidden(1)
            for e in range(EXPERTS):
                if e + 1 < EXPERTS:
                    hidden(2 * e + 2)
                    hidden(2 * e + 3)
                eng.wait_ge(tail_hidden_done, t * 8 + 2 * e + 2 + FREE)
                eng.wait_ge(tail_outputs_used, t * EXPERTS + (e + 1))
                for g in range(G):
                    for c in range(2):
                        n = 2 * e + c
                        ins = eng.matmul(Ys[e // 2][e % 2][:, g, :], HT[:, n % 4, g * N:(g + 1) * N], w2_4[:, n * D:(n + 1) * D],
                                         start=(c == 0), stop=(c == 1))
                ins.then_inc(tail_outputs_ready, 1)
            eng.wait_ge(tail_gate_ready, pair + 1)
            eng.wait_ge(out_ready, t + FREE)
            eng.transpose(T[0:G * EXPERTS, 0:P], tail_gate[:, i * G:(i + 1) * G, :].rearrange("p g e -> p (g e)"),
                          ident[:, :]).then_inc(tail_gates_turned, 1)
            eng.wait_ge(tail_gate_columns_ready, t + 1)
            eng.matmul(T[:, :], CT[0:G * EXPERTS, :], b2_4[:, :], start=True,
                       stop=True).then_inc(tail_bias_ready, 1)

        def load_tail_z(eng, pair, i):
            eng.dma_start(ZTs[i][:, :], zT_mid[bass.ds(pair * 2 + i, 1)].rearrange("t p c -> p (t c)"))\
                .then_inc(tail_z_loaded[i], 16)

        def load_tail_x(eng, pair, i):
            eng.dma_start(Xs[i][:, :, :].rearrange("p g d -> p (g d)"),
                          x_mid[bass.ds(pair * 2 + i, 1)].rearrange("t p c -> p (t c)")).then_inc(tail_x_loaded[i], 16)

        def sync_tail(eng, pair, i, more=True):
            t = pair * 2 + i
            if more:
                hold(eng, tail_outputs_ready, (t + 1) * EXPERTS, sync_ticks)
                load_tail_z(eng, pair + 1, i)
            hold(eng, out_ready, t + 1 + FREE, sync_ticks)
            if more:
                load_tail_x(eng, pair + 1, i)
            eng.dma_start(out[bass.ds(t * G, G)].rearrange("g n d -> n g d"), XINs[i][:, :, :]).then_inc(out_stored[i], 16)

        def pool_setup(eng):
            eng.iota(loop_ids[:, :], [[P, LOOPS]], base=0, channel_multiplier=1).then_inc(loops_made, 1)

        def sync_setup(eng):
            for free in (*results_stored, states_ready, *states_stored,
                         node_rows_used, tail_hidden_done, *out_stored, out_ready, next_copied,
                         ranks_taken):
                eng.sem_inc(free, FREE)
            eng.sem_inc(tail_outputs_used, EXPERTS)
            eng.sem_inc(pairs_counted, TWO_FREE)
            eng.sem_inc(tile_counted, FREE)
            eng.dma_start(POS.bitcast(I32)[:, LOOPS:TILES], edges[1].rearrange("(p c) -> p c", p=P))\
                .then_inc(edges_loaded, 16)
            eng.dma_start(VAL.bitcast(I32)[:, LOOPS:TILES], edges[0].rearrange("(p c) -> p c", p=P))\
                .then_inc(edges_loaded, 16)
            eng.dma_start(consts[:, :], consts_in).then_inc(consts_loaded, 16)
            eng.dma_start(row_tile[:, :], rows_in_dram.partition_broadcast(P)).then_inc(consts_loaded, 16)
            for i in range(2):
                load_x(eng, 0, i)
                load_adj(eng, 0, i)
                load_adjT(eng, 0, i)
            for name, _ in MATS:
                eng.dma_start(mat[name][:, :], mats[name]).then_inc(weights_loaded, 16)
            eng.wait_ge(cleared, 1)
            for tile, bias, n in ((b2_0, 0, 8), (b2_1, 1, 8), (b2_4, 2, EXPERTS)):
                for g in range(G):
                    eng.dma_start(tile[g * n:(g + 1) * n, g * D:(g + 1) * D], expert_biases[bias])\
                        .then_inc(weights_loaded, 16)
            for i in range(2):
                load_blocks(eng, 0, i)
            for c in range(4):
                eng.dma_start(order_rows[:, c * CHUNK:(c + 1) * CHUNK], high[:, 0:2 * CHUNK].bitcast(I32))\
                    .then_inc(places_blanked, 16)

        def vector_setup(eng, link):
            eng.memset(b2_0[:, :], 0.0)
            eng.memset(b2_1[:, :], 0.0)
            eng.memset(b2_4[:, :], 0.0)
            for i in range(2):
                eng.memset(ABINs[i][:, :], 0.0)
            eng.memset(digit[:, :], 0.0)
            eng.memset(high[:, :], 0.0).then_inc(cleared, 1)
            eng.memset(zeros_b[:, :], 0.0)
            eng.memset(ones[:, :], 1.0)
            eng.memset(zeros[:, :], 0.0)
            eng.memset(eps[:, :], EPS)
            link(eng.memset(one[:, :], 1.0))
            eng.wait_ge(consts_loaded, 32)
            link(eng.tensor_copy(iota4[:, :, :], iota[:, :].unsqueeze(2).broadcast_to([P, P, 4])))
            eng.tensor_copy(ident_b[:, :], ident)
            eng.tensor_scalar(ident128_b[:, :], ident, float(P), None, ALU.mult).then_inc(bf_consts_ready, 1)
            link(eng.tensor_tensor(gate_bias0[:, :], row("L0_ffn_bg"), row("L0_ffn_bias"), ALU.add))
            fusion = row("L3_gnn_fusion_w")
            link(eng.tensor_reduce(share_sum[:, :], fusion, AX.X, ALU.max))
            eng.tensor_scalar(share[:, :], fusion, share_sum[:, 0:1], None, ALU.subtract).then_inc(fusion_shifted, 1)
            eng.wait_ge(fusion_exp_ready, 1)
            link(eng.tensor_reduce(share_sum[:, :], share[:, :], AX.X, ALU.add))
            link(eng.reciprocal(share_sum[:, :], share_sum[:, :]))
            link(eng.tensor_scalar(share[:, :], share[:, :], share_sum[:, 0:1], None, ALU.mult))
            link(eng.tensor_tensor(share[:, :], share[:, :], const["joint_share"], ALU.mult))
            eng.wait_ge(weights_loaded, 16 * (len(MATS) + 3 * G))
            eng.tensor_copy(wr_wide[:, :], wr[:, 0:1].broadcast_to([P, P])).then_inc(weights_ready0, 1)

        block = ctx.enter_context(nc.Block())
        PAIRS = NET_TURNS // 2

        def both(part, lead=0):
            streams = [part(i) for i in range(2)]
            for _ in range(lead):
                next(streams[0])
            for _ in zip_longest(*streams):
                pass

        @block.sync
        def _(sp):
            sync_setup(sp)
            with sp.Fori(0, PAIRS - 1) as t:
                both(lambda i: sync_network(sp, t, i, True))
            both(lambda i: sync_network(sp, PAIRS - 1, i, False))
            for half in range(2):
                sp.wait_ge(scattered[half], SCATTERS * 256)
            load_indices(sp, 0, 0)
            load_indices(sp, 0, 1)
            with sp.Fori(0, SCAN_TURNS - 1) as t:
                sync_scan(sp, t)
            sync_scan(sp, SCAN_TURNS - 1, more=False)
            for i in range(2):
                load_tail_z(sp, 0, i)
                load_tail_x(sp, 0, i)
            sp.wait_ge(carry_ready, 1)
            sp.dma_start(carry_rows, carry_out[:, :]).then_inc(carry_stored, 16)
            with sp.Fori(0, PAIRS - 1) as t:
                for i in range(2):
                    sync_tail(sp, t, i)
            for i in range(2):
                sync_tail(sp, PAIRS - 1, i, more=False)
            for i in range(2):
                sp.wait_ge(out_stored[i], PAIRS * 16 + FREE)
                sp.wait_ge(results_stored[i], PAIRS * 48 + FREE)
            for h in range(2):
                sp.wait_ge(states_stored[h], SCAN_TURNS * 16 + FREE)

        @block.gpsimd
        def _(pool):
            pool_setup(pool)
            pool.wait_ge(places_blanked, 64)
            pool_scatter(pool, 0)
            with pool.Fori(1, SCATTERS) as t:
                pool_scatter(pool, t)
            pool.wait_ge(owner_written, 1)
            for i in range(2):
                pool.wait_ge(results_stored[i], PAIRS * 48 + FREE)
            pool.indirect_dma_start(owner_row[:, :], None, table, bass.IndirectOffsetOnAxis(owner[:, :].bitcast(U32), 0),
                                    bounds_check=NODES - 1, oob_is_err=False).then_inc(owner_row_loaded, 16)
            with pool.Fori(0, SCAN_TURNS) as t:
                pool_gather(pool, t)
            for h in range(2):
                pool.wait_ge(states_stored[h], SCAN_TURNS * 16 + FREE)
            pool.wait_ge(carry_stored, 16)
            with pool.Fori(0, PAIRS) as t:
                pool_tail(pool, t)

        @block.scalar
        def _(act):
            act.wait_ge(fusion_shifted, 1)
            act.activation(share[:, :], share[:, :], ACT.Exp).then_inc(fusion_exp_ready, 1)
            with act.Fori(0, TURNS) as t:
                scalar_rank(act, t)
            with act.Fori(0, PAIRS) as t:
                both(lambda i: scalar_network(act, t, i), lead=1)
            with act.Fori(0, SCAN_TURNS) as t:
                scalar_scan(act, t)
            act.wait_ge(chain_exponents_ready, 1)
            act.activation(chain[:, 0, :], chain[:, 0, :], ACT.Exp)
            act.activation(chain[:, 2, :], chain[:, 2, :], ACT.Exp).then_inc(chain_exps_ready, 1)
            for step in range(3):
                scalar_gates(act, 0, step)
            with act.Fori(0, PAIRS - 1) as t:
                for i in range(2):
                    scalar_tail(act, t, i, more=True)
            for i in range(2):
                scalar_tail(act, PAIRS - 1, i, more=False)

        @block.vector
        def _(dve):
            chain_count = [0]

            def link(ins):
                ins.then_inc(vector_links, 1)
                chain_count[0] += 1
                dve.wait_ge(vector_links, chain_count[0])

            def first_link(ins, n=[0]):
                ins.then_inc(scan_steps, 1)
                n[0] += 1
                dve.wait_ge(scan_steps, n[0])

            vector_setup(dve, link)
            dve.wait_ge(places_blanked, 64)
            vector_prepare(dve, link)
            with dve.Fori(0, TURNS) as t:
                vector_count(dve, t)
            vector_bases(dve, link)
            group_onehots(dve, 0, 0)
            with dve.Fori(0, TURNS) as t:
                vector_rank(dve, t)
            dve.wait_ge(next_copied, 4 * UNROLL * TURNS + FREE)
            with dve.Fori(0, PAIRS) as t:
                steps = [0]
                both(lambda i: vector_network(dve, t, i, steps))
            assert steps[0] == 2 * NET_STEPS, steps[0] / 2
            for half in range(2):
                dve.wait_ge(scattered[half], SCATTERS * 256)
            vector_owner(dve, link)
            vector_scan_start(dve, link)
            vector_sources(dve, 0, 0, first_link)
            with dve.Fori(0, SCAN_TURNS - 1) as t:
                vector_scan_turn(dve, t)
            vector_scan_turn(dve, SCAN_TURNS - 1, more=False)
            vector_chain(dve, link)
            vector_gates(dve, 0)
            with dve.Fori(0, PAIRS - 1) as t:
                vector_use_gates(dve, t)
                vector_sum(dve, t, 0)
                vector_gates(dve, t + 1)
                vector_sum(dve, t, 1)
            vector_use_gates(dve, PAIRS - 1)
            for i in range(2):
                vector_sum(dve, PAIRS - 1, i)

        @block.tensor
        def _(pe):
            pe.wait_ge(bf_consts_ready, 1)
            pe.matmul(T[:, 0:P], zeros_b[:, :], zeros_b[:, :], start=True, stop=False, skip_group_check=True)
            with pe.Fori(0, TURNS) as t:
                tensor_count(pe, t)
            pe.matmul(T[:, 0:P], zeros_b[:, :], zeros_b[:, :], start=False, stop=True,
                      skip_group_check=True).then_inc(counts_ready, 1)
            tensor_bases(pe)
            pe.wait_ge(weights_ready0, 1)
            with pe.Fori(0, TURNS) as t:
                tensor_rank(pe, t)
            pe.wait_ge(next_copied, 4 * UNROLL * TURNS + FREE)
            pe.matmul(NEXT, zeros_b[:, :], zeros_b[:, :], start=False, stop=True, skip_group_check=True)
            with pe.Fori(0, PAIRS) as t:
                both(lambda i: tensor_network(pe, t, i))
            pe.wait_ge(begun_ready, 1)
            pe.matmul(T[:, 0:1], begun_sum[:, :], ones[:, 0:1], start=True, stop=True).then_inc(owner_ready, 1)
            tensor_chain(pe)
            with pe.Fori(0, PAIRS) as t:
                for i in range(2):
                    tensor_tail(pe, t, i)

def kernel(**inputs):
    import concourse.bacc as bacc
    from concourse.bass_utils import run_bass_kernel_spmd

    a = {k: np.asarray(v) for k, v in inputs.items()}

    def hidden_major(w):
        e, h, d = w.shape
        return w.reshape(e, h // P, P, d).transpose(2, 0, 1, 3).reshape(P, -1)

    def feature_major(w):
        return w.transpose(1, 0, 2).reshape(P, -1)

    def bias_columns(b):
        return b.reshape(-1, P).transpose(1, 0)

    mats = {
        "wt0": a["L0_gnn_W"].T, "wg0": a["L0_ffn_Wg"], "w1_0": feature_major(a["L0_ffn_W1"]),
        "w2_0": hidden_major(a["L0_ffn_W2"]), "w_rel": a["L1_gnn_W_rel"], "w_root": a["L1_gnn_W_root"],
        "w1_1": a["L1_ffn_W1"], "wg1": hidden_major(a["L1_ffn_Wg"][None]), "wd_1": hidden_major(a["L1_ffn_Wd"]),
        "w_self": a["L2_gnn_W_self"], "w_neigh": a["L2_gnn_W_neigh"], "wr": a["L2_ffn_wr"], "w1_2": a["L2_ffn_w1"],
        "w2_2": hidden_major(a["L2_ffn_w2"][None]), "w1_3": feature_major(a["L3_gnn_W1"]),
        "w2_3": hidden_major(a["L3_gnn_W2"]), "w_gat": a["L3_ffn_W_gat"], "w1_4": feature_major(a["L3_ffn_W1"]),
        "w2_4": hidden_major(a["L3_ffn_W2"]), "b1_0": bias_columns(a["L0_ffn_b1"]),
        "b1_1": bias_columns(a["L1_ffn_b1"]), "b1_2": bias_columns(a["L2_ffn_b1"]),
        "b1_3": bias_columns(a["L3_gnn_b1"]), "b1_4": bias_columns(a["L3_ffn_b1"]),
    }
    lower = np.tril(np.ones((P, P), np.float32), -1)
    groups_of = np.zeros((GROUPS, JOINTS), np.float32)
    for k, nodes in enumerate(JOINT_GROUPS):
        groups_of[k, nodes] = 1.0
    one_of = np.tile(groups_of, (1, G))
    member = np.zeros((P, GROUPS, GJ), np.float32)
    member[:GJ] = one_of.T[:, :, None] * one_of[None]
    joint_share = np.zeros((P, GROUPS), np.float32)
    joint_share[:GJ] = one_of.T
    tables = {
        "ident": np.eye(P, dtype=np.float32), "iota": np.tile(np.arange(P, dtype=np.float32), (P, 1)),
        "before": lower.T, "earlier": lower, "falling": np.tile(np.arange(8, 0, -1, dtype=np.float32), (P, 1)),
        "cut_row": np.tile(np.arange(P, dtype=np.float32) * WIDTH, (P, 1)), "member": member.reshape(P, -1),
        "joint_share": joint_share,
    }
    data = {
        "x_in": a["x"], "adj_in": a["adj"], "adjT_in": a["adj"].transpose(0, 2, 1), "edges": a["L3_ffn_edge_index"],
        "rows_in_dram": np.concatenate([a[name].reshape(-1) for name, _ in ROWS]),
        "consts_in": np.concatenate([tables[name] for name, _ in CONSTS], axis=1),
        "bias0": a["L0_ffn_b2"], "bias1": a["L1_ffn_bd"], "bias2": a["L3_ffn_b2"],
    }
    data.update({f"m_{name}": w for name, w in mats.items()})
    data = {name: np.ascontiguousarray(v) for name, v in data.items()}

    nc = bacc.Bacc("TRN2", target_bir_lowering=False, num_devices=1)
    t = {name: nc.dram_tensor(name, v.shape, mybir.dt.from_np(v.dtype), kind="ExternalInput").ap()
         for name, v in data.items()}
    out = nc.dram_tensor("out", (B, N, D), F32, kind="ExternalOutput").ap()
    build(nc, t["x_in"], t["adj_in"], t["adjT_in"], t["edges"], t["rows_in_dram"], t["consts_in"],
          [t["bias0"], t["bias1"], t["bias2"]], {name: t[f"m_{name}"] for name, _ in MATS}, out)
    return run_bass_kernel_spmd(nc, [data], core_ids=[0]).results[0]["out"]
```
